# Optimizing a Trainium2 kernel written in Bass

```python
import numpy as np
import jax
import jax.numpy as jnp

def _softmax(x, axis=-1):
    return jax.nn.softmax(x, axis=axis)

def _gelu(x):
    return jax.nn.gelu(x, approximate=True)

def _silu(x):
    return jax.nn.silu(x)

def _sigmoid(x):
    return jax.nn.sigmoid(x)

def _layernorm(x, axis=-1, eps=1e-05):
    m = jnp.mean(x, axis=axis, keepdims=True)
    v = jnp.var(x, axis=axis, keepdims=True)
    return (x - m) / jnp.sqrt(v + eps)

def _scatter_add(tgt, idx, src, axis=0):
    return tgt.at[idx].add(src)

def _segment_sum(src, seg, n):
    return jax.ops.segment_sum(src, seg, n)
kernel_name = 'mk_seq_postln_d1_jaxref_r4_613535'

def setup_inputs(seed: int=0):
    np.random.seed(seed)
    _w = jnp.asarray

    def _L0_attn_setup():
        import jax, jax.numpy as jnp
        import numpy as np
        DIMS, HEAD = (256, 16)
        HD = DIMS // HEAD
        MAX_ITER = 3
        B, T = (4, 512)

        def _ln(x, w, eps=1e-05):
            m = jnp.mean(x, axis=-1, keepdims=True)
            v = jnp.var(x, axis=-1, keepdims=True)
            return (x - m) * jax.lax.rsqrt(v + eps) * w
        key = jax.random.key(seed)
        ks = jax.random.split(key, 10)
        n = lambda k, s: jax.random.normal(k, s, jnp.float32) * 0.02
        z = lambda s: jnp.zeros(s, jnp.float32)
        o = lambda s: jnp.ones(s, jnp.float32)
        return {'x': jax.random.normal(ks[0], (B, T, DIMS), jnp.float32), 'Wq': n(ks[1], (DIMS, DIMS)), 'bq': z((DIMS,)), 'Wk': n(ks[2], (DIMS, DIMS)), 'Wv': n(ks[3], (DIMS, DIMS)), 'bv': z((DIMS,)), 'Wo': n(ks[4], (DIMS, DIMS)), 'bo': z((DIMS,)), 'lna_w': o((DIMS,)), 'lnc_w': o((HD,)), 'lnd_w': o((HD,)), 'Wlq': n(ks[5], (HD, HD)), 'blq': z((HD,)), 'Wlk': n(ks[6], (HD, HD)), 'blk': z((HD,)), 'Wlv': n(ks[7], (HD, HD)), 'blv': z((HD,)), 'temp': jnp.float32(1.0), 'threshold': jnp.float32(0.01), 'factor': jnp.float32(0.1)}
    _L0_attn_in = _L0_attn_setup()

    def _L0_ffn_setup():
        import jax, jax.numpy as jnp
        import numpy as np
        H = 16
        TOP_K = 2
        EPS = 1e-05

        def _layer_norm(x, g, b):
            m = x.mean(-1, keepdims=True)
            v = ((x - m) ** 2).mean(-1, keepdims=True)
            return (x - m) * jax.lax.rsqrt(v + EPS) * g + b

        def _block(x, ln1_g, ln1_b, ln2_g, ln2_b, w_qkv, w_o, w_gate, w1, b1, w2, b2):
            B, S, D = x.shape
            hd = D // H
            h = _layer_norm(x, ln1_g, ln1_b)
            qkv = h @ w_qkv
            q, k, v = jnp.split(qkv, 3, axis=-1)
            q = q.reshape(B, S, H, hd)
            k = k.reshape(B, S, H, hd)
            v = v.reshape(B, S, H, hd)
            scores = jnp.einsum('bqhd,bkhd->bhqk', q, k) * hd ** (-0.5)
            causal = jnp.tril(jnp.ones((S, S), bool))
            scores = jnp.where(causal, scores, jnp.finfo(scores.dtype).min)
            attn = jax.nn.softmax(scores, axis=-1)
            o = jnp.einsum('bhqk,bkhd->bqhd', attn, v).reshape(B, S, D)
            x_resid = x + o @ w_o
            moe_in = _layer_norm(x_resid, ln2_g, ln2_b)
            N = B * S
            xf = moe_in.reshape(N, D)
            probs = jax.nn.softmax(xf @ w_gate, axis=-1)
            top_w, top_i = jax.lax.top_k(probs, TOP_K)
            top_w = top_w / top_w.sum(-1, keepdims=True)
            E = w1.shape[0]
            out = jnp.zeros_like(xf)
            for e in range(E):
                gate_e = jnp.sum(jnp.where(top_i == e, top_w, 0.0), axis=-1)
                he = jax.nn.gelu(xf @ w1[e] + b1[e])
                out = out + gate_e[:, None] * (he @ w2[e] + b2[e])
            return out.reshape(B, S, D) + x_resid
        key = jax.random.key(seed)
        ks = jax.random.split(key, 12)
        B, S, D, F, E = (8, 128, 256, 1024, 8)
        inp = {'x': jax.random.normal(ks[0], (B, S, D), jnp.float32), 'ln1_g': jnp.ones((D,), jnp.float32), 'ln1_b': jnp.zeros((D,), jnp.float32), 'ln2_g': jnp.ones((D,), jnp.float32), 'ln2_b': jnp.zeros((D,), jnp.float32), 'w_qkv': jax.random.normal(ks[1], (D, 3 * D), jnp.float32) * D ** (-0.5), 'w_o': jax.random.normal(ks[2], (D, D), jnp.float32) * D ** (-0.5), 'w_gate': jax.random.normal(ks[3], (D, E), jnp.float32) * D ** (-0.5), 'w1': jax.random.normal(ks[4], (E, D, F), jnp.float32) * D ** (-0.5), 'b1': jnp.zeros((E, F), jnp.float32), 'w2': jax.random.normal(ks[5], (E, F, D), jnp.float32) * F ** (-0.5), 'b2': jnp.zeros((E, D), jnp.float32)}
        return inp
    _L0_ffn_in = _L0_ffn_setup()
    _d = {'L0_attn_x': _L0_attn_in['x'], 'L0_attn_Wq': _L0_attn_in['Wq'], 'L0_attn_bq': _L0_attn_in['bq'], 'L0_attn_Wk': _L0_attn_in['Wk'], 'L0_attn_Wv': _L0_attn_in['Wv'], 'L0_attn_bv': _L0_attn_in['bv'], 'L0_attn_Wo': _L0_attn_in['Wo'], 'L0_attn_bo': _L0_attn_in['bo'], 'L0_attn_lna_w': _L0_attn_in['lna_w'], 'L0_attn_lnc_w': _L0_attn_in['lnc_w'], 'L0_attn_lnd_w': _L0_attn_in['lnd_w'], 'L0_attn_Wlq': _L0_attn_in['Wlq'], 'L0_attn_blq': _L0_attn_in['blq'], 'L0_attn_Wlk': _L0_attn_in['Wlk'], 'L0_attn_blk': _L0_attn_in['blk'], 'L0_attn_Wlv': _L0_attn_in['Wlv'], 'L0_attn_blv': _L0_attn_in['blv'], 'L0_attn_temp': _L0_attn_in['temp'], 'L0_attn_threshold': _L0_attn_in['threshold'], 'L0_attn_factor': _L0_attn_in['factor'], 'L0_ffn_ln1_g': _L0_ffn_in['ln1_g'], 'L0_ffn_ln1_b': _L0_ffn_in['ln1_b'], 'L0_ffn_ln2_g': _L0_ffn_in['ln2_g'], 'L0_ffn_ln2_b': _L0_ffn_in['ln2_b'], 'L0_ffn_w_qkv': _L0_ffn_in['w_qkv'], 'L0_ffn_w_o': _L0_ffn_in['w_o'], 'L0_ffn_w_gate': _L0_ffn_in['w_gate'], 'L0_ffn_w1': _L0_ffn_in['w1'], 'L0_ffn_b1': _L0_ffn_in['b1'], 'L0_ffn_w2': _L0_ffn_in['w2'], 'L0_ffn_b2': _L0_ffn_in['b2']}
    _x0 = _d['L0_attn_x']
    _d['L0_attn_x'] = jax.random.normal(jax.random.fold_in(jax.random.key(seed), 1), (2, 2048, 256), dtype=_x0.dtype)
    del _x0
    return _d

def reference(L0_attn_x, L0_attn_Wq, L0_attn_bq, L0_attn_Wk, L0_attn_Wv, L0_attn_bv, L0_attn_Wo, L0_attn_bo, L0_attn_lna_w, L0_attn_lnc_w, L0_attn_lnd_w, L0_attn_Wlq, L0_attn_blq, L0_attn_Wlk, L0_attn_blk, L0_attn_Wlv, L0_attn_blv, L0_attn_temp, L0_attn_threshold, L0_attn_factor, L0_ffn_ln1_g, L0_ffn_ln1_b, L0_ffn_ln2_g, L0_ffn_ln2_b, L0_ffn_w_qkv, L0_ffn_w_o, L0_ffn_w_gate, L0_ffn_w1, L0_ffn_b1, L0_ffn_w2, L0_ffn_b2):

    def _L0_attn_ref(x, Wq, bq, Wk, Wv, bv, Wo, bo, lna_w, lnc_w, lnd_w, Wlq, blq, Wlk, blk, Wlv, blv, temp, threshold, factor):
        import jax, jax.numpy as jnp
        import numpy as np
        DIMS, HEAD = (256, 16)
        HD = DIMS // HEAD
        MAX_ITER = 3
        B, T = (4, 512)

        def _ln(x, w, eps=1e-05):
            m = jnp.mean(x, axis=-1, keepdims=True)
            v = jnp.var(x, axis=-1, keepdims=True)
            return (x - m) * jax.lax.rsqrt(v + eps) * w
        Bn, Tn, D = x.shape
        H, hd = (HEAD, HD)
        temp0 = jax.lax.stop_gradient(temp)
        thr = jax.lax.stop_gradient(threshold)
        fac = jax.lax.stop_gradient(factor)
        scale = hd ** (-0.25)
        xn = _ln(x, lna_w)
        q = (xn @ Wq.T + bq) * scale
        k = xn @ Wk.T * scale
        v = xn @ Wv.T + bv
        shp = lambda t: t.reshape(Bn, Tn, H, hd).transpose(0, 2, 1, 3)
        q, k, v = (shp(q), shp(k), shp(v))
        E = H
        sm_scale = 1.0 / float(np.sqrt(hd))
        qcur, kcur, vcur = (q, k, v)
        prev = jnp.zeros_like(q)
        attn_out = jnp.zeros_like(q)
        done = jnp.asarray(False)
        for it in range(MAX_ITER):
            ql = qcur[:, :, :E] @ Wlq.T + blq
            kl = kcur[:, :, :E] @ Wlk.T + blk
            vl = vcur[:, :, :E] @ Wlv.T + blv
            t_it = temp0 + 0.005 * it
            tscale = jnp.where((t_it != 1.0) & (t_it > 0), jax.lax.rsqrt(t_it), 1.0)
            qs = _ln(ql, lnc_w) * tscale
            ks_ = _ln(kl, lnd_w)
            logits = jnp.einsum('bhqd,bhkd->bhqk', qs, ks_) * sm_scale
            ai = jnp.einsum('bhqk,bhkd->bhqd', jax.nn.softmax(logits, axis=-1), vl)
            iter_out = jnp.zeros_like(qcur).at[:, :, :E].set(ai)
            diff = jnp.mean(jnp.abs(iter_out - prev))
            attn_out = jnp.where(done, attn_out, iter_out)
            done = done | (diff < thr + fac * diff) & (it > 0)
            prev = iter_out
            qcur = qcur + iter_out
            kcur, vcur = (kl, vl)
        out = attn_out.transpose(0, 2, 1, 3).reshape(Bn, Tn, D)
        return out @ Wo.T + bo

    def _L0_ffn_ref(x, ln1_g, ln1_b, ln2_g, ln2_b, w_qkv, w_o, w_gate, w1, b1, w2, b2):
        import jax, jax.numpy as jnp
        import numpy as np
        H = 16
        TOP_K = 2
        EPS = 1e-05

        def _layer_norm(x, g, b):
            m = x.mean(-1, keepdims=True)
            v = ((x - m) ** 2).mean(-1, keepdims=True)
            return (x - m) * jax.lax.rsqrt(v + EPS) * g + b

        def _block(x, ln1_g, ln1_b, ln2_g, ln2_b, w_qkv, w_o, w_gate, w1, b1, w2, b2):
            B, S, D = x.shape
            hd = D // H
            h = _layer_norm(x, ln1_g, ln1_b)
            qkv = h @ w_qkv
            q, k, v = jnp.split(qkv, 3, axis=-1)
            q = q.reshape(B, S, H, hd)
            k = k.reshape(B, S, H, hd)
            v = v.reshape(B, S, H, hd)
            scores = jnp.einsum('bqhd,bkhd->bhqk', q, k) * hd ** (-0.5)
            causal = jnp.tril(jnp.ones((S, S), bool))
            scores = jnp.where(causal, scores, jnp.finfo(scores.dtype).min)
            attn = jax.nn.softmax(scores, axis=-1)
            o = jnp.einsum('bhqk,bkhd->bqhd', attn, v).reshape(B, S, D)
            x_resid = x + o @ w_o
            moe_in = _layer_norm(x_resid, ln2_g, ln2_b)
            N = B * S
            xf = moe_in.reshape(N, D)
            probs = jax.nn.softmax(xf @ w_gate, axis=-1)
            top_w, top_i = jax.lax.top_k(probs, TOP_K)
            top_w = top_w / top_w.sum(-1, keepdims=True)
            E = w1.shape[0]
            out = jnp.zeros_like(xf)
            for e in range(E):
                gate_e = jnp.sum(jnp.where(top_i == e, top_w, 0.0), axis=-1)
                he = jax.nn.gelu(xf @ w1[e] + b1[e])
                out = out + gate_e[:, None] * (he @ w2[e] + b2[e])
            return out.reshape(B, S, D) + x_resid
        return _block(x, ln1_g, ln1_b, ln2_g, ln2_b, w_qkv, w_o, w_gate, w1, b1, w2, b2)
    x = L0_attn_x
    x = _layernorm(x + _L0_attn_ref(x, L0_attn_Wq, L0_attn_bq, L0_attn_Wk, L0_attn_Wv, L0_attn_bv, L0_attn_Wo, L0_attn_bo, L0_attn_lna_w, L0_attn_lnc_w, L0_attn_lnd_w, L0_attn_Wlq, L0_attn_blq, L0_attn_Wlk, L0_attn_blk, L0_attn_Wlv, L0_attn_blv, L0_attn_temp, L0_attn_threshold, L0_attn_factor), axis=-1)
    x = _layernorm(x + _L0_ffn_ref(x, L0_ffn_ln1_g, L0_ffn_ln1_b, L0_ffn_ln2_g, L0_ffn_ln2_b, L0_ffn_w_qkv, L0_ffn_w_o, L0_ffn_w_gate, L0_ffn_w1, L0_ffn_b1, L0_ffn_w2, L0_ffn_b2), axis=-1)
    return x

_drawn_inputs = setup_inputs


def setup_inputs(seed=0):
    import zlib

    import numpy as np

    out = dict(_drawn_inputs(seed))
    spreads = {'L0_attn_bq': (0.0, 2.0),
     'L0_attn_bv': (0.0, 0.8),
     'L0_attn_bo': (0.0, 0.1),
     'L0_attn_lna_w': (1.0, 0.6),
     'L0_attn_lnc_w': (1.0, 0.6),
     'L0_attn_lnd_w': (1.0, 0.6),
     'L0_attn_blq': (0.0, 2.0),
     'L0_attn_blk': (0.0, 0.8),
     'L0_attn_blv': (0.0, 0.8),
     'L0_ffn_ln1_g': (1.0, 0.2),
     'L0_ffn_ln1_b': (0.0, 0.1),
     'L0_ffn_ln2_g': (1.0, 0.2),
     'L0_ffn_ln2_b': (0.0, 0.1),
     'L0_ffn_b1': (0.0, 0.322),
     'L0_ffn_b2': (0.0, 0.1)}
    factors = {'L0_attn_Wq': 8.0,
     'L0_attn_Wk': 8.0,
     'L0_attn_Wv': 8.0,
     'L0_attn_Wo': 7.153,
     'L0_attn_Wlq': 8.0,
     'L0_attn_Wlk': 8.0,
     'L0_attn_Wlv': 8.0}
    for name, (base, spread) in spreads.items():
        noise = np.random.default_rng([zlib.crc32(name.encode()), seed]).standard_normal(out[name].shape)
        drawn = base * np.exp(spread * noise) if base else spread * noise
        out[name] = jnp.asarray(drawn.astype(out[name].dtype))
    for name, factor in factors.items():
        out[name] = (out[name] * factor).astype(out[name].dtype)
    return out
```

```python
from contextlib import ExitStack

import numpy as np

import concourse.bass as bass
from concourse import mybir

F32 = mybir.dt.float32
BF16 = mybir.dt.bfloat16
ACT = mybir.ActivationFunctionType
ALU = mybir.AluOpType
AX_X = mybir.AxisListType.X

P = 128
B, T, D, H = 2, 2048, 256, 16
HD = D // H
HALVES = D // P
HG = P // HD
NG = B * HALVES
N = B * T
CH = 512
CPB = T // CH
NC = N // CH
TPC = CH // P
KT = T // P
ITERS = 3
TA = H
XB = HALVES * B
E_, F_ = 8, 1024
FT = F_ // P
EPS = 1e-5
NEG = -3.0e38
SM = 1.0 / float(np.sqrt(HD))
QKS = HD ** -0.25
STACK = 6 * HD
ROWS = STACK + 3
Q_PARTS = (0, 0, 0, 1, 1, 2)
K_PARTS = (0, 1, 2, 0, 1, 0)
VW = 2 * HD

COLS = ["bq0", "bq1", "bv0", "bv1", "lna0", "lna1", "g1_0", "g1_1", "c1_0", "c1_1",
        "g2_0", "g2_1", "c2_0", "c2_1", "lnc", "lnd", "blq", "blk", "blv", "temp", "thr", "fac"]
COL = {n: i for i, n in enumerate(COLS)}


class Signal:

    def __init__(self, sem):
        self.sem, self.n = sem, 0


class Queues:

    ENGINES = ("tensor", "vector", "scalar", "gpsimd", "sync")

    def __init__(self, new_sem):
        self.q = {e: [] for e in self.ENGINES}
        self.seen = {e: {} for e in self.ENGINES}
        self.new_sem = new_sem
        self.done = {}
        self.rings = {}

    def phase(self, name):
        self.done = {e: Signal(self.new_sem(f"{e}_done_{name}")) for e in self.ENGINES[:4]}

    def _waits(self, eng, waits):
        need = []
        for w in waits:
            if w is None:
                continue
            sig, v = w
            if self.seen[eng].get(sig, 0) < v:
                self.seen[eng][sig] = v
                need.append((sig.sem, v))
        return need

    def op(self, eng, build, waits=(), mark=True):
        need = self._waits(eng, waits)
        sig = self.done[eng] if mark else None
        if mark:
            sig.n += 1
        self.q[eng].append((need, build, sig.sem if mark else None, 1))
        return (sig, sig.n) if mark else None

    def dma_on(self, signal, dst, src, waits=()):
        need = self._waits("sync", waits)
        signal.n += 16
        self.q["sync"].append((need, lambda e, d=dst, s=src: e.dma_start(d, s), signal.sem, 16))
        return (signal, signal.n)

    def dma(self, ring, dst, src, waits=(), depth=8):
        if ring not in self.rings:
            self.rings[ring] = ([Signal(self.new_sem(f"{ring}_{i}")) for i in range(depth)], [0])
        sigs, at = self.rings[ring]
        s = sigs[at[0] % len(sigs)]
        at[0] += 1
        return self.dma_on(s, dst, src, list(waits) + [(s, s.n)] * (s.n > 0))

    def play(self, name, eng):
        for need, build, sem, by in self.q[name]:
            for s, v in need:
                eng.wait_ge(s, v)
            ins = build(eng)
            if sem is not None:
                ins.then_inc(sem, by)


def build_program(nc, a, out):
    ctx = ExitStack()
    with ctx:
        def sem(name):
            return ctx.enter_context(nc.semaphore(name))

        Q = Queues(sem)

        def sb(stack, name, shape, dt=F32):
            return stack.enter_context(nc.sbuf_tensor(name, shape, dt))

        def dram(name, shape, dt=F32):
            return nc.dram_tensor(name, shape, dt, kind="Internal").ap()

        psum = ctx.enter_context(nc.psum_tensor("psum", [P, 8 * CH], F32))
        banks = [psum[:, i * CH:(i + 1) * CH] for i in range(8)]
        bank_free = [None] * 8

        o_ffn = dram("o_ffn", [NG, P, T])
        parts = [{k: dram(f"parts_{k}{i}", [3, P, T], BF16) for k in "qk"} for i in range(NG)]
        x1_d = dram("x1_d", [N, D])

        cst = sb(ctx, "cst", [P, 7 * P])
        ident, bmean, center, mask_s, mask_t, ones, same = (cst[:, i * P:(i + 1) * P] for i in range(7))
        cols = sb(ctx, "cols", [P, len(COLS)])
        ident_bf = sb(ctx, "ident_bf", [P, P], BF16)
        mask_s_bf = sb(ctx, "mask_s_bf", [P, P], BF16)
        mask_t_bf = sb(ctx, "mask_t_bf", [P, P], BF16)
        eps_col = sb(ctx, "eps_col", [P, 1])
        wlin = {k: sb(ctx, f"wl_{k}", [P, P]) for k in "qkv"}
        wnq = sb(ctx, "wnq", [P, ITERS])
        ts_tmp = sb(ctx, "ts_tmp", [P, 4])
        diff_cols = sb(ctx, "diff_cols", [P, 1])
        flag = sb(ctx, "flag", [P, 4])
        v_stack = ExitStack()
        v_tok = sb(v_stack, "v_tok", [P, NG, KT, HG, VW])

        def col(name):
            return cols[:, COL[name]:COL[name] + 1]

        Q.phase("setup")
        setup_in = Signal(sem("setup_in"))
        Q.dma_on(setup_in, cst[:, :], a["consts"])
        m_small = Q.dma_on(setup_in, cols[:, :], a["cols"])
        m_blocks = []
        m_zero = None
        for k in "qkv":
            m_zero = Q.op("vector", lambda e, k=k: e.memset(wlin[k][:, :], 0.0))
        blocks_in = Signal(sem("blocks_in"))
        for k in "qkv":
            for g in range(HG):
                s = slice(g * HD, (g + 1) * HD)
                m_blocks = Q.dma_on(blocks_in, wlin[k][s, s], a[f"Wl{k}T"], [m_zero])
        m_c = None
        for d, s in ((ident_bf, ident), (mask_s_bf, mask_s), (mask_t_bf, mask_t)):
            m_c = Q.op("vector", lambda e, d=d, s=s: e.tensor_copy(d[:, :], s), [m_small])
        m_eps = Q.op("vector", lambda e: e.memset(eps_col[:, :], EPS))
        m_ones_v = Q.op("gpsimd", lambda e: e.memset(v_tok[:, :, :, :, HD:VW], 1.0))
        Q.op("scalar", lambda e: nc.scalar.preload_act_table_set("natural_log_exp_and_others"), mark=False)
        prev = None
        for it in range(ITERS):
            t_, r_, c_, d_ = (ts_tmp[:, i:i + 1] for i in range(4))
            m = Q.op("vector", lambda e, it=it, t_=t_: e.tensor_scalar(t_, col("temp"), 0.005 * it, None, ALU.add),
                     [m_small, prev])
            m2 = Q.op("vector", lambda e, r_=r_, t_=t_: e.tensor_scalar(r_, t_, 1e-18, None, ALU.max), [m])
            m3 = Q.op("vector", lambda e, c_=c_, t_=t_: e.tensor_scalar(c_, t_, 1.0, None, ALU.not_equal), [m])
            m4 = Q.op("vector", lambda e, d_=d_, t_=t_: e.tensor_scalar(d_, t_, 0.0, None, ALU.is_gt), [m])
            m5 = Q.op("vector", lambda e, c_=c_, d_=d_: e.tensor_tensor(c_, c_, d_, ALU.mult), [m3, m4])
            a1 = Q.op("scalar", lambda e, r_=r_: e.activation(r_, r_, ACT.Ln), [m2])
            a2 = Q.op("scalar", lambda e, r_=r_: e.activation(r_, r_, ACT.Exp, scale=-0.5), [a1])
            m6 = Q.op("vector", lambda e, r_=r_, c_=c_: e.scalar_tensor_tensor(r_, r_, -1.0, c_, ALU.add, ALU.mult),
                      [a2, m5])
            m7 = Q.op("vector", lambda e, r_=r_: e.tensor_scalar(r_, r_, 1.0, SM, ALU.add, ALU.mult), [m6])
            prev = Q.op("vector", lambda e, r_=r_, it=it: e.tensor_tensor(wnq[:, it:it + 1], r_, col("lnc"), ALU.mult),
                        [m7])
        m_wnq = prev

        def norm4(st, src, dst, waits, free=()):
            m = None
            for j in range(TPC):
                m = Q.op("vector", lambda e, j=j: e.bn_stats(st[:, j, 0:6], src[:, j, :]), list(waits) + list(free),
                         mark=j == TPC - 1)
            mv = None
            for j in range(TPC):
                mv = Q.op("vector", lambda e, j=j: e.bn_aggr(st[:, j, 6:8], st[:, j, 0:6]), [m], mark=j == TPC - 1)
            s1 = Q.op("scalar", lambda e: e.activation(st[:, :, 8], st[:, :, 7], ACT.Ln, bias=eps_col[:, :]), [mv, m_eps])
            s2 = Q.op("scalar", lambda e: e.activation(st[:, :, 8], st[:, :, 8], ACT.Exp, scale=-0.5), [s1])
            for j in range(TPC):
                m = Q.op("vector", lambda e, j=j: e.tensor_scalar(dst[:, j, :], src[:, j, :], st[:, j, 6:7],
                                                                 st[:, j, 8:9], ALU.subtract, ALU.mult), [s2, mv],
                         mark=j == TPC - 1)
            return m

        def transpose4(src, dst, b0, scales, biases, waits, free):
            marks = []
            for h in range(HALVES):
                bk = b0 + h
                for j in range(TPC):
                    m = Q.op("tensor", lambda e, h=h, j=j, bk=bk: e.transpose(
                        banks[bk][:, j * P:(j + 1) * P], src[:, j, h * P:(h + 1) * P], ident),
                        list(waits) + [bank_free[bk], m_small], mark=j == TPC - 1)
                kw = {} if biases is None else {"bias": biases[h]}
                bank_free[bk] = Q.op("scalar", lambda e, h=h, bk=bk, kw=kw: e.activation(
                    dst[h], banks[bk][:, :], ACT.Identity, scale=scales[h], **kw), [m, m_small] + list(free))
                marks.append(bank_free[bk])
            return marks[-1]

        Q.phase("mid")
        parts_stored, v_ready = {}, {}
        ORDER = [c for c in range(NC) if c % CPB] + [c for c in range(NC) if c % CPB == 0]
        with ExitStack() as st1:
            w_in = {k: sb(st1, f"w{k}_sb", [P, HALVES, D]) for k in "qkvo"}
            wqkv = sb(st1, "wqkv", [P, HALVES, 3 * D])
            bo4 = sb(st1, "bo4", [P, TPC, D])
            y_first = sb(st1, "y_first", [TA, B, D])
            weights_in = Signal(sem("weights_in"))
            xs = sb(st1, "xs", [B * TA, D])
            for b in range(B):
                Q.dma_on(weights_in, xs[b * TA:(b + 1) * TA, :], a["x"][b * T:b * T + TA, :])
            Q.dma_on(weights_in, bo4[:, :, :], a["bo4"].rearrange("p (j d) -> p j d", j=TPC))
            for k in "qkvo":
                Q.dma_on(weights_in, w_in[k][:, :, :], a[f"W{k}T"].rearrange("(h p) o -> p h o", p=P))
            m_w = Q.dma_on(weights_in, wqkv[:, :, :], a["w_qkv"].rearrange("(h p) o -> p h o", p=P))

            W = XB * TA
            B_LIN, B_CEN = 6, 7
            f_stat = sb(st1, "f_stat", [B * TA, 9])
            f_xn = sb(st1, "f_xn", [B * TA, D])
            f_xT = sb(st1, "f_xT", [P, HALVES, B * TA])
            f_cur = {k: sb(st1, f"f_cur_{k}", [P, W]) for k in "qkv"}
            f_lin = sb(st1, "f_lin", [P, 3 * W])
            f_cen = sb(st1, "f_cen", [P, 2 * W])
            f_sq = sb(st1, "f_sq", [P, 2 * W])
            f_rs = sb(st1, "f_rs", [P, 2 * W])
            f_nrm = sb(st1, "f_nrm", [P, 2 * W])
            f_kbd = sb(st1, "f_kbd", [P, XB, P])
            f_vbd = sb(st1, "f_vbd", [P, XB, P])
            f_vT = sb(st1, "f_vT", [P, XB, P])
            f_p = sb(st1, "f_p", [TA, XB * HG, TA])
            f_pT = sb(st1, "f_pT", [P, W])
            f_red = sb(st1, "f_red", [TA, XB * HG])
            f_out = [sb(st1, f"f_out{i}", [P, W]) for i in range(ITERS)]
            f_o = sb(st1, "f_o", [P, W])
            first_y = []

            def first_attention():
                last = [None]

                def step(eng, f, more=(), mark=True):
                    last[0] = Q.op(eng, f, [last[0]] + list(more))

                bank = [B_LIN]

                def flip():
                    bank[0] = B_LIN + B_CEN - bank[0]
                    return banks[bank[0]]

                step("vector", lambda e: e.bn_stats(f_stat[:, 0:6], xs[:, :]), [m_w, m_wnq])
                yield
                step("vector", lambda e: e.bn_aggr(f_stat[:, 6:8], f_stat[:, 0:6]))
                yield
                step("scalar", lambda e: e.activation(f_stat[:, 8:9], f_stat[:, 7:8], ACT.Ln, bias=eps_col[0:B * TA, :]), [m_eps])
                step("scalar", lambda e: e.activation(f_stat[:, 8:9], f_stat[:, 8:9], ACT.Exp, scale=-0.5))
                yield
                step("vector", lambda e: e.tensor_scalar(f_xn[:, :], xs[:, :], f_stat[:, 6:7], f_stat[:, 8:9],
                                                         ALU.subtract, ALU.mult))
                yield
                bk = flip()
                for h in range(HALVES):
                    step("tensor", lambda e, h=h, bk=bk: e.transpose(bk[:, h * B * TA:(h + 1) * B * TA],
                                                                    f_xn[:, h * P:(h + 1) * P], ident[0:B * TA, 0:B * TA]),
                         [m_w, m_small])
                for h in range(HALVES):
                    step("vector", lambda e, h=h, bk=bk: e.tensor_scalar(
                        f_xT[:, h, :], bk[:, h * B * TA:(h + 1) * B * TA], col(f"lna{h}"), None, ALU.mult))
                yield
                bk = flip()
                for i, k in enumerate("qkv"):
                    for o in range(HALVES):
                        at = slice(i * W + o * B * TA, i * W + (o + 1) * B * TA)
                        for h in range(HALVES):
                            m = Q.op("tensor", lambda e, k=k, o=o, h=h, at=at, bk=bk: e.matmul(
                                bk[:, at], w_in[k][:, h, o * P:(o + 1) * P], f_xT[:, h, :], start=h == 0, stop=h == 1),
                                [last[0]], mark=h == 1)
                last[0] = m
                for i, k in enumerate("qkv"):
                    for o in range(HALVES):
                        at = slice(i * W + o * B * TA, i * W + (o + 1) * B * TA)
                        dst = f_cur[k][:, o * B * TA:(o + 1) * B * TA]
                        if k == "q":
                            f = lambda e, at=at, dst=dst, o=o, bk=bk: e.tensor_scalar(dst, bk[:, at], col(f"bq{o}"), QKS,
                                                                                     ALU.add, ALU.mult)
                        elif k == "k":
                            f = lambda e, at=at, dst=dst, bk=bk: e.tensor_scalar(dst, bk[:, at], QKS, None, ALU.mult)
                        else:
                            f = lambda e, at=at, dst=dst, o=o, bk=bk: e.tensor_scalar(dst, bk[:, at], col(f"bv{o}"), None,
                                                                                     ALU.add)
                        step("vector", f)
                yield
                for it in range(ITERS):
                    src = dict(f_cur) if it == 0 else {"q": f_cur["q"], "k": f_lin[:, W:2 * W], "v": f_lin[:, 2 * W:3 * W]}
                    bk = flip()
                    for i, k in enumerate("qkv"):
                        step("tensor", lambda e, i=i, s=src[k], k=k, bk=bk: e.matmul(
                            bk[:, i * W:(i + 1) * W], wlin[k][:, :], s[:, :], start=True, stop=True), [m_blocks])
                    for i, k in enumerate("qkv"):
                        step("vector", lambda e, i=i, k=k, bk=bk: e.tensor_scalar(
                            f_lin[:, i * W:(i + 1) * W], bk[:, i * W:(i + 1) * W], col("bl" + k), None, ALU.add))
                    yield
                    bk = flip()
                    step("tensor", lambda e, bk=bk: e.matmul(bk[:, 0:2 * W], center, f_lin[:, 0:2 * W], start=True, stop=True))
                    step("vector", lambda e, bk=bk: e.tensor_copy(f_cen[:, :], bk[:, 0:2 * W]))
                    step("vector", lambda e: e.tensor_tensor(f_sq[:, :], f_cen[:, :], f_cen[:, :], ALU.mult))
                    yield
                    bk = flip()
                    step("tensor", lambda e, bk=bk: e.matmul(bk[:, 0:2 * W], bmean, f_sq[:, :], start=True, stop=True))
                    step("scalar", lambda e, bk=bk: e.activation(f_rs[:, :], bk[:, 0:2 * W], ACT.Ln, bias=eps_col[:, :]))
                    step("scalar", lambda e: e.activation(f_rs[:, :], f_rs[:, :], ACT.Exp, scale=-0.5))
                    yield
                    for i, w in ((0, wnq[:, it:it + 1]), (1, col("lnd"))):
                        step("vector", lambda e, i=i, w=w: e.scalar_tensor_tensor(
                            f_nrm[:, i * W:(i + 1) * W], f_cen[:, i * W:(i + 1) * W], w, f_rs[:, i * W:(i + 1) * W],
                            ALU.mult, ALU.mult))
                    for dst, s0 in ((f_kbd, f_nrm[:, W:2 * W]), (f_vbd, f_lin[:, 2 * W:3 * W])):
                        for x in range(XB):
                            step("vector", lambda e, dst=dst, s0=s0, x=x: e.tensor_tensor(
                                dst[:, x, :].rearrange("p (h t) -> p h t", h=HG),
                                s0[:, x * TA:(x + 1) * TA].unsqueeze(1).to_broadcast([P, HG, TA]),
                                same.rearrange("p (h t) -> p h t", h=HG), ALU.mult))
                        yield
                    bk = flip()
                    for x in range(XB):
                        step("tensor", lambda e, x=x, bk=bk: e.matmul(
                            bk[0:TA, x * P:(x + 1) * P], f_nrm[:, x * TA:(x + 1) * TA], f_kbd[:, x, :],
                            start=True, stop=True))
                    s3 = bk[0:TA, :].rearrange("p (x t) -> p x t", t=TA)

                    def bc(v):
                        return v[:, :].unsqueeze(2).to_broadcast([TA, XB * HG, TA])
                    step("vector", lambda e, s3=s3: e.tensor_reduce(f_red[:, :], s3, AX_X, ALU.max))
                    step("vector", lambda e, s3=s3, bc=bc: e.tensor_tensor(f_p[:, :, :], s3, bc(f_red), ALU.subtract))
                    yield
                    step("scalar", lambda e: e.activation(f_p[:, :, :], f_p[:, :, :], ACT.Exp))
                    step("vector", lambda e: e.tensor_reduce(f_red[:, :], f_p[:, :, :], AX_X, ALU.add))
                    step("vector", lambda e: e.reciprocal(f_red[:, :], f_red[:, :]))
                    step("vector", lambda e, bc=bc: e.tensor_tensor(f_p[:, :, :], f_p[:, :, :], bc(f_red), ALU.mult))
                    yield
                    bk = flip()
                    for x in range(XB):
                        step("tensor", lambda e, x=x, bk=bk: e.transpose(
                            bk[:, x * TA:(x + 1) * TA], f_p[:, x * HG:(x + 1) * HG, :].rearrange("p h t -> p (h t)"),
                            ident[0:TA, 0:TA]))
                    step("vector", lambda e, bk=bk: e.tensor_copy(f_pT[:, :], bk[:, 0:W]))
                    yield
                    bk = flip()
                    for x in range(XB):
                        step("tensor", lambda e, x=x, bk=bk: e.transpose(bk[:, x * P:(x + 1) * P], f_vbd[:, x, :], ident))
                    step("vector", lambda e, bk=bk: e.tensor_copy(f_vT[:, :, :], bk.rearrange("p (x f) -> p x f", x=XB)))
                    yield
                    bk = flip()
                    for x in range(XB):
                        step("tensor", lambda e, x=x, bk=bk: e.matmul(
                            bk[:, x * TA:(x + 1) * TA], f_vT[:, x, :], f_pT[:, x * TA:(x + 1) * TA], start=True, stop=True))
                    step("vector", lambda e, it=it, bk=bk: e.tensor_copy(f_out[it][:, :], bk[:, 0:W]))
                    step("vector", lambda e, it=it: e.tensor_tensor(f_cur["q"][:, :], f_cur["q"][:, :], f_out[it][:, :],
                                                                   ALU.add))
                    yield
                dsum, dlim, dflag, nflag = (flag[:, i:i + 1] for i in range(4))
                step("vector", lambda e: e.tensor_tensor(f_sq[:, 0:W], f_out[1][:, :], f_out[0][:, :], ALU.subtract))
                step("vector", lambda e: e.tensor_reduce(diff_cols[:, :], f_sq[:, 0:W], AX_X, ALU.add,
                                                         apply_absolute_value=True))
                bk = flip()
                step("tensor", lambda e, bk=bk: e.matmul(bk[:, 0:1], ones, diff_cols[:, :], start=True, stop=True))
                step("vector", lambda e, bk=bk: e.tensor_scalar(dsum, bk[:, 0:1], 1.0 / (N * D), None, ALU.mult))
                step("vector", lambda e: e.scalar_tensor_tensor(dlim, dsum, col("fac"), col("thr"), ALU.mult, ALU.add))
                step("vector", lambda e: e.tensor_tensor(dflag, dsum, dlim, ALU.is_lt))
                step("vector", lambda e: e.tensor_scalar(nflag, dflag, -1.0, 1.0, ALU.mult, ALU.add))
                step("vector", lambda e: e.tensor_scalar(f_o[:, :], f_out[1][:, :], dflag, None, ALU.mult))
                step("vector", lambda e: e.scalar_tensor_tensor(f_o[:, :], f_out[2][:, :], nflag, f_o[:, :],
                                                                ALU.mult, ALU.add))
                yield
                bk = flip()
                for b in range(B):
                    for h in range(HALVES):
                        at = slice((h * B + b) * TA, (h * B + b + 1) * TA)
                        m = Q.op("tensor", lambda e, b=b, h=h, at=at, bk=bk: e.matmul(
                            bk[0:TA, b * D:(b + 1) * D], f_o[:, at], w_in["o"][:, h, :], start=h == 0, stop=h == 1),
                            [last[0]], mark=h == 1)
                last[0] = m
                step("vector", lambda e, bk=bk: e.tensor_copy(y_first[:, :, :], bk[0:TA, :].rearrange("p (b d) -> p b d", b=B)))
                first_y.append(last[0])
                yield

            xr = [sb(st1, f"xr{i}", [P, TPC, D]) for i in range(3)]
            x1t = [sb(st1, f"x1t{i}", [P, TPC, D]) for i in range(2)]
            hno = [sb(st1, f"hno{i}", [P, TPC, D]) for i in range(2)]
            hT = [sb(st1, f"hT{i}", [P, HALVES, CH]) for i in range(2)]
            stt = [sb(st1, f"st1_{i}", [P, TPC, 9]) for i in range(4)]
            sp = [[sb(st1, f"sp{i}{n}", [P, CH], BF16) for n in ("hi", "mid", "lo")] + [sb(st1, f"sp{i}rem", [P, CH])]
                  for i in range(2)]
            ld, x1m, hm, htm, mm_h, st_x1 = {}, {}, {}, {}, {}, {}
            spn, sp_free = [0], [[], []]

            def mid_load(i):
                c = ORDER[i]
                ld[i] = Q.dma("mid_in", xr[i % 3][:, :, :], a["x"][c * CH:(c + 1) * CH, :].rearrange("(j p) d -> p j d", p=P),
                              [x1m.get(i - 3)])

            def mid_a(i):
                c, r = ORDER[i], i % 2
                x = xr[i % 3]
                m = Q.op("gpsimd", lambda e: e.tensor_tensor(x[:, :, :], x[:, :, :], bo4[:, :, :], ALU.add), [ld[i], m_w])
                if c % CPB == 0:
                    b = c // CPB
                    m = Q.op("vector", lambda e: e.tensor_tensor(x[0:TA, 0, :], x[0:TA, 0, :], y_first[:, b, :], ALU.add),
                             [m, first_y[0]])
                x1m[i] = norm4(stt[r], x, x1t[r], [m], [st_x1.get(i - 2), hm.get(i - 2)])
                st_x1[i] = Q.dma("x1_out", x1_d[c * CH:(c + 1) * CH, :].rearrange("(j p) d -> p j d", p=P),
                                 x1t[r][:, :, :], [x1m[i]])
                hm[i] = norm4(stt[2 + r], x1t[r], hno[r], [x1m[i]], [htm.get(i - 2)])

            def mid_b(i):
                c, r = ORDER[i], i % 2
                b, cc = c // CPB, c % CPB
                at = slice(cc * CH, (cc + 1) * CH)
                htm[i] = transpose4(hno[r], [hT[r][:, h, :] for h in range(HALVES)], 0,
                                    [col("g1_0"), col("g1_1")], [col("c1_0"), col("c1_1")], [hm[i]], [mm_h.get(i - 2)])
                for kind, o0 in (("q", 0), ("k", D)):
                    for o in range(HALVES):
                        k = spn[0] % 2
                        bk = 2 + k
                        spn[0] += 1
                        for h in range(HALVES):
                            m = Q.op("tensor", lambda e, h=h, o=o, o0=o0, bk=bk: e.matmul(
                                banks[bk][:, :], wqkv[:, h, o0 + o * P:o0 + (o + 1) * P], hT[r][:, h, :],
                                start=h == 0, stop=h == 1), [htm[i], m_w, bank_free[bk]], mark=h == 1)
                        sc = SM if kind == "q" else 1.0
                        hi, mid, lo, rem = sp[k]
                        g = b * HALVES + o
                        m1 = Q.op("scalar", lambda e, hi=hi, bk=bk, sc=sc: e.activation(
                            hi[:, :], banks[bk][:, :], ACT.Identity, scale=sc), [m] + sp_free[k])
                        m2 = Q.op("vector", lambda e, hi=hi, rem=rem, bk=bk, sc=sc: e.scalar_tensor_tensor(
                            rem[:, :], banks[bk][:, :], sc, hi[:, :], ALU.mult, ALU.subtract), [m1])
                        bank_free[bk] = m2
                        m3 = Q.op("vector", lambda e, mid=mid, rem=rem: e.tensor_copy(mid[:, :], rem[:, :]),
                                  [m2] + sp_free[k])
                        m4 = Q.op("vector", lambda e, mid=mid, rem=rem, lo=lo: e.tensor_tensor(
                            lo[:, :], rem[:, :], mid[:, :], ALU.subtract), [m3])
                        sp_free[k] = [Q.dma("parts_out", parts[g][kind][n, :, at], t[:, :], [mm])
                                      for n, (t, mm) in enumerate(((hi, m1), (mid, m3), (lo, m4)))]
                        parts_stored.setdefault(g, []).extend(sp_free[k])
                for j in range(TPC):
                    bk = 4 + j // 2
                    for h in range(HALVES):
                        m = Q.op("tensor", lambda e, j=j, h=h, bk=bk: e.matmul(
                            banks[bk][:, (j % 2) * D:(j % 2 + 1) * D], hT[r][:, h, j * P:(j + 1) * P],
                            wqkv[:, h, 2 * D:3 * D], start=h == 0, stop=h == 1), [htm[i], bank_free[bk]], mark=h == 1)
                    if j % 2 == 0:
                        continue
                    for jj in (j - 1, j):
                        for o in range(HALVES):
                            bank_free[bk] = Q.op("scalar", lambda e, j=jj, o=o, bk=bk, kt=cc * TPC + jj: e.activation(
                                v_tok[:, b * HALVES + o, kt, :, 0:HD],
                                banks[bk][:, (j % 2) * D + o * P:(j % 2) * D + (o + 1) * P].rearrange(
                                    "p (h d) -> p h d", h=HG), ACT.Identity), [m, m_ones_v])
                            v_ready[b * HALVES + o] = bank_free[bk]
                mm_h[i] = m

            chain = first_attention()
            PIECES = 4

            def pump(n):
                for _ in range(n):
                    next(chain, None)

            for i in range(3):
                mid_load(i)
            mid_a(0)
            for i in range(NC):
                if i + 1 < NC:
                    if ORDER[i + 1] % CPB == 0:
                        for _ in chain:
                            pass
                    mid_a(i + 1)
                if i + 3 < NC:
                    mid_load(i + 3)
                pump(PIECES)
                mid_b(i)
                pump(PIECES)
            mid_end = [(s, s.n) for s in Q.done.values()] + [x for f in sp_free for x in f] + [st_x1[NC - 1], st_x1[NC - 2]]

        def attention(bufs, heads, fillers, on_assembled, start):
            LEAD = 3
            AHEAD = KT + LEAD
            S_BANKS, T_BANKS, PV, MISC = ((0, 1), (2, 3)), (4, 5), 6, 7
            n_heads = len(heads)
            reduced = [None, None]
            s_at, t_at = [0], [0]
            t_marks = [None, None]
            stack_mark, nmax_mark, s_last, t_last = {}, {}, {}, {}
            pv_mark, exp_mark, evac = {}, {}, {}
            max_marks = {}
            oev_dma = {}

            def load_stack(n):
                inst, hh = heads[n]
                sl = n % 3
                sig = bufs["stack_sig"][sl]
                waits = [t_last.get(n - 3), s_last.get(n - 3)] + list(parts_stored[inst])
                for j in range(6):
                    rows = slice(hh * HD, (hh + 1) * HD)
                    dst = slice(j * HD, (j + 1) * HD)
                    Q.dma_on(sig, bufs["qst"][sl][dst, :], parts[inst]["q"][Q_PARTS[j], rows, :], waits)
                    stack_mark[n] = Q.dma_on(sig, bufs["kst"][sl][dst, :], parts[inst]["k"][K_PARTS[j], rows, :], waits)

            def scores(n, qt):
                sl, width = n % 3, (qt + 1) * P
                mx = bufs["mx"][n % 2]
                for half in range(2):
                    w = min(width - half * 2 * CH, 2 * CH)
                    if w <= 0:
                        continue
                    buf = s_at[0] % 2
                    s_at[0] += 1
                    m = None
                    for i in range((w + CH - 1) // CH):
                        k0 = half * 2 * CH + i * CH
                        kw = min(CH, width - k0)
                        bk = S_BANKS[buf][i]
                        diag = k0 <= qt * P < k0 + CH
                        last = i == (w + CH - 1) // CH - 1
                        m = Q.op("tensor", lambda e, bk=bk, k0=k0, kw=kw, diag=diag: e.matmul(
                            banks[bk][:, 0:kw], bufs["qst"][sl][0:STACK, qt * P:(qt + 1) * P],
                            bufs["kst"][sl][0:STACK, k0:k0 + kw], start=True, stop=not diag),
                            [reduced[buf], stack_mark[n]] + start, mark=last and not diag)
                        if diag:
                            off = qt * P - k0
                            m = Q.op("tensor", lambda e, bk=bk, off=off: e.matmul(
                                banks[bk][:, off:off + P], ident_bf[:, :], mask_s_bf[:, :], start=False, stop=True),
                                [m_c], mark=last)
                    s_last[n] = m
                    src = (bufs["s_wide"][buf][:, 0:w])
                    reduced[buf] = Q.op("vector", lambda e, src=src, qt=qt, half=half: e.tensor_reduce(
                        mx[:, qt, half:half + 1], src, AX_X, ALU.max), [m, max_marks.get(n - 2), bufs["ones_mark"]])

            def combine_max(n):
                mx, mf = bufs["mx"][n % 2], bufs["mf"]
                max_marks[n] = Q.op("vector", lambda e: e.tensor_reduce(mf[:, :], mx[:, :, :], AX_X, ALU.max),
                                    [reduced[0], reduced[1], bank_free[MISC]])

            def turn_max(n):
                mf, nm, rem, mp = bufs["mf"], bufs["nm"], bufs["nm_rem"], bufs["nm_parts"][n % 2]
                m = Q.op("tensor", lambda e: e.transpose(banks[MISC][0:KT, 0:P], mf[:, :], ident),
                         [max_marks[n], bank_free[MISC]])
                v0 = Q.op("vector", lambda e: e.tensor_scalar(nm[:, :], banks[MISC][0:KT, 0:P], -1.0, None, ALU.mult),
                          [m, bufs.get("nm_free")])
                bank_free[MISC] = v0
                v1 = Q.op("vector", lambda e: e.tensor_copy(mp[:, 0, :], nm[:, :]), [v0, nmax_mark.get(n - 2)])
                v2 = Q.op("vector", lambda e: e.tensor_tensor(rem[:, :], nm[:, :], mp[:, 0, :], ALU.subtract), [v1])
                v3 = Q.op("vector", lambda e: e.tensor_copy(mp[:, 1, :], rem[:, :]), [v2])
                v4 = Q.op("vector", lambda e: e.tensor_tensor(mp[:, 2, :], rem[:, :], mp[:, 1, :], ALU.subtract), [v3])
                bufs["nm_free"] = v4
                sl = n % 3
                for i in range(3):
                    nmax_mark[n] = Q.dma_on(bufs["nmax_sig"][sl], bufs["qst"][sl][STACK + i:STACK + i + 1, :].rearrange(
                        "p (q t) -> p q t", q=KT), mp[:, i, :], [v4, t_last.get(n - 3)])

            def chunks(kt):
                c0 = kt * P // CH
                return [(c, kt * P - c0 * CH if c == c0 else 0) for c in range(c0, CPB)]

            def scores_t(t, c, off):
                n, kt = t // KT, t % KT
                sl, r = n % 3, t_at[0] % 2
                bk = T_BANKS[r]
                t_at[0] += 1
                diag = kt * P // CH == c
                m = Q.op("tensor", lambda e: e.matmul(
                    banks[bk][:, off:CH], bufs["kst"][sl][0:ROWS, kt * P:(kt + 1) * P],
                    bufs["qst"][sl][0:ROWS, c * CH + off:(c + 1) * CH], start=True, stop=not diag),
                    [t_marks[r], nmax_mark[n], bufs["ones_mark"]], mark=not diag)
                if diag:
                    m = Q.op("tensor", lambda e: e.matmul(banks[bk][:, off:off + P], ident_bf[:, :], mask_t_bf[:, :],
                                                         start=False, stop=True), [m_c])
                t_last[n] = m
                t_marks[r] = Q.op("scalar", lambda e: e.activation(
                    bufs["p"][t % 3][:, c * CH + off:(c + 1) * CH], banks[bk][:, off:CH], ACT.Exp),
                    [m, pv_mark.get(t - 3)])
                exp_mark[t] = t_marks[r]

            def values(t):
                n, kt = t // KT, t % KT
                g, hh = heads[n]
                for r in range(CPB):
                    m0 = max(0, -((r - kt) // CPB))
                    if m0 >= KT // CPB:
                        continue
                    mov = bufs["p"][t % 3][:, :].rearrange("p (m r i) -> p r m i", r=CPB, i=P)[:, r, m0:, :]
                    m = Q.op("tensor", lambda e, r=r, m0=m0, mov=mov: e.matmul(
                        banks[PV][r * VW:(r + 1) * VW, m0 * P:CH], v_tok[:, g, kt, hh, :], mov,
                        start=kt == 0, stop=kt == KT - CPB + r),
                        [exp_mark[t], v_ready[g], bank_free[PV] if kt == 0 else None], mark=r == CPB - 1)
                pv_mark[t] = m

            def evacuate(n):
                inst, hh = heads[n]
                o = bufs["oev"][n % 2]
                bank_free[PV] = Q.op("scalar", lambda e: e.activation(o[:, :], banks[PV][:, :], ACT.Identity),
                                     [pv_mark[n * KT + KT - 1]] + list(oev_dma.get(n - 2, ())))
                marks = []
                rows = slice(hh * HD, (hh + 1) * HD)
                for r in range(CPB):
                    for buf, r0 in (("num", r * VW), ("den", r * VW + HD)):
                        dst = bufs[buf][inst % 2][rows, :].rearrange("p (m r i) -> p r m i", r=CPB, i=P)[:, r, :, :]
                        marks.append(Q.dma("assemble", dst, o[r0:r0 + HD, :].rearrange("p (m i) -> p m i", i=P),
                                           [bank_free[PV]] + list(asm_free.get(inst - 2, ())), depth=16))
                oev_dma[n] = marks
                on_assembled.setdefault(inst, []).extend(marks)

            last_t = n_heads * KT
            for t in range(-2 * KT, last_t + 1):
                if t % KT == 0 and 0 <= t // KT + 2 < n_heads:
                    load_stack(t // KT + 2)
                s = t + AHEAD
                todo = chunks(t % KT) if 0 <= t < last_t else []
                for c, off in todo[:2]:
                    scores_t(t, c, off)
                s_ok = 0 <= s < n_heads * KT
                if s_ok:
                    scores(s // KT, s % KT)
                for c, off in todo[2:]:
                    scores_t(t, c, off)
                if 0 <= t - 1 < last_t:
                    values(t - 1)
                    if (t - 1) % KT == KT - 1:
                        evacuate((t - 1) // KT)
                if s_ok and s % KT == KT - 1:
                    combine_max(s // KT)
                if 0 <= s - 1 < n_heads * KT and (s - 1) % KT == KT - 1:
                    turn_max((s - 1) // KT)
                for f in fillers.get(t, ()):
                    f()
            for extra in sorted(k for k in fillers if k > last_t):
                for f in fillers[extra]:
                    f()

        Q.phase("attn")
        att = ExitStack()
        bufs = {
            "stack_sig": [Signal(sem(f"stack_in{i}")) for i in range(3)],
            "nmax_sig": [Signal(sem(f"nmax_in{i}")) for i in range(3)],
            "s_wide": [psum[:, 2 * i * CH:2 * (i + 1) * CH] for i in range(2)],
        }
        for name, shape, dt, cnt in (("qst", [P, T], BF16, 3), ("kst", [P, T], BF16, 3), ("p", [P, T], F32, 3),
                                     ("num", [P, T], F32, 2), ("den", [P, T], F32, 2), ("oev", [P, CH], F32, 2),
                                     ("mx", [P, KT, 2], F32, 2), ("nm_parts", [KT, 3, P], BF16, 2)):
            bufs[name] = [sb(att, f"{name}{i}", shape, dt) for i in range(cnt)]
        for name, shape in (("mf", [P, KT]), ("nm", [KT, P]), ("nm_rem", [KT, P])):
            bufs[name] = sb(att, name, shape)
        for sl in range(3):
            Q.op("vector", lambda e, sl=sl: e.memset(bufs["kst"][sl][STACK:ROWS, :], 1.0), mid_end)
        for i in range(2):
            m_o = Q.op("vector", lambda e, i=i: e.memset(bufs["mx"][i][:, :, :], NEG))
        bufs["ones_mark"] = m_o
        for g in parts_stored:
            parts_stored[g] = parts_stored[g] + mid_end
        assembled, asm_free, o_stored = {}, {}, {}

        def fin_stages(g):
            num, den = bufs["num"][g % 2], bufs["den"][g % 2]
            asm_free[g] = []
            stages = []
            for cc in range(CPB):
                at = slice(cc * CH, (cc + 1) * CH)
                for j in range(TPC):
                    def rec(cc=cc, j=j):
                        p = slice(cc * CH + j * P, cc * CH + (j + 1) * P)
                        Q.op("vector", lambda e: e.reciprocal(den[:, p], den[:, p]), assembled[g], mark=j == TPC - 1)
                    stages.append(rec)

                def mul(cc=cc, at=at):
                    m = Q.op("vector", lambda e: e.tensor_tensor(num[:, at], num[:, at], den[:, at], ALU.mult),
                             [(Q.done["vector"], Q.done["vector"].n)])
                    o_stored[g, cc] = Q.dma("o_out", o_ffn[g, :, at], num[:, at], [m])
                    asm_free[g].append(o_stored[g, cc])
                stages.append(mul)
            return stages

        fillers = {}
        for g in range(NG):
            for i, f in enumerate(fin_stages(g)):
                fillers.setdefault(HG * KT * (g + 1) + 2 + i, []).append(f)
        attention(bufs, [(g, hh) for g in range(NG) for hh in range(HG)], fillers, assembled, mid_end)
        att2_end = [(s, s.n) for s in Q.done.values()] + [x for v in asm_free.values() for x in v]
        att.close()

        Q.phase("gate")
        v_stack.close()
        acc = sb(ctx, "acc", [P, NC, TPC, D])
        xfT = sb(ctx, "xfT", [P, HALVES, N])
        gates = sb(ctx, "gates", [P, NC * TPC, E_])
        b2_sb = sb(ctx, "b2_sb", [E_, D])
        b1_sb = sb(ctx, "b1_sb", [P, E_, FT])
        x1_free = None
        with ExitStack() as st4:
            wo2 = sb(st4, "wo2", [P, HALVES, D])
            wg = sb(st4, "wg", [P, HALVES, E_])
            idx8 = sb(st4, "idx8", [P, NC * TPC, E_])
            oin_g = [[sb(st4, f"of{r}{h}", [P, CH]) for h in range(HALVES)] for r in range(2)]
            xr_g = [sb(st4, f"x1r{i}", [P, TPC, D]) for i in range(2)]
            rs_ = [sb(st4, f"res{i}", [P, TPC, D]) for i in range(2)]
            xno_g = [sb(st4, f"xfn{i}", [P, TPC, D]) for i in range(2)]
            stt_g = [sb(st4, f"st4_{i}", [P, TPC, 9]) for i in range(2)]
            w4_in = Signal(sem("w4_in"))
            Q.dma_on(w4_in, wo2[:, :, :], a["w_o"].rearrange("(h p) o -> p h o", p=P), att2_end)
            Q.dma_on(w4_in, wg[:, :, :], a["w_gate"].rearrange("(h p) o -> p h o", p=P))
            Q.dma_on(w4_in, idx8[:, :, :], a["idx8"].rearrange("p (t e) -> p t e", e=E_))
            Q.dma_on(w4_in, b2_sb[:, :], a["b2"])
            m_w4 = Q.dma_on(w4_in, b1_sb[:, :, :], a["b1"].rearrange("p (e f) -> p e f", e=E_))
            ld, xn_m, tr_m, mm_o, res_m, acc_m = {}, {}, {}, {}, {}, {}

            def g_load(c):
                b, cc, r = c // CPB, c % CPB, c % 2
                at = slice(cc * CH, (cc + 1) * CH)
                ms = [Q.dma("mid_in", oin_g[r][h][:, :], o_ffn[b * HALVES + h, :, at],
                            [mm_o.get(c - 2), m_w4]) for h in range(HALVES)]
                ms.append(Q.dma("mid_in", xr_g[r][:, :, :], x1_d[c * CH:(c + 1) * CH, :].rearrange("(j p) d -> p j d", p=P),
                                [acc_m.get(c - 2), m_w4]))
                ld[c] = ms

            def g_a(c):
                r = c % 2
                for j in range(TPC):
                    bk = j // 2
                    for h in range(HALVES):
                        m = Q.op("tensor", lambda e, j=j, h=h, bk=bk: e.matmul(
                            banks[bk][:, (j % 2) * D:(j % 2 + 1) * D], oin_g[r][h][:, j * P:(j + 1) * P], wo2[:, h, :],
                            start=h == 0, stop=h == 1), ld[c] + [m_w4, bank_free[bk]], mark=h == 1)
                    if j % 2 == 1:
                        m1 = Q.op("vector", lambda e, bk=bk, j=j: e.tensor_tensor(
                            rs_[r][:, j - 1:j + 1, :], banks[bk][:, :].rearrange("p (j d) -> p j d", j=2),
                            xr_g[r][:, j - 1:j + 1, :], ALU.add), [m, xn_m.get(c - 2), acc_m.get(c - 2)] + ld[c])
                        bank_free[bk] = m1
                mm_o[c] = m
                acc_m[c] = Q.op("gpsimd", lambda e: e.tensor_tensor(acc[:, c, :, :], rs_[r][:, :, :], xr_g[r][:, :, :],
                                                                   ALU.add), [m1])
                xn_m[c] = norm4(stt_g[r], rs_[r], xno_g[r], [m1], [tr_m.get(c - 2)])

            lg_m = None

            def g_b(c):
                r = c % 2
                tr_m[c] = transpose4(xno_g[r], [xfT[:, h, c * CH:(c + 1) * CH] for h in range(HALVES)], 2,
                                     [col("g2_0"), col("g2_1")], [col("c2_0"), col("c2_1")], [xn_m[c]], [])
                bk = 4 + c % 2
                for j in range(TPC):
                    for h in range(HALVES):
                        m = Q.op("tensor", lambda e, j=j, h=h, bk=bk: e.matmul(
                            banks[bk][:, j * E_:(j + 1) * E_], xfT[:, h, c * CH + j * P:c * CH + (j + 1) * P], wg[:, h, :],
                            start=h == 0, stop=h == 1), [tr_m[c], bank_free[bk]], mark=h == 1)
                bank_free[bk] = Q.op("vector", lambda e: e.tensor_copy(
                    gates[:, c * TPC:(c + 1) * TPC, :], banks[bk][:, 0:TPC * E_].rearrange("p (t e) -> p t e", e=E_)), [m])
                return bank_free[bk]

            g_load(0)
            g_load(1)
            g_a(0)
            for c in range(NC):
                if c + 1 < NC:
                    g_a(c + 1)
                if c + 2 < NC:
                    g_load(c + 2)
                lg_m = g_b(c)

            NT = NC * TPC
            one = sb(st4, "g_one", [P, NT])
            t1, t2, hot1, hot2 = (sb(st4, f"g_{n}", [P, NT, E_]) for n in ("t1", "t2", "hot1", "hot2"))
            w1_, w2_ = sb(st4, "g_w1", [P, NT]), sb(st4, "g_w2", [P, NT])

            def bc(x):
                return x[:, :].unsqueeze(2).to_broadcast([P, NT, E_])

            def dve(f, waits=()):
                return Q.op("vector", f, [(Q.done["vector"], Q.done["vector"].n)] + list(waits))

            dve(lambda e: e.tensor_reduce(one[:, :], gates[:, :, :], AX_X, ALU.max))
            m = dve(lambda e: e.tensor_tensor(gates[:, :, :], gates[:, :, :], bc(one), ALU.subtract))
            m = Q.op("scalar", lambda e: e.activation(gates[:, :, :], gates[:, :, :], ACT.Exp), [m])
            dve(lambda e: e.tensor_reduce(one[:, :], gates[:, :, :], AX_X, ALU.add), [m])
            dve(lambda e: e.reciprocal(one[:, :], one[:, :]))
            dve(lambda e: e.tensor_tensor(gates[:, :, :], gates[:, :, :], bc(one), ALU.mult))

            def pick(src, w, hot):
                dve(lambda e: e.tensor_reduce(w[:, :], src[:, :, :], AX_X, ALU.max))
                dve(lambda e: e.tensor_tensor(hot[:, :, :], src[:, :, :], bc(w), ALU.is_equal))
                dve(lambda e: e.tensor_tensor(hot[:, :, :], hot[:, :, :], idx8[:, :, :], ALU.mult))
                dve(lambda e: e.tensor_reduce(one[:, :], hot[:, :, :], AX_X, ALU.max))
                dve(lambda e: e.tensor_tensor(hot[:, :, :], idx8[:, :, :], bc(one), ALU.is_equal))
            pick(gates, w1_, hot1)
            dve(lambda e: e.scalar_tensor_tensor(t1[:, :, :], hot1[:, :, :], -2.0, gates[:, :, :], ALU.mult, ALU.add))
            pick(t1, w2_, hot2)
            dve(lambda e: e.tensor_tensor(one[:, :], w1_[:, :], w2_[:, :], ALU.add))
            dve(lambda e: e.reciprocal(one[:, :], one[:, :]))
            dve(lambda e: e.tensor_tensor(w1_[:, :], w1_[:, :], one[:, :], ALU.mult))
            dve(lambda e: e.tensor_tensor(w2_[:, :], w2_[:, :], one[:, :], ALU.mult))
            dve(lambda e: e.tensor_tensor(t1[:, :, :], hot1[:, :, :], bc(w1_), ALU.mult))
            dve(lambda e: e.tensor_tensor(t2[:, :, :], hot2[:, :, :], bc(w2_), ALU.mult))
            m_gates = dve(lambda e: e.tensor_tensor(gates[:, :, :], t1[:, :, :], t2[:, :, :], ALU.add))
            gate_end = [(s, s.n) for s in Q.done.values()]

        Q.phase("moe")
        w1s = [sb(ctx, f"w1s{i}", [P, HALVES, F_]) for i in range(2)]
        w2s = [sb(ctx, f"w2s{i}", [P, FT, D]) for i in range(2)]
        he = [sb(ctx, f"he{i}", [P, FT, CH]) for i in range(2)]
        gT = [sb(ctx, f"gT{i}", [E_, P]) for i in range(2)]
        fst = [sb(ctx, f"fst{i}", [P, TPC, 9]) for i in range(2)]
        fin = [sb(ctx, f"fin{i}", [P, TPC, D]) for i in range(2)]
        w_sig = [Signal(sem(f"expert_in{i}")) for i in range(2)]
        last_y, last_h = {}, {}
        w_mark = {}

        def load_expert(e_):
            i = e_ % 2
            w = [last_y.get(e_ - 2), last_h.get(e_ - 2)] + gate_end
            Q.dma_on(w_sig[i], w1s[i][:, :, :], a["w1"][e_].rearrange("(h p) f -> p h f", p=P), w)
            w_mark[e_] = Q.dma_on(w_sig[i], w2s[i][:, :, :], a["w2"][e_].rearrange("(f p) d -> p f d", p=P), w)

        h_at, y_at = [0], [0]
        he_m, y_m = {}, {}
        acc_last = {}
        load_expert(0)
        load_expert(1)
        for i in range(NC * TPC):
            c, j, r = i // TPC, i % TPC, i % 2
            bk = 4 + i % 2
            m = Q.op("tensor", lambda e, i=i, bk=bk: e.transpose(banks[bk][0:E_, 0:P], gates[:, i, :], ident),
                     [m_gates, bank_free[bk]] + gate_end)
            m = Q.op("vector", lambda e, r=r, bk=bk: e.tensor_copy(gT[r][:, :], banks[bk][0:E_, 0:P]),
                     [m, acc_last.get(("g", i - 2))])
            bank_free[bk] = m
            bk2 = 6 + i % 2
            m = Q.op("tensor", lambda e, r=r, bk2=bk2: e.matmul(banks[bk2][:, 0:D], gT[r][:, :], b2_sb[:, :], start=True,
                                                               stop=True), [m, bank_free[bk2]])
            acc_last["g", i] = m
            acc_last[i] = bank_free[bk2] = Q.op("vector", lambda e, c=c, j=j, bk2=bk2: e.tensor_tensor(
                acc[:, c, j, :], acc[:, c, j, :], banks[bk2][:, 0:D], ALU.add), [m])

        def hidden(e_, c):
            s = e_ * NC + c
            for f in range(FT):
                bk = h_at[0] % 4
                h_at[0] += 1
                for h in range(HALVES):
                    m = Q.op("tensor", lambda e, f=f, h=h, bk=bk: e.matmul(
                        banks[bk][:, :], w1s[e_ % 2][:, h, f * P:(f + 1) * P], xfT[:, h, c * CH:(c + 1) * CH],
                        start=h == 0, stop=h == 1), [w_mark[e_], bank_free[bk]], mark=h == 1)
                bank_free[bk] = Q.op("scalar", lambda e, f=f, bk=bk: e.activation(
                    he[s % 2][:, f, :], banks[bk][:, :], ACT.Gelu_apprx_tanh, bias=b1_sb[:, e_, f:f + 1]),
                    [m, y_m.get(s - 2)])
                he_m[s, f] = bank_free[bk]
            last_h[e_] = m

        def down(e_, c):
            s = e_ * NC + c
            for j in range(TPC):
                bk = 4 + y_at[0] % 4
                y_at[0] += 1
                for f in range(FT):
                    m = Q.op("tensor", lambda e, f=f, j=j, bk=bk: e.matmul(
                        banks[bk][:, 0:D], he[s % 2][:, f, j * P:(j + 1) * P], w2s[e_ % 2][:, f, :],
                        start=f == 0, stop=f == FT - 1), [he_m[s, f], bank_free[bk]], mark=f == FT - 1)
                t = c * TPC + j
                acc_last[t] = bank_free[bk] = Q.op("vector", lambda e, t=t, j=j, bk=bk: e.scalar_tensor_tensor(
                    acc[:, c, j, :], banks[bk][:, 0:D], gates[:, t, e_:e_ + 1], acc[:, c, j, :], ALU.mult, ALU.add),
                    [m, acc_last[t]])
            y_m[s] = last_y[e_] = m

        fin_st = {}

        def finish(c):
            r = c % 2
            m = norm4(fst[r], acc[:, c, :, :], fin[r], [acc_last[c * TPC + j] for j in range(TPC)], [fin_st.get(c - 2)])
            fin_st[c] = Q.dma("final_out", out[c * CH:(c + 1) * CH, :].rearrange("(j p) d -> p j d", p=P),
                              fin[r][:, :, :], [m])

        seq = [(e_, c) for e_ in range(E_) for c in range(NC)]
        hidden(*seq[0])
        for i, (e_, c) in enumerate(seq):
            if i + 1 < len(seq):
                hidden(*seq[i + 1])
            down(e_, c)
            if c == NC - 1 and e_ + 2 < E_:
                load_expert(e_ + 2)
        for c in range(NC):
            finish(c)
        all_dma = [s for sigs, _ in Q.rings.values() for s in sigs if s.n]
        final_waits = [(s.sem, s.n) for s in all_dma]

        block = ctx.enter_context(nc.Block())

        @block.sync
        def _(eng):
            Q.play("sync", eng)
            for s, v in final_waits:
                eng.wait_ge(s, v)

        @block.tensor
        def _(eng):
            Q.play("tensor", eng)

        @block.vector
        def _(eng):
            Q.play("vector", eng)

        @block.scalar
        def _(eng):
            Q.play("scalar", eng)

        @block.gpsimd
        def _(eng):
            Q.play("gpsimd", eng)


def shape_constants():
    p = np.arange(P)
    same = (p[:, None] // HD == p[None, :] // HD).astype(np.float32)
    eye = np.eye(P, dtype=np.float32)
    later = np.float32(NEG)
    mask_s = np.where(p[None, :] > p[:, None], later, np.float32(0))
    consts = np.concatenate([eye, same / HD, eye - same / HD, mask_s, mask_s.T, np.ones((P, P), np.float32), same], 1)
    idx8 = np.broadcast_to(np.arange(E_, 0, -1, dtype=np.float32), (P, N // P, E_)).reshape(P, -1)
    return np.ascontiguousarray(consts.astype(np.float32)), np.ascontiguousarray(idx8)


def kernel(**inputs):
    import concourse.bacc as _bacc
    from concourse.bass_utils import run_bass_kernel_spmd as _run

    A = {k[len("L0_attn_"):]: np.asarray(v) for k, v in inputs.items() if k.startswith("L0_attn_")}
    G = {k[len("L0_ffn_"):]: np.asarray(v) for k, v in inputs.items() if k.startswith("L0_ffn_")}

    def halves(v):
        return [v[i * P:(i + 1) * P] for i in range(HALVES)]

    def per_head(v):
        return np.tile(v, HG)

    def everywhere(v):
        return np.broadcast_to(v, (P,))

    cols = np.stack(halves(A["bq"]) + halves(A["bv"]) + halves(A["lna_w"]) + halves(G["ln1_g"]) + halves(G["ln1_b"])
                    + halves(G["ln2_g"]) + halves(G["ln2_b"])
                    + [per_head(A["lnc_w"]), per_head(A["lnd_w"]), per_head(A["blq"]), per_head(A["blk"]), per_head(A["blv"]),
                       everywhere(A["temp"]), everywhere(A["threshold"]), everywhere(A["factor"])], axis=1)
    consts, idx8 = shape_constants()
    arrays = {
        "x": A["x"].reshape(N, D), "consts": consts, "idx8": idx8, "cols": cols,
        "WqT": A["Wq"].T, "WkT": A["Wk"].T, "WvT": A["Wv"].T, "WoT": A["Wo"].T,
        "WlqT": A["Wlq"].T, "WlkT": A["Wlk"].T, "WlvT": A["Wlv"].T,
        "bo4": np.tile(A["bo"], (P, TPC)),
        "w_qkv": G["w_qkv"], "w_o": G["w_o"], "w_gate": G["w_gate"], "w1": G["w1"], "w2": G["w2"], "b2": G["b2"],
        "b1": G["b1"].reshape(E_, FT, P).transpose(2, 0, 1).reshape(P, E_ * FT),
    }
    arrays = {f"in_{k}": np.ascontiguousarray(v) for k, v in arrays.items()}
    nc = _bacc.Bacc("TRN2", target_bir_lowering=False, num_devices=1)
    aps = {k[3:]: nc.dram_tensor(k, v.shape, mybir.dt.from_np(v.dtype), kind="ExternalInput").ap()
           for k, v in arrays.items()}
    res = nc.dram_tensor("out_0", (N, D), F32, kind="ExternalOutput").ap()
    build_program(nc, aps, res)
    r = _run(nc, [arrays], core_ids=[0])
    return r.results[0]["out_0"].reshape(B, T, D)
```

```python
from contextlib import ExitStack, contextmanager

import numpy as np

import concourse.bass as bass
from concourse import mybir

F32 = mybir.dt.float32
BF16 = mybir.dt.bfloat16
I32 = mybir.dt.int32
U32 = mybir.dt.uint32
ACT = mybir.ActivationFunctionType
ALU = mybir.AluOpType
AX_X = mybir.AxisListType.X

P = 128
B, T, D, H = 2, 2048, 256, 16
HD = D // H
HALVES = D // P
HG = P // HD
NG = B * HALVES
N = B * T
CH = 512
CPB = T // CH
NC = N // CH
TPC = CH // P
KT = T // P
ITERS = 3
TA = H
XB = HALVES * B
E_, F_ = 8, 1024
FT = F_ // P
BLK = 256
BT = BLK // P
EPS = 1e-5
NEG = -3.0e38
SM = 1.0 / float(np.sqrt(HD))
QKS = HD ** -0.25
STACK = 6 * HD
ROWS = STACK + 3
Q_PARTS = (0, 0, 0, 1, 1, 2)
K_PARTS = (0, 1, 2, 0, 1, 0)
VW = 2 * HD

COLS = ["bq0", "bq1", "bv0", "bv1", "lna0", "lna1", "g1_0", "g1_1", "c1_0", "c1_1",
        "g2_0", "g2_1", "c2_0", "c2_1", "lnc", "lnd", "blq", "blk", "blv", "temp", "thr", "fac"]
COL = {n: i for i, n in enumerate(COLS)}


class Signal:

    def __init__(self, sem):
        self.sem, self.n = sem, 0


class Queues:

    ENGINES = ("tensor", "vector", "scalar", "gpsimd", "sync")

    def __init__(self, new_sem):
        self.q = {e: [] for e in self.ENGINES}
        self.seen = {e: {} for e in self.ENGINES}
        self.new_sem = new_sem
        self.done = {}
        self.rings = {}

    def phase(self, name, engines=ENGINES[:4]):
        self.done = {e: Signal(self.new_sem(f"{e}_done_{name}")) for e in engines}

    def _waits(self, eng, waits):
        need = []
        for w in waits:
            if w is None:
                continue
            sig, v = w
            if self.seen[eng].get(sig, 0) < v:
                self.seen[eng][sig] = v
                need.append((sig.sem, v))
        return need

    def op(self, eng, build, waits=(), mark=True, signal=None):
        need = self._waits(eng, waits)
        sig = signal or self.done[eng] if mark else None
        if mark:
            sig.n += 1
        self.q[eng].append((need, build, sig.sem if mark else None, 1))
        return (sig, sig.n) if mark else None

    def dma_on(self, signal, dst, src, waits=()):
        need = self._waits("sync", waits)
        signal.n += 16
        self.q["sync"].append((need, lambda e, d=dst, s=src: e.dma_start(d, s), signal.sem, 16))
        return (signal, signal.n)

    def dma(self, ring, dst, src, waits=(), depth=6):
        if ring not in self.rings:
            self.rings[ring] = ([Signal(self.new_sem(f"{ring}_{i}")) for i in range(depth)], [0])
        sigs, at = self.rings[ring]
        s = sigs[at[0] % len(sigs)]
        at[0] += 1
        return self.dma_on(s, dst, src, list(waits) + [(s, s.n)] * (s.n > 0))

    def gather(self, signal, out, table, index, waits=()):
        need = self._waits("gpsimd", waits)
        signal.n += 16
        self.q["gpsimd"].append((need, lambda e, o=out, t=table, i=index: e.indirect_dma_start(
            out=o, out_offset=None, in_=t, in_offset=bass.IndirectOffsetOnAxis(ap=i, axis=0)), signal.sem, 16))
        return (signal, signal.n)

    def scatter(self, signal, table, index, src, waits=()):
        need = self._waits("gpsimd", waits)
        signal.n += 16
        self.q["gpsimd"].append((need, lambda e, s=src, t=table, i=index: e.indirect_dma_start(
            out=t, out_offset=bass.IndirectOffsetOnAxis(ap=i, axis=0), in_=s, in_offset=None), signal.sem, 16))
        return (signal, signal.n)

    def wait(self, eng, mark):
        self.q[eng].append(([(mark[0].sem, mark[1])], lambda e: None, None, 0))

    def settle(self, eng, signal):
        signal.n += 1
        self.q[eng].append(([], lambda e: e.drain(), signal.sem, 1))
        return (signal, signal.n)

    @contextmanager
    def more_than(self, expert, tokens):
        outer, seen = self.q, self.seen
        self.q = {e: [] for e in self.ENGINES}
        self.seen = {e: dict(v) for e, v in seen.items()}
        yield
        inner, self.q, self.seen = self.q, outer, seen
        for e in self.ENGINES:
            if inner[e]:
                self.q[e].append(("more_than", expert, tokens, inner[e]))

    def play(self, name, eng, counts=None):
        self._play(self.q[name], eng, counts, {})

    def _play(self, items, eng, counts, loaded):
        for item in items:
            if item[0] == "count":
                loaded[item[1]] = eng.value_load(counts[0:1, item[1]:item[1] + 1], min_val=0, max_val=N)
                continue
            if item[0] == "more_than":
                with eng.If(loaded[item[1]] > item[2]):
                    self._play(item[3], eng, counts, loaded)
                continue
            need, build, sem, by = item
            for s, v in need:
                eng.wait_ge(s, v)
            ins = build(eng)
            if sem is not None:
                ins.then_inc(sem, by)


def build_program(nc, a, out):
    ctx = ExitStack()
    with ctx:
        def sem(name):
            return ctx.enter_context(nc.semaphore(name))

        Q = Queues(sem)

        def sb(stack, name, shape, dt=F32):
            return stack.enter_context(nc.sbuf_tensor(name, shape, dt))

        def dram(name, shape, dt=F32):
            return nc.dram_tensor(name, shape, dt, kind="Internal").ap()

        psum = ctx.enter_context(nc.psum_tensor("psum", [P, 8 * CH], F32))
        banks = [psum[:, i * CH:(i + 1) * CH] for i in range(8)]
        bank_free = [None] * 8

        o_ffn = dram("o_ffn", [NG, P, T])
        parts = [{k: dram(f"parts_{k}{i}", [3, P, T], BF16) for k in "qk"} for i in range(NG)]
        x1_d = dram("x1_d", [N, D])

        cst = sb(ctx, "cst", [P, 7 * P])
        ident, bmean, center, mask_s, mask_t, ones, same = (cst[:, i * P:(i + 1) * P] for i in range(7))
        cols = sb(ctx, "cols", [P, len(COLS)])
        ident_bf = sb(ctx, "ident_bf", [P, P], BF16)
        mask_s_bf = sb(ctx, "mask_s_bf", [P, P], BF16)
        mask_t_bf = sb(ctx, "mask_t_bf", [P, P], BF16)
        eps_col = sb(ctx, "eps_col", [P, 1])
        wlin = {k: sb(ctx, f"wl_{k}", [P, P]) for k in "qkv"}
        wnq = sb(ctx, "wnq", [P, ITERS])
        ts_tmp = sb(ctx, "ts_tmp", [P, 4])
        diff_cols = sb(ctx, "diff_cols", [P, 1])
        flag = sb(ctx, "flag", [P, 4])
        v_stack = ExitStack()
        v_tok = sb(v_stack, "v_tok", [P, NG, KT, HG, VW])

        def col(name):
            return cols[:, COL[name]:COL[name] + 1]

        Q.phase("early")
        setup_in = Signal(sem("setup_in"))
        Q.dma_on(setup_in, cst[:, :], a["consts"])
        m_small = Q.dma_on(setup_in, cols[:, :], a["cols"])
        m_blocks = []
        m_zero = None
        for k in "qkv":
            m_zero = Q.op("vector", lambda e, k=k: e.memset(wlin[k][:, :], 0.0))
        blocks_in = Signal(sem("blocks_in"))
        for k in "qkv":
            for g in range(HG):
                s = slice(g * HD, (g + 1) * HD)
                m_blocks = Q.dma_on(blocks_in, wlin[k][s, s], a[f"Wl{k}T"], [m_zero])
        m_c = None
        for d, s in ((ident_bf, ident), (mask_s_bf, mask_s), (mask_t_bf, mask_t)):
            m_c = Q.op("vector", lambda e, d=d, s=s: e.tensor_copy(d[:, :], s), [m_small])
        m_eps = Q.op("vector", lambda e: e.memset(eps_col[:, :], EPS))
        m_ones_v = Q.op("gpsimd", lambda e: e.memset(v_tok[:, :, :, :, HD:VW], 1.0))
        Q.op("scalar", lambda e: nc.scalar.preload_act_table_set("natural_log_exp_and_others"), mark=False)
        prev = None
        for it in range(ITERS):
            t_, r_, c_, d_ = (ts_tmp[:, i:i + 1] for i in range(4))
            m = Q.op("vector", lambda e, it=it, t_=t_: e.tensor_scalar(t_, col("temp"), 0.005 * it, None, ALU.add),
                     [m_small, prev])
            m2 = Q.op("vector", lambda e, r_=r_, t_=t_: e.tensor_scalar(r_, t_, 1e-18, None, ALU.max), [m])
            m3 = Q.op("vector", lambda e, c_=c_, t_=t_: e.tensor_scalar(c_, t_, 1.0, None, ALU.not_equal), [m])
            m4 = Q.op("vector", lambda e, d_=d_, t_=t_: e.tensor_scalar(d_, t_, 0.0, None, ALU.is_gt), [m])
            m5 = Q.op("vector", lambda e, c_=c_, d_=d_: e.tensor_tensor(c_, c_, d_, ALU.mult), [m3, m4])
            a1 = Q.op("scalar", lambda e, r_=r_: e.activation(r_, r_, ACT.Ln), [m2])
            a2 = Q.op("scalar", lambda e, r_=r_: e.activation(r_, r_, ACT.Exp, scale=-0.5), [a1])
            m6 = Q.op("vector", lambda e, r_=r_, c_=c_: e.scalar_tensor_tensor(r_, r_, -1.0, c_, ALU.add, ALU.mult),
                      [a2, m5])
            m7 = Q.op("vector", lambda e, r_=r_: e.tensor_scalar(r_, r_, 1.0, SM, ALU.add, ALU.mult), [m6])
            prev = Q.op("vector", lambda e, r_=r_, it=it: e.tensor_tensor(wnq[:, it:it + 1], r_, col("lnc"), ALU.mult),
                        [m7])
        m_wnq = prev

        def norm4(st, src, dst, waits, free=()):
            m = None
            for j in range(TPC):
                m = Q.op("vector", lambda e, j=j: e.bn_stats(st[:, j, 0:6], src[:, j, :]), list(waits) + list(free),
                         mark=j == TPC - 1)
            mv = None
            for j in range(TPC):
                mv = Q.op("vector", lambda e, j=j: e.bn_aggr(st[:, j, 6:8], st[:, j, 0:6]), [m], mark=j == TPC - 1)
            s1 = Q.op("scalar", lambda e: e.activation(st[:, :, 8], st[:, :, 7], ACT.Ln, bias=eps_col[:, :]), [mv, m_eps])
            s2 = Q.op("scalar", lambda e: e.activation(st[:, :, 8], st[:, :, 8], ACT.Exp, scale=-0.5), [s1])
            for j in range(TPC):
                m = Q.op("vector", lambda e, j=j: e.tensor_scalar(dst[:, j, :], src[:, j, :], st[:, j, 6:7],
                                                                 st[:, j, 8:9], ALU.subtract, ALU.mult), [s2, mv],
                         mark=j == TPC - 1)
            return m

        def transpose4(src, dst, b0, scales, biases, waits, free):
            marks = []
            for h in range(HALVES):
                bk = b0 + h
                for j in range(TPC):
                    m = Q.op("tensor", lambda e, h=h, j=j, bk=bk: e.transpose(
                        banks[bk][:, j * P:(j + 1) * P], src[:, j, h * P:(h + 1) * P], ident),
                        list(waits) + [bank_free[bk], m_small], mark=j == TPC - 1)
                kw = {} if biases is None else {"bias": biases[h]}
                bank_free[bk] = Q.op("scalar", lambda e, h=h, bk=bk, kw=kw: e.activation(
                    dst[h], banks[bk][:, :], ACT.Identity, scale=scales[h], **kw), [m, m_small] + list(free))
                marks.append(bank_free[bk])
            return marks[-1]

        parts_stored, v_ready = {}, {}
        ORDER = [c for c in range(NC) if c % CPB] + [c for c in range(NC) if c % CPB == 0]
        with ExitStack() as st1:
            w_in = {k: sb(st1, f"w{k}_sb", [P, HALVES, D]) for k in "qkvo"}
            wqkv = sb(st1, "wqkv", [P, HALVES, 3 * D])
            bo4 = sb(st1, "bo4", [P, TPC, D])
            y_first = sb(st1, "y_first", [TA, B, D])
            weights_in = Signal(sem("weights_in"))
            xs = sb(st1, "xs", [B * TA, D])
            for b in range(B):
                Q.dma_on(weights_in, xs[b * TA:(b + 1) * TA, :], a["x"][b * T:b * T + TA, :])
            Q.dma_on(weights_in, bo4[:, :, :], a["bo4"].rearrange("p (j d) -> p j d", j=TPC))
            for k in "qkvo":
                Q.dma_on(weights_in, w_in[k][:, :, :], a[f"W{k}T"].rearrange("(h p) o -> p h o", p=P))
            m_w = Q.dma_on(weights_in, wqkv[:, :, :], a["w_qkv"].rearrange("(h p) o -> p h o", p=P))

            W = XB * TA
            B_LIN, B_CEN = 6, 7
            f_stat = sb(st1, "f_stat", [B * TA, 9])
            f_xn = sb(st1, "f_xn", [B * TA, D])
            f_xT = sb(st1, "f_xT", [P, HALVES, B * TA])
            f_cur = {k: sb(st1, f"f_cur_{k}", [P, W]) for k in "qkv"}
            f_lin = sb(st1, "f_lin", [P, 3 * W])
            f_cen = sb(st1, "f_cen", [P, 2 * W])
            f_sq = sb(st1, "f_sq", [P, 2 * W])
            f_rs = sb(st1, "f_rs", [P, 2 * W])
            f_nrm = sb(st1, "f_nrm", [P, 2 * W])
            f_kbd = sb(st1, "f_kbd", [P, XB, P])
            f_vbd = sb(st1, "f_vbd", [P, XB, P])
            f_vT = sb(st1, "f_vT", [P, XB, P])
            f_p = sb(st1, "f_p", [TA, XB * HG, TA])
            f_pT = sb(st1, "f_pT", [P, W])
            f_red = sb(st1, "f_red", [TA, XB * HG])
            f_out = [sb(st1, f"f_out{i}", [P, W]) for i in range(ITERS)]
            f_o = sb(st1, "f_o", [P, W])
            first_y = []

            def first_attention():
                last = [None]

                def step(eng, f, more=(), mark=True):
                    last[0] = Q.op(eng, f, [last[0]] + list(more))

                bank = [B_LIN]

                def flip():
                    bank[0] = B_LIN + B_CEN - bank[0]
                    return banks[bank[0]]

                step("vector", lambda e: e.bn_stats(f_stat[:, 0:6], xs[:, :]), [m_w, m_wnq])
                yield
                step("vector", lambda e: e.bn_aggr(f_stat[:, 6:8], f_stat[:, 0:6]))
                yield
                step("scalar", lambda e: e.activation(f_stat[:, 8:9], f_stat[:, 7:8], ACT.Ln, bias=eps_col[0:B * TA, :]), [m_eps])
                step("scalar", lambda e: e.activation(f_stat[:, 8:9], f_stat[:, 8:9], ACT.Exp, scale=-0.5))
                yield
                step("vector", lambda e: e.tensor_scalar(f_xn[:, :], xs[:, :], f_stat[:, 6:7], f_stat[:, 8:9],
                                                         ALU.subtract, ALU.mult))
                yield
                bk = flip()
                for h in range(HALVES):
                    step("tensor", lambda e, h=h, bk=bk: e.transpose(bk[:, h * B * TA:(h + 1) * B * TA],
                                                                    f_xn[:, h * P:(h + 1) * P], ident[0:B * TA, 0:B * TA]),
                         [m_w, m_small])
                for h in range(HALVES):
                    step("vector", lambda e, h=h, bk=bk: e.tensor_scalar(
                        f_xT[:, h, :], bk[:, h * B * TA:(h + 1) * B * TA], col(f"lna{h}"), None, ALU.mult))
                yield
                bk = flip()
                for i, k in enumerate("qkv"):
                    for o in range(HALVES):
                        at = slice(i * W + o * B * TA, i * W + (o + 1) * B * TA)
                        for h in range(HALVES):
                            m = Q.op("tensor", lambda e, k=k, o=o, h=h, at=at, bk=bk: e.matmul(
                                bk[:, at], w_in[k][:, h, o * P:(o + 1) * P], f_xT[:, h, :], start=h == 0, stop=h == 1),
                                [last[0]], mark=h == 1)
                last[0] = m
                for i, k in enumerate("qkv"):
                    for o in range(HALVES):
                        at = slice(i * W + o * B * TA, i * W + (o + 1) * B * TA)
                        dst = f_cur[k][:, o * B * TA:(o + 1) * B * TA]
                        if k == "q":
                            f = lambda e, at=at, dst=dst, o=o, bk=bk: e.tensor_scalar(dst, bk[:, at], col(f"bq{o}"), QKS,
                                                                                     ALU.add, ALU.mult)
                        elif k == "k":
                            f = lambda e, at=at, dst=dst, bk=bk: e.tensor_scalar(dst, bk[:, at], QKS, None, ALU.mult)
                        else:
                            f = lambda e, at=at, dst=dst, o=o, bk=bk: e.tensor_scalar(dst, bk[:, at], col(f"bv{o}"), None,
                                                                                     ALU.add)
                        step("vector", f)
                yield
                for it in range(ITERS):
                    src = dict(f_cur) if it == 0 else {"q": f_cur["q"], "k": f_lin[:, W:2 * W], "v": f_lin[:, 2 * W:3 * W]}
                    bk = flip()
                    for i, k in enumerate("qkv"):
                        step("tensor", lambda e, i=i, s=src[k], k=k, bk=bk: e.matmul(
                            bk[:, i * W:(i + 1) * W], wlin[k][:, :], s[:, :], start=True, stop=True), [m_blocks])
                    for i, k in enumerate("qkv"):
                        step("vector", lambda e, i=i, k=k, bk=bk: e.tensor_scalar(
                            f_lin[:, i * W:(i + 1) * W], bk[:, i * W:(i + 1) * W], col("bl" + k), None, ALU.add))
                    yield
                    bk = flip()
                    step("tensor", lambda e, bk=bk: e.matmul(bk[:, 0:2 * W], center, f_lin[:, 0:2 * W], start=True, stop=True))
                    step("vector", lambda e, bk=bk: e.tensor_copy(f_cen[:, :], bk[:, 0:2 * W]))
                    step("vector", lambda e: e.tensor_tensor(f_sq[:, :], f_cen[:, :], f_cen[:, :], ALU.mult))
                    yield
                    bk = flip()
                    step("tensor", lambda e, bk=bk: e.matmul(bk[:, 0:2 * W], bmean, f_sq[:, :], start=True, stop=True))
                    step("scalar", lambda e, bk=bk: e.activation(f_rs[:, :], bk[:, 0:2 * W], ACT.Ln, bias=eps_col[:, :]))
                    step("scalar", lambda e: e.activation(f_rs[:, :], f_rs[:, :], ACT.Exp, scale=-0.5))
                    yield
                    for i, w in ((0, wnq[:, it:it + 1]), (1, col("lnd"))):
                        step("vector", lambda e, i=i, w=w: e.scalar_tensor_tensor(
                            f_nrm[:, i * W:(i + 1) * W], f_cen[:, i * W:(i + 1) * W], w, f_rs[:, i * W:(i + 1) * W],
                            ALU.mult, ALU.mult))
                    for dst, s0 in ((f_kbd, f_nrm[:, W:2 * W]), (f_vbd, f_lin[:, 2 * W:3 * W])):
                        for x in range(XB):
                            step("vector", lambda e, dst=dst, s0=s0, x=x: e.tensor_tensor(
                                dst[:, x, :].rearrange("p (h t) -> p h t", h=HG),
                                s0[:, x * TA:(x + 1) * TA].unsqueeze(1).to_broadcast([P, HG, TA]),
                                same.rearrange("p (h t) -> p h t", h=HG), ALU.mult))
                        yield
                    bk = flip()
                    for x in range(XB):
                        step("tensor", lambda e, x=x, bk=bk: e.matmul(
                            bk[0:TA, x * P:(x + 1) * P], f_nrm[:, x * TA:(x + 1) * TA], f_kbd[:, x, :],
                            start=True, stop=True))
                    s3 = bk[0:TA, :].rearrange("p (x t) -> p x t", t=TA)

                    def bc(v):
                        return v[:, :].unsqueeze(2).to_broadcast([TA, XB * HG, TA])
                    step("vector", lambda e, s3=s3: e.tensor_reduce(f_red[:, :], s3, AX_X, ALU.max))
                    step("vector", lambda e, s3=s3, bc=bc: e.tensor_tensor(f_p[:, :, :], s3, bc(f_red), ALU.subtract))
                    yield
                    step("scalar", lambda e: e.activation(f_p[:, :, :], f_p[:, :, :], ACT.Exp))
                    step("vector", lambda e: e.tensor_reduce(f_red[:, :], f_p[:, :, :], AX_X, ALU.add))
                    step("vector", lambda e: e.reciprocal(f_red[:, :], f_red[:, :]))
                    step("vector", lambda e, bc=bc: e.tensor_tensor(f_p[:, :, :], f_p[:, :, :], bc(f_red), ALU.mult))
                    yield
                    bk = flip()
                    for x in range(XB):
                        step("tensor", lambda e, x=x, bk=bk: e.transpose(
                            bk[:, x * TA:(x + 1) * TA], f_p[:, x * HG:(x + 1) * HG, :].rearrange("p h t -> p (h t)"),
                            ident[0:TA, 0:TA]))
                    step("vector", lambda e, bk=bk: e.tensor_copy(f_pT[:, :], bk[:, 0:W]))
                    yield
                    bk = flip()
                    for x in range(XB):
                        step("tensor", lambda e, x=x, bk=bk: e.transpose(bk[:, x * P:(x + 1) * P], f_vbd[:, x, :], ident))
                    step("vector", lambda e, bk=bk: e.tensor_copy(f_vT[:, :, :], bk.rearrange("p (x f) -> p x f", x=XB)))
                    yield
                    bk = flip()
                    for x in range(XB):
                        step("tensor", lambda e, x=x, bk=bk: e.matmul(
                            bk[:, x * TA:(x + 1) * TA], f_vT[:, x, :], f_pT[:, x * TA:(x + 1) * TA], start=True, stop=True))
                    step("vector", lambda e, it=it, bk=bk: e.tensor_copy(f_out[it][:, :], bk[:, 0:W]))
                    step("vector", lambda e, it=it: e.tensor_tensor(f_cur["q"][:, :], f_cur["q"][:, :], f_out[it][:, :],
                                                                   ALU.add))
                    yield
                dsum, dlim, dflag, nflag = (flag[:, i:i + 1] for i in range(4))
                step("vector", lambda e: e.tensor_tensor(f_sq[:, 0:W], f_out[1][:, :], f_out[0][:, :], ALU.subtract))
                step("vector", lambda e: e.tensor_reduce(diff_cols[:, :], f_sq[:, 0:W], AX_X, ALU.add,
                                                         apply_absolute_value=True))
                bk = flip()
                step("tensor", lambda e, bk=bk: e.matmul(bk[:, 0:1], ones, diff_cols[:, :], start=True, stop=True))
                step("vector", lambda e, bk=bk: e.tensor_scalar(dsum, bk[:, 0:1], 1.0 / (N * D), None, ALU.mult))
                step("vector", lambda e: e.scalar_tensor_tensor(dlim, dsum, col("fac"), col("thr"), ALU.mult, ALU.add))
                step("vector", lambda e: e.tensor_tensor(dflag, dsum, dlim, ALU.is_lt))
                step("vector", lambda e: e.tensor_scalar(nflag, dflag, -1.0, 1.0, ALU.mult, ALU.add))
                step("vector", lambda e: e.tensor_scalar(f_o[:, :], f_out[1][:, :], dflag, None, ALU.mult))
                step("vector", lambda e: e.scalar_tensor_tensor(f_o[:, :], f_out[2][:, :], nflag, f_o[:, :],
                                                                ALU.mult, ALU.add))
                yield
                bk = flip()
                for b in range(B):
                    for h in range(HALVES):
                        at = slice((h * B + b) * TA, (h * B + b + 1) * TA)
                        m = Q.op("tensor", lambda e, b=b, h=h, at=at, bk=bk: e.matmul(
                            bk[0:TA, b * D:(b + 1) * D], f_o[:, at], w_in["o"][:, h, :], start=h == 0, stop=h == 1),
                            [last[0]], mark=h == 1)
                last[0] = m
                step("vector", lambda e, bk=bk: e.tensor_copy(y_first[:, :, :], bk[0:TA, :].rearrange("p (b d) -> p b d", b=B)))
                first_y.append(last[0])
                yield

            xr = [sb(st1, f"xr{i}", [P, TPC, D]) for i in range(3)]
            x1t = [sb(st1, f"x1t{i}", [P, TPC, D]) for i in range(2)]
            hno = [sb(st1, f"hno{i}", [P, TPC, D]) for i in range(2)]
            hT = [sb(st1, f"hT{i}", [P, HALVES, CH]) for i in range(2)]
            stt = [sb(st1, f"st1_{i}", [P, TPC, 9]) for i in range(4)]
            sp = [[sb(st1, f"sp{i}{n}", [P, CH], BF16) for n in ("hi", "mid", "lo")] + [sb(st1, f"sp{i}rem", [P, CH])]
                  for i in range(2)]
            ld, x1m, hm, htm, mm_h, st_x1 = {}, {}, {}, {}, {}, {}
            spn, sp_free = [0], [[], []]

            def mid_load(i):
                c = ORDER[i]
                ld[i] = Q.dma("mid_in", xr[i % 3][:, :, :], a["x"][c * CH:(c + 1) * CH, :].rearrange("(j p) d -> p j d", p=P),
                              [x1m.get(i - 3)])

            def mid_a(i):
                c, r = ORDER[i], i % 2
                x = xr[i % 3]
                m = Q.op("gpsimd", lambda e: e.tensor_tensor(x[:, :, :], x[:, :, :], bo4[:, :, :], ALU.add), [ld[i], m_w])
                if c % CPB == 0:
                    b = c // CPB
                    m = Q.op("vector", lambda e: e.tensor_tensor(x[0:TA, 0, :], x[0:TA, 0, :], y_first[:, b, :], ALU.add),
                             [m, first_y[0]])
                x1m[i] = norm4(stt[r], x, x1t[r], [m], [st_x1.get(i - 2), hm.get(i - 2)])
                st_x1[i] = Q.dma("x1_out", x1_d[c * CH:(c + 1) * CH, :].rearrange("(j p) d -> p j d", p=P),
                                 x1t[r][:, :, :], [x1m[i]])
                hm[i] = norm4(stt[2 + r], x1t[r], hno[r], [x1m[i]], [htm.get(i - 2)])

            def mid_b(i):
                c, r = ORDER[i], i % 2
                b, cc = c // CPB, c % CPB
                at = slice(cc * CH, (cc + 1) * CH)
                htm[i] = transpose4(hno[r], [hT[r][:, h, :] for h in range(HALVES)], 0,
                                    [col("g1_0"), col("g1_1")], [col("c1_0"), col("c1_1")], [hm[i]], [mm_h.get(i - 2)])
                for kind, o0 in (("q", 0), ("k", D)):
                    for o in range(HALVES):
                        k = spn[0] % 2
                        bk = 2 + k
                        spn[0] += 1
                        for h in range(HALVES):
                            m = Q.op("tensor", lambda e, h=h, o=o, o0=o0, bk=bk: e.matmul(
                                banks[bk][:, :], wqkv[:, h, o0 + o * P:o0 + (o + 1) * P], hT[r][:, h, :],
                                start=h == 0, stop=h == 1), [htm[i], m_w, bank_free[bk]], mark=h == 1)
                        sc = SM if kind == "q" else 1.0
                        hi, mid, lo, rem = sp[k]
                        g = b * HALVES + o
                        m1 = Q.op("scalar", lambda e, hi=hi, bk=bk, sc=sc: e.activation(
                            hi[:, :], banks[bk][:, :], ACT.Identity, scale=sc), [m] + sp_free[k])
                        m2 = Q.op("vector", lambda e, hi=hi, rem=rem, bk=bk, sc=sc: e.scalar_tensor_tensor(
                            rem[:, :], banks[bk][:, :], sc, hi[:, :], ALU.mult, ALU.subtract), [m1])
                        bank_free[bk] = m2
                        m3 = Q.op("vector", lambda e, mid=mid, rem=rem: e.tensor_copy(mid[:, :], rem[:, :]),
                                  [m2] + sp_free[k])
                        m4 = Q.op("vector", lambda e, mid=mid, rem=rem, lo=lo: e.tensor_tensor(
                            lo[:, :], rem[:, :], mid[:, :], ALU.subtract), [m3])
                        sp_free[k] = [Q.dma("parts_out", parts[g][kind][n, :, at], t[:, :], [mm])
                                      for n, (t, mm) in enumerate(((hi, m1), (mid, m3), (lo, m4)))]
                        parts_stored.setdefault(g, []).extend(sp_free[k])
                for j in range(TPC):
                    bk = 4 + j // 2
                    for h in range(HALVES):
                        m = Q.op("tensor", lambda e, j=j, h=h, bk=bk: e.matmul(
                            banks[bk][:, (j % 2) * D:(j % 2 + 1) * D], hT[r][:, h, j * P:(j + 1) * P],
                            wqkv[:, h, 2 * D:3 * D], start=h == 0, stop=h == 1), [htm[i], bank_free[bk]], mark=h == 1)
                    if j % 2 == 0:
                        continue
                    for jj in (j - 1, j):
                        for o in range(HALVES):
                            bank_free[bk] = Q.op("scalar", lambda e, j=jj, o=o, bk=bk, kt=cc * TPC + jj: e.activation(
                                v_tok[:, b * HALVES + o, kt, :, 0:HD],
                                banks[bk][:, (j % 2) * D + o * P:(j % 2) * D + (o + 1) * P].rearrange(
                                    "p (h d) -> p h d", h=HG), ACT.Identity), [m, m_ones_v])
                            v_ready[b * HALVES + o] = bank_free[bk]
                mm_h[i] = m

            chain = first_attention()
            PIECES = 4

            def pump(n):
                for _ in range(n):
                    next(chain, None)

            for i in range(3):
                mid_load(i)
            mid_a(0)
            for i in range(NC):
                if i + 1 < NC:
                    if ORDER[i + 1] % CPB == 0:
                        for _ in chain:
                            pass
                    mid_a(i + 1)
                if i + 3 < NC:
                    mid_load(i + 3)
                pump(PIECES)
                mid_b(i)
                pump(PIECES)
            mid_end = [(s, s.n) for s in Q.done.values()] + [x for f in sp_free for x in f] + [st_x1[NC - 1], st_x1[NC - 2]]

        def attention(bufs, heads, fillers, on_assembled, start):
            LEAD = 3
            AHEAD = KT + LEAD
            S_BANKS, T_BANKS, PV, MISC = ((0, 1), (2, 3)), (4, 5), 6, 7
            n_heads = len(heads)
            reduced = [None, None]
            s_at, t_at = [0], [0]
            t_marks = [None, None]
            stack_mark, nmax_mark, s_last, t_last = {}, {}, {}, {}
            pv_mark, exp_mark, evac = {}, {}, {}
            max_marks = {}
            oev_dma = {}

            def load_stack(n):
                inst, hh = heads[n]
                sl = n % 3
                sig = bufs["stack_sig"][sl]
                waits = [t_last.get(n - 3), s_last.get(n - 3)] + list(parts_stored[inst])
                for j in range(6):
                    rows = slice(hh * HD, (hh + 1) * HD)
                    dst = slice(j * HD, (j + 1) * HD)
                    Q.dma_on(sig, bufs["qst"][sl][dst, :], parts[inst]["q"][Q_PARTS[j], rows, :], waits)
                    stack_mark[n] = Q.dma_on(sig, bufs["kst"][sl][dst, :], parts[inst]["k"][K_PARTS[j], rows, :], waits)

            def scores(n, qt):
                sl, width = n % 3, (qt + 1) * P
                mx = bufs["mx"][n % 2]
                for half in range(2):
                    w = min(width - half * 2 * CH, 2 * CH)
                    if w <= 0:
                        continue
                    buf = s_at[0] % 2
                    s_at[0] += 1
                    m = None
                    for i in range((w + CH - 1) // CH):
                        k0 = half * 2 * CH + i * CH
                        kw = min(CH, width - k0)
                        bk = S_BANKS[buf][i]
                        diag = k0 <= qt * P < k0 + CH
                        last = i == (w + CH - 1) // CH - 1
                        m = Q.op("tensor", lambda e, bk=bk, k0=k0, kw=kw, diag=diag: e.matmul(
                            banks[bk][:, 0:kw], bufs["qst"][sl][0:STACK, qt * P:(qt + 1) * P],
                            bufs["kst"][sl][0:STACK, k0:k0 + kw], start=True, stop=not diag),
                            [reduced[buf], stack_mark[n]] + start, mark=last and not diag)
                        if diag:
                            off = qt * P - k0
                            m = Q.op("tensor", lambda e, bk=bk, off=off: e.matmul(
                                banks[bk][:, off:off + P], ident_bf[:, :], mask_s_bf[:, :], start=False, stop=True),
                                [m_c], mark=last)
                    s_last[n] = m
                    src = (bufs["s_wide"][buf][:, 0:w])
                    reduced[buf] = Q.op("vector", lambda e, src=src, qt=qt, half=half: e.tensor_reduce(
                        mx[:, qt, half:half + 1], src, AX_X, ALU.max), [m, max_marks.get(n - 2), bufs["ones_mark"]])

            def combine_max(n):
                mx, mf = bufs["mx"][n % 2], bufs["mf"]
                max_marks[n] = Q.op("vector", lambda e: e.tensor_reduce(mf[:, :], mx[:, :, :], AX_X, ALU.max),
                                    [reduced[0], reduced[1], bank_free[MISC]])

            def turn_max(n):
                mf, nm, rem, mp = bufs["mf"], bufs["nm"], bufs["nm_rem"], bufs["nm_parts"][n % 2]
                m = Q.op("tensor", lambda e: e.transpose(banks[MISC][0:KT, 0:P], mf[:, :], ident),
                         [max_marks[n], bank_free[MISC]])
                v0 = Q.op("vector", lambda e: e.tensor_scalar(nm[:, :], banks[MISC][0:KT, 0:P], -1.0, None, ALU.mult),
                          [m, bufs.get("nm_free")])
                bank_free[MISC] = v0
                v1 = Q.op("vector", lambda e: e.tensor_copy(mp[:, 0, :], nm[:, :]), [v0, nmax_mark.get(n - 2)])
                v2 = Q.op("vector", lambda e: e.tensor_tensor(rem[:, :], nm[:, :], mp[:, 0, :], ALU.subtract), [v1])
                v3 = Q.op("vector", lambda e: e.tensor_copy(mp[:, 1, :], rem[:, :]), [v2])
                v4 = Q.op("vector", lambda e: e.tensor_tensor(mp[:, 2, :], rem[:, :], mp[:, 1, :], ALU.subtract), [v3])
                bufs["nm_free"] = v4
                sl = n % 3
                for i in range(3):
                    nmax_mark[n] = Q.dma_on(bufs["nmax_sig"][sl], bufs["qst"][sl][STACK + i:STACK + i + 1, :].rearrange(
                        "p (q t) -> p q t", q=KT), mp[:, i, :], [v4, t_last.get(n - 3)])

            def chunks(kt):
                c0 = kt * P // CH
                return [(c, kt * P - c0 * CH if c == c0 else 0) for c in range(c0, CPB)]

            def scores_t(t, c, off):
                n, kt = t // KT, t % KT
                sl, r = n % 3, t_at[0] % 2
                bk = T_BANKS[r]
                t_at[0] += 1
                diag = kt * P // CH == c
                m = Q.op("tensor", lambda e: e.matmul(
                    banks[bk][:, off:CH], bufs["kst"][sl][0:ROWS, kt * P:(kt + 1) * P],
                    bufs["qst"][sl][0:ROWS, c * CH + off:(c + 1) * CH], start=True, stop=not diag),
                    [t_marks[r], nmax_mark[n], bufs["ones_mark"]], mark=not diag)
                if diag:
                    m = Q.op("tensor", lambda e: e.matmul(banks[bk][:, off:off + P], ident_bf[:, :], mask_t_bf[:, :],
                                                         start=False, stop=True), [m_c])
                t_last[n] = m
                t_marks[r] = Q.op("scalar", lambda e: e.activation(
                    bufs["p"][t % 3][:, c * CH + off:(c + 1) * CH], banks[bk][:, off:CH], ACT.Exp),
                    [m, pv_mark.get(t - 3)])
                exp_mark[t] = t_marks[r]

            def values(t):
                n, kt = t // KT, t % KT
                g, hh = heads[n]
                for r in range(CPB):
                    m0 = max(0, -((r - kt) // CPB))
                    if m0 >= KT // CPB:
                        continue
                    mov = bufs["p"][t % 3][:, :].rearrange("p (m r i) -> p r m i", r=CPB, i=P)[:, r, m0:, :]
                    m = Q.op("tensor", lambda e, r=r, m0=m0, mov=mov: e.matmul(
                        banks[PV][r * VW:(r + 1) * VW, m0 * P:CH], v_tok[:, g, kt, hh, :], mov,
                        start=kt == 0, stop=kt == KT - CPB + r),
                        [exp_mark[t], v_ready[g], bank_free[PV] if kt == 0 else None], mark=r == CPB - 1)
                pv_mark[t] = m

            def evacuate(n):
                inst, hh = heads[n]
                o = bufs["oev"][n % 2]
                bank_free[PV] = Q.op("scalar", lambda e: e.activation(o[:, :], banks[PV][:, :], ACT.Identity),
                                     [pv_mark[n * KT + KT - 1]] + list(oev_dma.get(n - 2, ())))
                marks = []
                rows = slice(hh * HD, (hh + 1) * HD)
                for r in range(CPB):
                    for buf, r0 in (("num", r * VW), ("den", r * VW + HD)):
                        dst = bufs[buf][inst % 2][rows, :].rearrange("p (m r i) -> p r m i", r=CPB, i=P)[:, r, :, :]
                        marks.append(Q.dma("assemble", dst, o[r0:r0 + HD, :].rearrange("p (m i) -> p m i", i=P),
                                           [bank_free[PV]] + list(asm_free.get(inst - 2, ())), depth=12))
                oev_dma[n] = marks
                on_assembled.setdefault(inst, []).extend(marks)

            last_t = n_heads * KT
            for t in range(-2 * KT, last_t + 1):
                if t % KT == 0 and 0 <= t // KT + 2 < n_heads:
                    load_stack(t // KT + 2)
                s = t + AHEAD
                todo = chunks(t % KT) if 0 <= t < last_t else []
                for c, off in todo[:2]:
                    scores_t(t, c, off)
                s_ok = 0 <= s < n_heads * KT
                if s_ok:
                    scores(s // KT, s % KT)
                for c, off in todo[2:]:
                    scores_t(t, c, off)
                if 0 <= t - 1 < last_t:
                    values(t - 1)
                    if (t - 1) % KT == KT - 1:
                        evacuate((t - 1) // KT)
                if s_ok and s % KT == KT - 1:
                    combine_max(s // KT)
                if 0 <= s - 1 < n_heads * KT and (s - 1) % KT == KT - 1:
                    turn_max((s - 1) // KT)
                for f in fillers.get(t, ()):
                    f()
            for extra in sorted(k for k in fillers if k > last_t):
                for f in fillers[extra]:
                    f()

        Q.phase("attn")
        att = ExitStack()
        bufs = {
            "stack_sig": [Signal(sem(f"stack_in{i}")) for i in range(3)],
            "nmax_sig": [Signal(sem(f"nmax_in{i}")) for i in range(3)],
            "s_wide": [psum[:, 2 * i * CH:2 * (i + 1) * CH] for i in range(2)],
        }
        for name, shape, dt, cnt in (("qst", [P, T], BF16, 3), ("kst", [P, T], BF16, 3), ("p", [P, T], F32, 3),
                                     ("num", [P, T], F32, 2), ("den", [P, T], F32, 2), ("oev", [P, CH], F32, 2),
                                     ("mx", [P, KT, 2], F32, 2), ("nm_parts", [KT, 3, P], BF16, 2)):
            bufs[name] = [sb(att, f"{name}{i}", shape, dt) for i in range(cnt)]
        for name, shape in (("mf", [P, KT]), ("nm", [KT, P]), ("nm_rem", [KT, P])):
            bufs[name] = sb(att, name, shape)
        for sl in range(3):
            Q.op("vector", lambda e, sl=sl: e.memset(bufs["kst"][sl][STACK:ROWS, :], 1.0), mid_end)
        for i in range(2):
            m_o = Q.op("vector", lambda e, i=i: e.memset(bufs["mx"][i][:, :, :], NEG))
        bufs["ones_mark"] = m_o
        for g in parts_stored:
            parts_stored[g] = parts_stored[g] + mid_end
        assembled, asm_free, o_stored = {}, {}, {}

        def fin_stages(g):
            num, den = bufs["num"][g % 2], bufs["den"][g % 2]
            asm_free[g] = []
            stages = []
            for cc in range(CPB):
                at = slice(cc * CH, (cc + 1) * CH)
                for j in range(TPC):
                    def rec(cc=cc, j=j):
                        p = slice(cc * CH + j * P, cc * CH + (j + 1) * P)
                        Q.op("vector", lambda e: e.reciprocal(den[:, p], den[:, p]), assembled[g], mark=j == TPC - 1)
                    stages.append(rec)

                def mul(cc=cc, at=at):
                    m = Q.op("vector", lambda e: e.tensor_tensor(num[:, at], num[:, at], den[:, at], ALU.mult),
                             [(Q.done["vector"], Q.done["vector"].n)])
                    o_stored[g, cc] = Q.dma("o_out", o_ffn[g, :, at], num[:, at], [m])
                    asm_free[g].append(o_stored[g, cc])
                stages.append(mul)
            return stages

        fillers = {}
        for g in range(NG):
            for i, f in enumerate(fin_stages(g)):
                fillers.setdefault(HG * KT * (g + 1) + 2 + i, []).append(f)
        attention(bufs, [(g, hh) for g in range(NG) for hh in range(HG)], fillers, assembled, mid_end)
        att2_end = [(s, s.n) for s in Q.done.values()] + [x for v in asm_free.values() for x in v]
        att.close()

        Q.phase("gate")
        v_stack.close()
        NT = NC * TPC
        xn_d = dram("xn_d", [N, D])
        y_d = dram("y_d", [2 * N + P, D])
        acc = sb(ctx, "acc", [P, NC, TPC, D])
        gate_w = sb(ctx, "gate_w", [P, NT, 2])
        from_u = sb(ctx, "from_u", [P, E_ * NT], U32)
        to_u = sb(ctx, "to_u", [P, E_ * NT], U32)
        counts_i = sb(ctx, "counts_i", [P, E_], I32)
        b1_sb = sb(ctx, "b1_sb", [P, E_, FT])
        w1s = [sb(ctx, f"w1s{i}", [P, HALVES, F_]) for i in range(2)]
        w2s = [sb(ctx, f"w2s{i}", [P, FT, D]) for i in range(2)]
        with ExitStack() as st3:
            wo2 = sb(st3, "wo2", [P, HALVES, D])
            wg = sb(st3, "wg", [P, HALVES, E_])
            b2_sb = sb(st3, "b2_sb", [E_, D])
            rc = sb(st3, "rc", [P, P + (E_ + 2) * NT + 2 * E_ + 1])
            before = rc[:, 0:P]
            iota = rc[:, P:P + E_ * NT]
            row1 = rc[:, P + E_ * NT:P + (E_ + 2) * NT]
            slot0 = rc[:, P + (E_ + 2) * NT:P + (E_ + 2) * NT + E_]
            rank8 = rc[:, P + (E_ + 2) * NT + E_:P + (E_ + 2) * NT + 2 * E_]
            spare1 = rc[:, P + (E_ + 2) * NT + 2 * E_:]
            oin = [[sb(st3, f"of{r}{h}", [P, CH]) for h in range(HALVES)] for r in range(2)]
            x1r = [sb(st3, f"x1r{i}", [P, TPC, D]) for i in range(2)]
            res = [sb(st3, f"res{i}", [P, TPC, D]) for i in range(2)]
            xno = [sb(st3, f"xno{i}", [P, TPC, D]) for i in range(2)]
            xfT = [sb(st3, f"xfT{i}", [P, HALVES, CH]) for i in range(2)]
            stg = [sb(st3, f"stg{i}", [P, TPC, 9]) for i in range(2)]
            w3_in = Signal(sem("w3_in"))
            Q.dma_on(w3_in, wo2[:, :, :], a["w_o"].rearrange("(h p) o -> p h o", p=P), att2_end)
            Q.dma_on(w3_in, wg[:, :, :], a["w_gate"].rearrange("(h p) o -> p h o", p=P))
            Q.dma_on(w3_in, rc[:, :], a["routes"])
            Q.dma_on(w3_in, b2_sb[:, :], a["b2"])
            m_w3 = Q.dma_on(w3_in, b1_sb[:, :, :], a["b1"].rearrange("p (e f) -> p e f", e=E_))
            ld, xn_m, tr_m, mm_o, acc_m, st_xn, lg_ev, mm_lg = {}, {}, {}, {}, {}, {}, {}, {}

            def g_load(c):
                b, cc, r = c // CPB, c % CPB, c % 2
                at = slice(cc * CH, (cc + 1) * CH)
                ms = [Q.dma("mid_in", oin[r][h][:, :], o_ffn[b * HALVES + h, :, at],
                            [mm_o.get(c - 2), m_w3]) for h in range(HALVES)]
                ms.append(Q.dma("mid_in", x1r[r][:, :, :], x1_d[c * CH:(c + 1) * CH, :].rearrange("(j p) d -> p j d", p=P),
                                [acc_m.get(c - 2), m_w3]))
                ld[c] = ms

            def g_a(c):
                r = c % 2
                for j in range(TPC):
                    bk = j // 2
                    for h in range(HALVES):
                        m = Q.op("tensor", lambda e, j=j, h=h, bk=bk: e.matmul(
                            banks[bk][:, (j % 2) * D:(j % 2 + 1) * D], oin[r][h][:, j * P:(j + 1) * P], wo2[:, h, :],
                            start=h == 0, stop=h == 1), ld[c] + [m_w3, bank_free[bk]], mark=h == 1)
                    if j % 2 == 1:
                        m1 = Q.op("vector", lambda e, bk=bk, j=j: e.tensor_tensor(
                            res[r][:, j - 1:j + 1, :], banks[bk][:, :].rearrange("p (j d) -> p j d", j=2),
                            x1r[r][:, j - 1:j + 1, :], ALU.add), [m, xn_m.get(c - 2), acc_m.get(c - 2)] + ld[c])
                        bank_free[bk] = m1
                mm_o[c] = m
                acc_m[c] = Q.op("gpsimd", lambda e: e.tensor_tensor(acc[:, c, :, :], res[r][:, :, :], x1r[r][:, :, :],
                                                                   ALU.add), [m1])
                xn_m[c] = norm4(stg[r], res[r], xno[r], [m1], [tr_m.get(c - 2), st_xn.get(c - 2)])
                st_xn[c] = Q.dma("x1_out", xn_d[c * CH:(c + 1) * CH, :].rearrange("(j p) d -> p j d", p=P),
                                 xno[r][:, :, :], [xn_m[c]])

            B_LG, B_TABLE, B_GT, B_B2 = 4, 5, 6, 7
            lg = [sb(st3, f"lg{i}", [P, TPC, E_]) for i in range(2)]

            def g_b(c):
                r = c % 2
                tr_m[c] = transpose4(xno[r], [xfT[r][:, h, :] for h in range(HALVES)], 2,
                                     [col("g2_0"), col("g2_1")], [col("c2_0"), col("c2_1")], [xn_m[c]], [mm_lg.get(c - 2)])
                for j in range(TPC):
                    for h in range(HALVES):
                        m = Q.op("tensor", lambda e, j=j, h=h: e.matmul(
                            banks[B_LG][:, j * E_:(j + 1) * E_], xfT[r][:, h, j * P:(j + 1) * P], wg[:, h, :],
                            start=h == 0, stop=h == 1), [tr_m[c], bank_free[B_LG]], mark=h == 1)
                mm_lg[c] = m
                bank_free[B_LG] = lg_ev[c] = Q.op("vector", lambda e: e.tensor_copy(
                    lg[r][:, :, :], banks[B_LG][:, 0:TPC * E_].rearrange("p (t e) -> p t e", e=E_)), [m])

            one = sb(st3, "g_one", [P, TPC])
            t1, t2, hot1, hot2, sel, pos = (sb(st3, f"g_{n}", [P, TPC, E_]) for n in ("t1", "t2", "hot1", "hot2", "sel", "pos"))
            base = sb(st3, "g_base", [P, E_])
            slot_f = sb(st3, "g_slot_f", [P, TPC, 2])
            slot_i, lo_i, hi_i = (sb(st3, f"g_{n}", [P, TPC, 2], I32) for n in ("slot_i", "lo_i", "hi_i"))
            lo_f, hi_f = (sb(st3, f"g_{n}", [P, TPC, 2]) for n in ("lo_f", "hi_f"))
            RING = 4
            at_lo = [sb(st3, f"at_lo{i}", [P, P]) for i in range(RING)]
            at_hi = [sb(st3, f"at_hi{i}", [P, E_ * NT]) for i in range(RING)]
            gT = sb(st3, "gT", [E_, TPC, P])
            put = {}

            def bc(x):
                return x.unsqueeze(2).to_broadcast([P, TPC, E_])

            def dve(f, waits=()):
                return Q.op("vector", f, [(Q.done["vector"], Q.done["vector"].n)] + list(waits))

            def pick(src, w, hot):
                dve(lambda e: e.tensor_reduce(w, src[:, :, :], AX_X, ALU.max))
                dve(lambda e: e.tensor_tensor(hot[:, :, :], src[:, :, :], bc(w), ALU.is_equal))
                dve(lambda e: e.tensor_tensor(hot[:, :, :], hot[:, :, :], rank4, ALU.mult))
                dve(lambda e: e.tensor_reduce(one[:, :], hot[:, :, :], AX_X, ALU.max))
                dve(lambda e: e.tensor_tensor(hot[:, :, :], rank4, bc(one[:, :]), ALU.is_equal))

            rank4 = rank8.unsqueeze(1).to_broadcast([P, TPC, E_])

            def g_route(c):
                g = lg[c % 2]
                if c == 0:
                    dve(lambda e: e.tensor_copy(base[:, :], slot0), [m_w3])
                dve(lambda e: e.tensor_reduce(one[:, :], g[:, :, :], AX_X, ALU.max), [lg_ev[c]])
                m = dve(lambda e: e.tensor_tensor(g[:, :, :], g[:, :, :], bc(one[:, :]), ALU.subtract))
                m = Q.op("scalar", lambda e: e.activation(g[:, :, :], g[:, :, :], ACT.Exp), [m])
                dve(lambda e: e.tensor_reduce(one[:, :], g[:, :, :], AX_X, ALU.add), [m])
                dve(lambda e: e.reciprocal(one[:, :], one[:, :]))
                dve(lambda e: e.tensor_tensor(g[:, :, :], g[:, :, :], bc(one[:, :]), ALU.mult))
                tiles = slice(c * TPC, (c + 1) * TPC)
                w1_, w2_ = gate_w[:, tiles, 0], gate_w[:, tiles, 1]
                pick(g, w1_, hot1)
                dve(lambda e: e.scalar_tensor_tensor(t1[:, :, :], hot1[:, :, :], -2.0, g[:, :, :], ALU.mult, ALU.add))
                pick(t1, w2_, hot2)
                m_sel = dve(lambda e: e.tensor_tensor(sel[:, :, :], hot1[:, :, :], hot2[:, :, :], ALU.add))
                s2 = sel[:, :, :].rearrange("p t e -> p (t e)")
                w = TPC * E_
                Q.op("tensor", lambda e: e.matmul(banks[B_LG][:, 2 * w:3 * w], before, s2, start=True, stop=True),
                     [m_sel, bank_free[B_LG]], mark=False)
                m_pre = Q.op("tensor", lambda e: e.matmul(banks[B_LG][:, 3 * w:4 * w], ones, s2, start=True, stop=True))
                dve(lambda e: e.tensor_tensor(one[:, :], w1_, w2_, ALU.add))
                dve(lambda e: e.reciprocal(one[:, :], one[:, :]))
                dve(lambda e: e.tensor_tensor(w1_, w1_, one[:, :], ALU.mult))
                dve(lambda e: e.tensor_tensor(w2_, w2_, one[:, :], ALU.mult))
                dve(lambda e: e.tensor_tensor(t1[:, :, :], hot1[:, :, :], bc(w1_), ALU.mult))
                dve(lambda e: e.tensor_tensor(t2[:, :, :], hot2[:, :, :], bc(w2_), ALU.mult))
                m_g = dve(lambda e: e.tensor_tensor(t1[:, :, :], t1[:, :, :], t2[:, :, :], ALU.add))
                for j in range(TPC):
                    m = Q.op("tensor", lambda e, j=j: e.transpose(banks[B_GT][0:E_, j * P:(j + 1) * P], t1[:, j, :], ident),
                             [m_g, bank_free[B_GT]], mark=j == TPC - 1)
                bank_free[B_GT] = dve(lambda e: e.tensor_copy(
                    gT[:, :, :], banks[B_GT][0:E_, :].rearrange("p (t i) -> p t i", t=TPC)), [m])
                for j in range(TPC):
                    m = Q.op("tensor", lambda e, j=j: e.matmul(banks[B_B2][:, (j % 2) * D:(j % 2 + 1) * D], gT[:, j, :],
                                                              b2_sb[:, :], start=True, stop=True),
                             [bank_free[B_GT], bank_free[B_B2]], mark=j % 2 == 1)
                    if j % 2 == 1:
                        bank_free[B_B2] = dve(lambda e, j=j: e.tensor_tensor(
                            acc[:, c, j - 1:j + 1, :], acc[:, c, j - 1:j + 1, :],
                            banks[B_B2][:, :].rearrange("p (j d) -> p j d", j=2), ALU.add), [m, acc_m[c]])
                for j in range(TPC):
                    dve(lambda e, j=j: e.tensor_tensor(pos[:, j, :], banks[B_LG][:, 2 * w + j * E_:2 * w + (j + 1) * E_],
                                                       base[:, :], ALU.add), [m_pre])
                    bank_free[B_LG] = dve(lambda e, j=j: e.tensor_tensor(
                        base[:, :], banks[B_LG][:, 3 * w + j * E_:3 * w + (j + 1) * E_], base[:, :], ALU.add))
                for k, hot in ((0, hot1), (1, hot2)):
                    dve(lambda e, hot=hot: e.tensor_tensor(t2[:, :, :], hot[:, :, :], pos[:, :, :], ALU.mult))
                    dve(lambda e, k=k: e.tensor_reduce(slot_f[:, :, k], t2[:, :, :], AX_X, ALU.add))
                dve(lambda e: e.tensor_copy(slot_i[:, :, :], slot_f[:, :, :]))
                dve(lambda e: e.tensor_scalar(lo_i[:, :, :], slot_i[:, :, :], P - 1, None, ALU.bitwise_and))
                dve(lambda e: e.tensor_scalar(hi_i[:, :, :], slot_i[:, :, :], 7, None, ALU.logical_shift_right))
                dve(lambda e: e.tensor_copy(lo_f[:, :, :], lo_i[:, :, :]))
                m_lh = dve(lambda e: e.tensor_copy(hi_f[:, :, :], hi_i[:, :, :]))
                for j in range(TPC):
                    for k in range(2):
                        n = (c * TPC + j) * 2 + k
                        r = n % RING
                        Q.op("vector", lambda e, j=j, k=k, r=r: e.tensor_scalar(
                            at_lo[r][:, :], iota[:, 0:P], lo_f[:, j, k:k + 1], None, ALU.is_equal),
                            [m_lh, put.get(n - RING)], mark=False)
                        m = Q.op("vector", lambda e, j=j, k=k, r=r, t=c * TPC + j: e.tensor_scalar(
                            at_hi[r][:, :], iota, hi_f[:, j, k:k + 1], row1[:, 2 * t + k:2 * t + k + 1], ALU.is_equal, ALU.mult))
                        put[n] = Q.op("tensor", lambda e, n=n, r=r: e.matmul(
                            banks[B_TABLE][:, 0:E_ * NT], at_lo[r][:, :], at_hi[r][:, :], start=n == 0,
                            stop=n == 2 * NT - 1), [m, bank_free[B_TABLE] if n == 0 else None])

            g_load(0)
            g_load(1)
            g_a(0)
            for c in range(NC):
                if c + 1 < NC:
                    g_a(c + 1)
                if c + 2 < NC:
                    g_load(c + 2)
                g_b(c)
                if c >= 1:
                    g_route(c - 1)
            g_route(NC - 1)
            table, empty, to_f = at_hi[:3]
            bank_free[B_TABLE] = dve(lambda e: e.tensor_copy(table[:, :], banks[B_TABLE][:, 0:E_ * NT]), [put[2 * NT - 1]])
            dve(lambda e: e.tensor_scalar(empty[:, :], table[:, :], 0.0, None, ALU.is_equal))
            dve(lambda e: e.scalar_tensor_tensor(to_f[:, :], empty[:, :], spare1, table[:, :], ALU.mult, ALU.add))
            dve(lambda e: e.tensor_scalar(to_u[:, :], to_f[:, :], -1.0, None, ALU.add))
            dve(lambda e: e.tensor_tensor(table[:, :], table[:, :], empty[:, :], ALU.add))
            dve(lambda e: e.tensor_scalar(from_u[:, :], table[:, :], -1.0, None, ALU.add))
            dve(lambda e: e.tensor_scalar(from_u[:, :], from_u[:, :], 1, None, ALU.logical_shift_right))
            m_counts = dve(lambda e: e.tensor_tensor(counts_i[:, :], base[:, :], slot0, ALU.subtract))
            gate_end = [(s, s.n) for s in Q.done.values()] + [st_xn[NC - 1], st_xn[NC - 2]] + list(st_xn.values())

        T_BANK, H_BANKS, Y_BANKS = 0, (1, 2, 3, 4), (5, 6)
        xg = [[sb(ctx, f"xg{i}{k}", [P, BT, D]) for k in range(2)] for i in range(2)]
        xgT = sb(ctx, "xgT", [P, HALVES, BLK])
        he = sb(ctx, "he", [P, FT, BLK])
        yb = [[sb(ctx, f"yb{i}{k}", [P, BT, D]) for k in range(2)] for i in range(2)]
        w_sig = [Signal(sem(f"expert_in{i}")) for i in range(2)]
        settled = {e: Signal(sem(f"settled_{e}")) for e in ("tensor", "vector", "gpsimd")}
        w_mark = {}

        def load_expert(e_, waits):
            i = e_ % 2
            Q.dma_on(w_sig[i], w1s[i][:, :, :], a["w1"][e_].rearrange("(h p) f -> p h f", p=P), waits)
            w_mark[e_] = Q.dma_on(w_sig[i], w2s[i][:, :, :], a["w2"][e_].rearrange("(f p) d -> p f d", p=P), waits)

        load_expert(0, gate_end)
        load_expert(1, gate_end)
        for e in Q.ENGINES:
            Q.q[e].append((Q._waits(e, gate_end), lambda g: None, None, 0))
            for e_ in range(E_):
                Q.q[e].append(("count", e_))

        rows, turned, got = {}, {}, {}

        def fetch(e_, j):
            pe_before = (settled["tensor"], e_ - 1) if e_ >= 2 else None
            for t in range(BT):
                colm = e_ * NT + j * BT + t
                rows[e_, j] = Q.gather(got[e_][j % 2], xg[e_ % 2][j % 2][:, t, :], xn_d, from_u[:, colm:colm + 1],
                                       [turned.get((e_, j - 2)), pe_before])

        def fetch_first(e_):
            got[e_] = [Signal(sem(f"rows{e_}_{k}")) for k in range(2)]
            with Q.more_than(e_, 0):
                fetch(e_, 0)

        def expert(e_):
            par = e_ % 2
            Q.phase(f"expert{e_}", ("tensor", "vector", "scalar"))
            turn_sig = Signal(sem(f"turned{e_}"))
            out_sig = Signal(sem(f"y_out{e_}"))
            y_before = (settled["vector"], e_) if e_ >= 1 else None
            out_before = (settled["gpsimd"], e_) if e_ >= 1 else None
            xT_m, he_m, y_ev, stored = {}, {}, {}, {}

            def turn(j):
                for h in range(HALVES):
                    for t in range(BT):
                        m = Q.op("tensor", lambda e, h=h, t=t: e.transpose(
                            banks[T_BANK][:, (h * BT + t) * P:(h * BT + t + 1) * P], xg[par][j % 2][:, t, h * P:(h + 1) * P],
                            ident), [rows[e_, j], xT_m.get(j - 1)], mark=h == 1 and t == BT - 1, signal=turn_sig)
                turned[e_, j] = m
                for h in range(HALVES):
                    xT_m[j] = Q.op("scalar", lambda e, h=h: e.activation(
                        xgT[:, h, :], banks[T_BANK][:, h * BLK:(h + 1) * BLK], ACT.Identity, scale=col(f"g2_{h}"),
                        bias=col(f"c2_{h}")), [m])

            def hidden(j):
                for pair in range(FT // 2):
                    bk = H_BANKS[pair]
                    for f in (2 * pair, 2 * pair + 1):
                        at = slice((f % 2) * BLK, (f % 2 + 1) * BLK)
                        for h in range(HALVES):
                            m = Q.op("tensor", lambda e, f=f, h=h, bk=bk, at=at: e.matmul(
                                banks[bk][:, at], w1s[par][:, h, f * P:(f + 1) * P], xgT[:, h, :],
                                start=h == 0, stop=h == 1), [xT_m[j], w_mark[e_]], mark=h == 1 and f % 2 == 1)
                    for f in (2 * pair, 2 * pair + 1):
                        at = slice((f % 2) * BLK, (f % 2 + 1) * BLK)
                        he_m[j, f] = Q.op("scalar", lambda e, f=f, bk=bk, at=at: e.activation(
                            he[:, f, :], banks[bk][:, at], ACT.Gelu_apprx_tanh, bias=b1_sb[:, e_, f:f + 1]), [m])

            def down(j):
                for t in range(BT):
                    bk = Y_BANKS[t]
                    for f in range(FT):
                        m = Q.op("tensor", lambda e, f=f, t=t, bk=bk: e.matmul(
                            banks[bk][:, 0:D], he[:, f, t * P:(t + 1) * P], w2s[par][:, f, :],
                            start=f == 0, stop=f == FT - 1), [he_m[j, f], y_ev.get((j - 1, t)), y_before],
                            mark=f == FT - 1)
                    y_ev[j, t] = Q.op("vector", lambda e, t=t, bk=bk: e.tensor_copy(
                        yb[par][j % 2][:, t, :], banks[bk][:, 0:D]), [m, stored.get(j - 2, out_before)])
                for t in range(BT):
                    colm = e_ * NT + j * BT + t
                    stored[j] = Q.scatter(out_sig, y_d, to_u[:, colm:colm + 1], yb[par][j % 2][:, t, :],
                                          [y_ev[j, t], (out_sig, out_sig.n), out_before])

            def block(j):
                hidden(j)
                more = j + 1 < N // BLK
                if more:
                    with Q.more_than(e_, (j + 1) * BLK):
                        fetch(e_, j + 1)
                        turn(j + 1)
                down(j)
                last_store = stored[j]
                if more:
                    with Q.more_than(e_, (j + 1) * BLK):
                        block(j + 1)
                Q.wait("gpsimd", last_store)

            if e_ + 1 < E_:
                fetch_first(e_ + 1)
            with Q.more_than(e_, 0):
                turn(0)
                block(0)
            for eng, signal in settled.items():
                Q.settle(eng, signal)
            if e_ + 2 < E_:
                load_expert(e_ + 2, [(settled["tensor"], e_ + 1)])

        fetch_first(0)
        for e_ in range(E_):
            expert(e_)

        Q.phase("final", ("vector", "scalar"))
        yg = [sb(ctx, f"yg{i}", [P, TPC, 2, D]) for i in range(2)]
        fst = [sb(ctx, f"fst{i}", [P, TPC, 9]) for i in range(2)]
        fin = [sb(ctx, f"fin{i}", [P, TPC, D]) for i in range(2)]
        used, fin_st, yg_m = {}, {}, {}

        def load_rows(c):
            yg_m[c] = Q.dma("mid_in", yg[c % 2][:, :, :, :], y_d[2 * c * CH:2 * (c + 1) * CH, :].rearrange(
                "(j p k) d -> p j k d", p=P, k=2), [used.get(c - 2), (settled["gpsimd"], E_)])

        load_rows(0)
        load_rows(1)
        for c in range(NC):
            for j in range(TPC):
                for k in range(2):
                    m = Q.op("vector", lambda e, c=c, j=j, k=k: e.scalar_tensor_tensor(
                        acc[:, c, j, :], yg[c % 2][:, j, k, :], gate_w[:, c * TPC + j, k:k + 1], acc[:, c, j, :],
                        ALU.mult, ALU.add), [yg_m[c], m if k else None])
            used[c] = m
            if c + 2 < NC:
                load_rows(c + 2)
            r = c % 2
            m = norm4(fst[r], acc[:, c, :, :], fin[r], [used[c]], [fin_st.get(c - 2)])
            fin_st[c] = Q.dma("x1_out", out[c * CH:(c + 1) * CH, :].rearrange("(j p) d -> p j d", p=P),
                              fin[r][:, :, :], [m])
        all_dma = [s for sigs, _ in Q.rings.values() for s in sigs if s.n]
        final_waits = [(s.sem, s.n) for s in all_dma]

        block = ctx.enter_context(nc.Block())

        @block.sync
        def _(eng):
            Q.play("sync", eng, counts_i)
            for s, v in final_waits:
                eng.wait_ge(s, v)

        @block.tensor
        def _(eng):
            Q.play("tensor", eng, counts_i)

        @block.vector
        def _(eng):
            Q.play("vector", eng, counts_i)

        @block.scalar
        def _(eng):
            Q.play("scalar", eng, counts_i)

        @block.gpsimd
        def _(eng):
            Q.play("gpsimd", eng, counts_i)


def shape_constants():
    p = np.arange(P)
    same = (p[:, None] // HD == p[None, :] // HD).astype(np.float32)
    eye = np.eye(P, dtype=np.float32)
    later = np.float32(NEG)
    mask_s = np.where(p[None, :] > p[:, None], later, np.float32(0))
    consts = np.concatenate([eye, same / HD, eye - same / HD, mask_s, mask_s.T, np.ones((P, P), np.float32), same], 1)
    nt = N // P
    row1 = 1 + 2 * (p[:, None, None] + P * np.arange(nt)[None, :, None]) + np.arange(2)[None, None, :]
    rows = [np.broadcast_to(r, (P, len(r))) for r in (np.arange(E_ * nt), np.arange(E_) * N, np.arange(E_, 0, -1))]
    routes = np.concatenate([p[:, None] < p[None, :], rows[0], row1.reshape(P, 2 * nt), rows[1], rows[2],
                             1 + 2 * N + p[:, None]], 1)
    return np.ascontiguousarray(consts.astype(np.float32)), np.ascontiguousarray(routes.astype(np.float32))


def kernel(**inputs):
    import concourse.bacc as _bacc
    from concourse.bass_utils import run_bass_kernel_spmd as _run

    A = {k[len("L0_attn_"):]: np.asarray(v) for k, v in inputs.items() if k.startswith("L0_attn_")}
    G = {k[len("L0_ffn_"):]: np.asarray(v) for k, v in inputs.items() if k.startswith("L0_ffn_")}

    def halves(v):
        return [v[i * P:(i + 1) * P] for i in range(HALVES)]

    def per_head(v):
        return np.tile(v, HG)

    def everywhere(v):
        return np.broadcast_to(v, (P,))

    cols = np.stack(halves(A["bq"]) + halves(A["bv"]) + halves(A["lna_w"]) + halves(G["ln1_g"]) + halves(G["ln1_b"])
                    + halves(G["ln2_g"]) + halves(G["ln2_b"])
                    + [per_head(A["lnc_w"]), per_head(A["lnd_w"]), per_head(A["blq"]), per_head(A["blk"]), per_head(A["blv"]),
                       everywhere(A["temp"]), everywhere(A["threshold"]), everywhere(A["factor"])], axis=1)
    consts, routes = shape_constants()
    arrays = {
        "x": A["x"].reshape(N, D), "consts": consts, "routes": routes, "cols": cols,
        "WqT": A["Wq"].T, "WkT": A["Wk"].T, "WvT": A["Wv"].T, "WoT": A["Wo"].T,
        "WlqT": A["Wlq"].T, "WlkT": A["Wlk"].T, "WlvT": A["Wlv"].T,
        "bo4": np.tile(A["bo"], (P, TPC)),
        "w_qkv": G["w_qkv"], "w_o": G["w_o"], "w_gate": G["w_gate"], "w1": G["w1"], "w2": G["w2"], "b2": G["b2"],
        "b1": G["b1"].reshape(E_, FT, P).transpose(2, 0, 1).reshape(P, E_ * FT),
    }
    arrays = {f"in_{k}": np.ascontiguousarray(v) for k, v in arrays.items()}
    nc = _bacc.Bacc("TRN2", target_bir_lowering=False, num_devices=1)
    aps = {k[3:]: nc.dram_tensor(k, v.shape, mybir.dt.from_np(v.dtype), kind="ExternalInput").ap()
           for k, v in arrays.items()}
    res = nc.dram_tensor("out_0", (N, D), F32, kind="ExternalOutput").ap()
    build_program(nc, aps, res)
    r = _run(nc, [arrays], core_ids=[0])
    return r.results[0]["out_0"].reshape(B, T, D)
```

```python
from contextlib import ExitStack, contextmanager

import numpy as np

import concourse.bass as bass
from concourse import mybir

F32 = mybir.dt.float32
BF16 = mybir.dt.bfloat16
I32 = mybir.dt.int32
U32 = mybir.dt.uint32
ACT = mybir.ActivationFunctionType
ALU = mybir.AluOpType
AX_X = mybir.AxisListType.X

P = 128
B, T, D, H = 2, 2048, 256, 16
HD = D // H
HALVES = D // P
HG = P // HD
NG = B * HALVES
N = B * T
CH = 512
CPB = T // CH
NC = N // CH
TPC = CH // P
KT = T // P
ITERS = 3
TA = H
XB = HALVES * B
E_, F_ = 8, 1024
FT = F_ // P
BLK = 256
BT = BLK // P
EPS = 1e-5
NEG = -3.0e38
SM = 1.0 / float(np.sqrt(HD))
QKS = HD ** -0.25
STACK = 6 * HD
ROWS = STACK + 3
Q_PARTS = (0, 0, 0, 1, 1, 2)
K_PARTS = (0, 1, 2, 0, 1, 0)
VW = 2 * HD

COLS = ["bq0", "bq1", "bv0", "bv1", "lna0", "lna1", "g1_0", "g1_1", "c1_0", "c1_1",
        "g2_0", "g2_1", "c2_0", "c2_1", "lnc", "lnd", "blq", "blk", "blv", "temp", "thr", "fac"]
COL = {n: i for i, n in enumerate(COLS)}


class Signal:

    def __init__(self, sem):
        self.sem, self.n = sem, 0


class Queues:

    ENGINES = ("tensor", "vector", "scalar", "gpsimd", "sync")

    def __init__(self, new_sem):
        self.q = {e: [] for e in self.ENGINES}
        self.seen = {e: {} for e in self.ENGINES}
        self.new_sem = new_sem
        self.done = {}
        self.rings = {}

    def phase(self, name, engines=ENGINES[:4]):
        self.done = {e: Signal(self.new_sem(f"{e}_done_{name}")) for e in engines}

    def _waits(self, eng, waits):
        need = []
        for w in waits:
            if w is None:
                continue
            sig, v = w
            if self.seen[eng].get(sig, 0) < v:
                self.seen[eng][sig] = v
                need.append((sig.sem, v))
        return need

    def op(self, eng, build, waits=(), mark=True, signal=None):
        need = self._waits(eng, waits)
        sig = signal or self.done[eng] if mark else None
        if mark:
            sig.n += 1
        self.q[eng].append((need, build, sig.sem if mark else None, 1))
        return (sig, sig.n) if mark else None

    def dma_on(self, signal, dst, src, waits=()):
        need = self._waits("sync", waits)
        signal.n += 16
        self.q["sync"].append((need, lambda e, d=dst, s=src: e.dma_start(d, s), signal.sem, 16))
        return (signal, signal.n)

    def dma(self, ring, dst, src, waits=(), depth=6):
        if ring not in self.rings:
            self.rings[ring] = ([Signal(self.new_sem(f"{ring}_{i}")) for i in range(depth)], [0])
        sigs, at = self.rings[ring]
        s = sigs[at[0] % len(sigs)]
        at[0] += 1
        return self.dma_on(s, dst, src, list(waits) + [(s, s.n)] * (s.n > 0))

    def gather(self, signal, out, table, index, waits=()):
        need = self._waits("gpsimd", waits)
        signal.n += 16
        self.q["gpsimd"].append((need, lambda e, o=out, t=table, i=index: e.indirect_dma_start(
            out=o, out_offset=None, in_=t, in_offset=bass.IndirectOffsetOnAxis(ap=i, axis=0)), signal.sem, 16))
        return (signal, signal.n)

    def scatter(self, signal, table, index, src, waits=()):
        need = self._waits("gpsimd", waits)
        signal.n += 16
        self.q["gpsimd"].append((need, lambda e, s=src, t=table, i=index: e.indirect_dma_start(
            out=t, out_offset=bass.IndirectOffsetOnAxis(ap=i, axis=0), in_=s, in_offset=None), signal.sem, 16))
        return (signal, signal.n)

    def wait(self, eng, mark):
        self.q[eng].append(([(mark[0].sem, mark[1])], lambda e: None, None, 0))

    def settle(self, eng, signal):
        signal.n += 1
        self.q[eng].append(([], lambda e: e.drain(), signal.sem, 1))
        return (signal, signal.n)

    @contextmanager
    def more_than(self, expert, tokens):
        outer, seen = self.q, self.seen
        self.q = {e: [] for e in self.ENGINES}
        self.seen = {e: dict(v) for e, v in seen.items()}
        yield
        inner, self.q, self.seen = self.q, outer, seen
        for e in self.ENGINES:
            if inner[e]:
                self.q[e].append(("more_than", expert, tokens, inner[e]))

    def play(self, name, eng, counts=None):
        self._play(self.q[name], eng, counts, {})

    def _play(self, items, eng, counts, loaded):
        for item in items:
            if item[0] == "count":
                loaded[item[1]] = eng.value_load(counts[0:1, item[1]:item[1] + 1], min_val=0, max_val=N)
                continue
            if item[0] == "more_than":
                with eng.If(loaded[item[1]] > item[2]):
                    self._play(item[3], eng, counts, loaded)
                continue
            need, build, sem, by = item
            for s, v in need:
                eng.wait_ge(s, v)
            ins = build(eng)
            if sem is not None:
                ins.then_inc(sem, by)


def build_program(nc, a, out):
    ctx = ExitStack()
    with ctx:
        def sem(name):
            return ctx.enter_context(nc.semaphore(name))

        Q = Queues(sem)

        def sb(stack, name, shape, dt=F32):
            return stack.enter_context(nc.sbuf_tensor(name, shape, dt))

        def dram(name, shape, dt=F32):
            return nc.dram_tensor(name, shape, dt, kind="Internal").ap()

        psum = ctx.enter_context(nc.psum_tensor("psum", [P, 8 * CH], F32))
        banks = [psum[:, i * CH:(i + 1) * CH] for i in range(8)]
        bank_free = [None] * 8

        o_ffn = dram("o_ffn", [NG, P, T])
        parts = [{k: dram(f"parts_{k}{i}", [3, P, T], BF16) for k in "qk"} for i in range(NG)]
        x1_d = dram("x1_d", [N, D])

        cst = sb(ctx, "cst", [P, 7 * P])
        ident, bmean, center, mask_s, mask_t, ones, same = (cst[:, i * P:(i + 1) * P] for i in range(7))
        cols = sb(ctx, "cols", [P, len(COLS)])
        ident_bf = sb(ctx, "ident_bf", [P, P], BF16)
        mask_s_bf = sb(ctx, "mask_s_bf", [P, P], BF16)
        mask_t_bf = sb(ctx, "mask_t_bf", [P, P], BF16)
        eps_col = sb(ctx, "eps_col", [P, 1])
        wlin = {k: sb(ctx, f"wl_{k}", [P, P]) for k in "qkv"}
        wnq = sb(ctx, "wnq", [P, ITERS])
        ts_tmp = sb(ctx, "ts_tmp", [P, 4])
        diff_cols = sb(ctx, "diff_cols", [P, 1])
        flag = sb(ctx, "flag", [P, 4])
        NT = NC * TPC
        b1_sb = sb(ctx, "b1_sb", [P, E_, FT])
        b2_sb = sb(ctx, "b2_sb", [P, E_, D])
        wo2 = sb(ctx, "wo2", [P, HALVES, D])
        wg = sb(ctx, "wg", [P, HALVES, E_])
        rc = sb(ctx, "rc", [P, P + (E_ + 2) * NT + 2 * E_ + 1])
        num = [sb(ctx, f"num{i}", [P, T]) for i in range(2)]
        den = [sb(ctx, f"den{i}", [P, T]) for i in range(2)]
        v_stack = ExitStack()
        v_tok = sb(v_stack, "v_tok", [P, NG, KT, HG, VW])

        def col(name):
            return cols[:, COL[name]:COL[name] + 1]

        Q.phase("early")
        setup_in = Signal(sem("setup_in"))
        Q.dma_on(setup_in, cst[:, :], a["consts"])
        m_small = Q.dma_on(setup_in, cols[:, :], a["cols"])
        m_blocks = []
        m_zero = None
        for k in "qkv":
            m_zero = Q.op("vector", lambda e, k=k: e.memset(wlin[k][:, :], 0.0))
        blocks_in = Signal(sem("blocks_in"))
        for k in "qkv":
            for g in range(HG):
                s = slice(g * HD, (g + 1) * HD)
                m_blocks = Q.dma_on(blocks_in, wlin[k][s, s], a[f"Wl{k}T"], [m_zero])
        m_c = None
        for d, s in ((ident_bf, ident), (mask_s_bf, mask_s), (mask_t_bf, mask_t)):
            m_c = Q.op("vector", lambda e, d=d, s=s: e.tensor_copy(d[:, :], s), [m_small])
        m_eps = Q.op("vector", lambda e: e.memset(eps_col[:, :], EPS))
        m_ones_v = Q.op("gpsimd", lambda e: e.memset(v_tok[:, :, :, :, HD:VW], 1.0))
        Q.op("scalar", lambda e: nc.scalar.preload_act_table_set("natural_log_exp_and_others"), mark=False)
        prev = None
        for it in range(ITERS):
            t_, r_, c_, d_ = (ts_tmp[:, i:i + 1] for i in range(4))
            m = Q.op("vector", lambda e, it=it, t_=t_: e.tensor_scalar(t_, col("temp"), 0.005 * it, None, ALU.add),
                     [m_small, prev])
            m2 = Q.op("vector", lambda e, r_=r_, t_=t_: e.tensor_scalar(r_, t_, 1e-18, None, ALU.max), [m])
            m3 = Q.op("vector", lambda e, c_=c_, t_=t_: e.tensor_scalar(c_, t_, 1.0, None, ALU.not_equal), [m])
            m4 = Q.op("vector", lambda e, d_=d_, t_=t_: e.tensor_scalar(d_, t_, 0.0, None, ALU.is_gt), [m])
            m5 = Q.op("vector", lambda e, c_=c_, d_=d_: e.tensor_tensor(c_, c_, d_, ALU.mult), [m3, m4])
            a1 = Q.op("scalar", lambda e, r_=r_: e.activation(r_, r_, ACT.Ln), [m2])
            a2 = Q.op("scalar", lambda e, r_=r_: e.activation(r_, r_, ACT.Exp, scale=-0.5), [a1])
            m6 = Q.op("vector", lambda e, r_=r_, c_=c_: e.scalar_tensor_tensor(r_, r_, -1.0, c_, ALU.add, ALU.mult),
                      [a2, m5])
            m7 = Q.op("vector", lambda e, r_=r_: e.tensor_scalar(r_, r_, 1.0, SM, ALU.add, ALU.mult), [m6])
            prev = Q.op("vector", lambda e, r_=r_, it=it: e.tensor_tensor(wnq[:, it:it + 1], r_, col("lnc"), ALU.mult),
                        [m7])
        m_wnq = prev

        def norm4(st, src, dst, waits, free=(), helper=None):
            m = None
            for j in range(TPC):
                m = Q.op("vector", lambda e, j=j: e.bn_stats(st[:, j, 0:6], src[:, j, :]), list(waits) + list(free),
                         mark=j == TPC - 1)
            yield
            mv = None
            for j in range(TPC):
                mv = Q.op("vector", lambda e, j=j: e.bn_aggr(st[:, j, 6:8], st[:, j, 0:6]), [m], mark=j == TPC - 1)
            s1 = Q.op("scalar", lambda e: e.activation(st[:, :, 8], st[:, :, 7], ACT.Ln, bias=eps_col[:, :]), [mv, m_eps])
            s2 = Q.op("scalar", lambda e: e.activation(st[:, :, 8], st[:, :, 8], ACT.Exp, scale=-0.5), [s1])
            yield
            mine = TPC - 1 if helper else TPC
            marks = []
            for j in range(TPC):
                m = Q.op("vector" if j < mine else helper, lambda e, j=j: e.tensor_scalar(
                    dst[:, j, :], src[:, j, :], st[:, j, 6:7], st[:, j, 8:9], ALU.subtract, ALU.mult), [s2, mv] + list(free),
                    mark=j >= mine - 1)
                if m is not None:
                    marks.append(m)
            if helper:
                return marks
            return m

        def in_turn(*works):
            works = list(works)
            while works:
                for w in list(works):
                    if next(w, works) is works:
                        works.remove(w)
                yield

        def transpose4(src, dst, b0, scales, biases, waits, free):
            marks = []
            for h in range(HALVES):
                bk = b0 + h
                for j in range(TPC):
                    m = Q.op("tensor", lambda e, h=h, j=j, bk=bk: e.transpose(
                        banks[bk][:, j * P:(j + 1) * P], src[:, j, h * P:(h + 1) * P], ident),
                        list(waits) + [bank_free[bk], m_small], mark=j == TPC - 1)
                kw = {} if biases is None else {"bias": biases[h]}
                bank_free[bk] = Q.op("scalar", lambda e, h=h, bk=bk, kw=kw: e.activation(
                    dst[h], banks[bk][:, :], ACT.Identity, scale=scales[h], **kw), [m, m_small] + list(free))
                marks.append(bank_free[bk])
            return marks[-1]

        parts_stored, v_ready = {}, {}
        ORDER = [c for c in range(NC) if c % CPB] + [c for c in range(NC) if c % CPB == 0]
        with ExitStack() as st1:
            w_in = {k: sb(st1, f"w{k}_sb", [P, HALVES, D]) for k in "qkvo"}
            wqkv = sb(st1, "wqkv", [P, HALVES, 3 * D])
            bo4 = sb(st1, "bo4", [P, TPC, D])
            y_first = sb(st1, "y_first", [TA, B, D])
            weights_in = Signal(sem("weights_in"))
            xs = sb(st1, "xs", [B * TA, D])
            for b in range(B):
                Q.dma_on(weights_in, xs[b * TA:(b + 1) * TA, :], a["x"][b * T:b * T + TA, :])
            Q.dma_on(weights_in, bo4[:, :, :], a["bo4"].rearrange("p (j d) -> p j d", j=TPC))
            for k in "qkvo":
                Q.dma_on(weights_in, w_in[k][:, :, :], a[f"W{k}T"].rearrange("(h p) o -> p h o", p=P))
            m_w = Q.dma_on(weights_in, wqkv[:, :, :], a["w_qkv"].rearrange("(h p) o -> p h o", p=P))

            W = XB * TA
            B_LIN, B_CEN = 6, 7
            f_stat = sb(st1, "f_stat", [B * TA, 9])
            f_xn = sb(st1, "f_xn", [B * TA, D])
            f_xT = sb(st1, "f_xT", [P, HALVES, B * TA])
            f_cur = {k: sb(st1, f"f_cur_{k}", [P, W]) for k in "qkv"}
            f_lin = sb(st1, "f_lin", [P, 3 * W])
            f_cen = sb(st1, "f_cen", [P, 2 * W])
            f_sq = sb(st1, "f_sq", [P, 2 * W])
            f_rs = sb(st1, "f_rs", [P, 2 * W])
            f_nrm = sb(st1, "f_nrm", [P, 2 * W])
            f_kbd = sb(st1, "f_kbd", [P, XB, P])
            f_vbd = sb(st1, "f_vbd", [P, XB, P])
            f_vT = sb(st1, "f_vT", [P, XB, P])
            f_p = sb(st1, "f_p", [TA, XB * HG, TA])
            f_pT = sb(st1, "f_pT", [P, W])
            f_red = sb(st1, "f_red", [TA, XB * HG])
            f_out = [sb(st1, f"f_out{i}", [P, W]) for i in range(ITERS)]
            f_o = sb(st1, "f_o", [P, W])
            first_y = []

            def first_attention():
                last = [None]

                def step(eng, f, more=(), mark=True):
                    last[0] = Q.op(eng, f, [last[0]] + list(more))

                bank = [B_LIN]

                def flip():
                    bank[0] = B_LIN + B_CEN - bank[0]
                    return banks[bank[0]]

                step("vector", lambda e: e.bn_stats(f_stat[:, 0:6], xs[:, :]), [m_w, m_wnq])
                yield
                step("vector", lambda e: e.bn_aggr(f_stat[:, 6:8], f_stat[:, 0:6]))
                yield
                step("scalar", lambda e: e.activation(f_stat[:, 8:9], f_stat[:, 7:8], ACT.Ln, bias=eps_col[0:B * TA, :]), [m_eps])
                step("scalar", lambda e: e.activation(f_stat[:, 8:9], f_stat[:, 8:9], ACT.Exp, scale=-0.5))
                yield
                step("vector", lambda e: e.tensor_scalar(f_xn[:, :], xs[:, :], f_stat[:, 6:7], f_stat[:, 8:9],
                                                         ALU.subtract, ALU.mult))
                yield
                bk = flip()
                for h in range(HALVES):
                    step("tensor", lambda e, h=h, bk=bk: e.transpose(bk[:, h * B * TA:(h + 1) * B * TA],
                                                                    f_xn[:, h * P:(h + 1) * P], ident[0:B * TA, 0:B * TA]),
                         [m_w, m_small])
                for h in range(HALVES):
                    step("vector", lambda e, h=h, bk=bk: e.tensor_scalar(
                        f_xT[:, h, :], bk[:, h * B * TA:(h + 1) * B * TA], col(f"lna{h}"), None, ALU.mult))
                yield
                bk = flip()
                for i, k in enumerate("qkv"):
                    for o in range(HALVES):
                        at = slice(i * W + o * B * TA, i * W + (o + 1) * B * TA)
                        for h in range(HALVES):
                            m = Q.op("tensor", lambda e, k=k, o=o, h=h, at=at, bk=bk: e.matmul(
                                bk[:, at], w_in[k][:, h, o * P:(o + 1) * P], f_xT[:, h, :], start=h == 0, stop=h == 1),
                                [last[0]], mark=h == 1)
                last[0] = m
                for i, k in enumerate("qkv"):
                    for o in range(HALVES):
                        at = slice(i * W + o * B * TA, i * W + (o + 1) * B * TA)
                        dst = f_cur[k][:, o * B * TA:(o + 1) * B * TA]
                        if k == "q":
                            f = lambda e, at=at, dst=dst, o=o, bk=bk: e.tensor_scalar(dst, bk[:, at], col(f"bq{o}"), QKS,
                                                                                     ALU.add, ALU.mult)
                        elif k == "k":
                            f = lambda e, at=at, dst=dst, bk=bk: e.tensor_scalar(dst, bk[:, at], QKS, None, ALU.mult)
                        else:
                            f = lambda e, at=at, dst=dst, o=o, bk=bk: e.tensor_scalar(dst, bk[:, at], col(f"bv{o}"), None,
                                                                                     ALU.add)
                        step("vector", f)
                yield
                for it in range(ITERS):
                    src = dict(f_cur) if it == 0 else {"q": f_cur["q"], "k": f_lin[:, W:2 * W], "v": f_lin[:, 2 * W:3 * W]}
                    bk = flip()
                    for i, k in enumerate("qkv"):
                        step("tensor", lambda e, i=i, s=src[k], k=k, bk=bk: e.matmul(
                            bk[:, i * W:(i + 1) * W], wlin[k][:, :], s[:, :], start=True, stop=True), [m_blocks])
                    for i, k in enumerate("qkv"):
                        step("vector", lambda e, i=i, k=k, bk=bk: e.tensor_scalar(
                            f_lin[:, i * W:(i + 1) * W], bk[:, i * W:(i + 1) * W], col("bl" + k), None, ALU.add))
                    yield
                    bk = flip()
                    step("tensor", lambda e, bk=bk: e.matmul(bk[:, 0:2 * W], center, f_lin[:, 0:2 * W], start=True, stop=True))
                    step("vector", lambda e, bk=bk: e.tensor_copy(f_cen[:, :], bk[:, 0:2 * W]))
                    step("vector", lambda e: e.tensor_tensor(f_sq[:, :], f_cen[:, :], f_cen[:, :], ALU.mult))
                    yield
                    bk = flip()
                    step("tensor", lambda e, bk=bk: e.matmul(bk[:, 0:2 * W], bmean, f_sq[:, :], start=True, stop=True))
                    step("scalar", lambda e, bk=bk: e.activation(f_rs[:, :], bk[:, 0:2 * W], ACT.Ln, bias=eps_col[:, :]))
                    step("scalar", lambda e: e.activation(f_rs[:, :], f_rs[:, :], ACT.Exp, scale=-0.5))
                    yield
                    for i, w in ((0, wnq[:, it:it + 1]), (1, col("lnd"))):
                        step("vector", lambda e, i=i, w=w: e.scalar_tensor_tensor(
                            f_nrm[:, i * W:(i + 1) * W], f_cen[:, i * W:(i + 1) * W], w, f_rs[:, i * W:(i + 1) * W],
                            ALU.mult, ALU.mult))
                    for dst, s0 in ((f_kbd, f_nrm[:, W:2 * W]), (f_vbd, f_lin[:, 2 * W:3 * W])):
                        for x in range(XB):
                            step("vector", lambda e, dst=dst, s0=s0, x=x: e.tensor_tensor(
                                dst[:, x, :].rearrange("p (h t) -> p h t", h=HG),
                                s0[:, x * TA:(x + 1) * TA].unsqueeze(1).to_broadcast([P, HG, TA]),
                                same.rearrange("p (h t) -> p h t", h=HG), ALU.mult))
                        yield
                    bk = flip()
                    for x in range(XB):
                        step("tensor", lambda e, x=x, bk=bk: e.matmul(
                            bk[0:TA, x * P:(x + 1) * P], f_nrm[:, x * TA:(x + 1) * TA], f_kbd[:, x, :],
                            start=True, stop=True))
                    s3 = bk[0:TA, :].rearrange("p (x t) -> p x t", t=TA)

                    def bc(v):
                        return v[:, :].unsqueeze(2).to_broadcast([TA, XB * HG, TA])
                    step("vector", lambda e, s3=s3: e.tensor_reduce(f_red[:, :], s3, AX_X, ALU.max))
                    step("vector", lambda e, s3=s3, bc=bc: e.tensor_tensor(f_p[:, :, :], s3, bc(f_red), ALU.subtract))
                    yield
                    step("scalar", lambda e: e.activation(f_p[:, :, :], f_p[:, :, :], ACT.Exp))
                    step("vector", lambda e: e.tensor_reduce(f_red[:, :], f_p[:, :, :], AX_X, ALU.add))
                    step("vector", lambda e: e.reciprocal(f_red[:, :], f_red[:, :]))
                    step("vector", lambda e, bc=bc: e.tensor_tensor(f_p[:, :, :], f_p[:, :, :], bc(f_red), ALU.mult))
                    yield
                    bk = flip()
                    for x in range(XB):
                        step("tensor", lambda e, x=x, bk=bk: e.transpose(
                            bk[:, x * TA:(x + 1) * TA], f_p[:, x * HG:(x + 1) * HG, :].rearrange("p h t -> p (h t)"),
                            ident[0:TA, 0:TA]))
                    step("vector", lambda e, bk=bk: e.tensor_copy(f_pT[:, :], bk[:, 0:W]))
                    yield
                    bk = flip()
                    for x in range(XB):
                        step("tensor", lambda e, x=x, bk=bk: e.transpose(bk[:, x * P:(x + 1) * P], f_vbd[:, x, :], ident))
                    step("vector", lambda e, bk=bk: e.tensor_copy(f_vT[:, :, :], bk.rearrange("p (x f) -> p x f", x=XB)))
                    yield
                    bk = flip()
                    for x in range(XB):
                        step("tensor", lambda e, x=x, bk=bk: e.matmul(
                            bk[:, x * TA:(x + 1) * TA], f_vT[:, x, :], f_pT[:, x * TA:(x + 1) * TA], start=True, stop=True))
                    step("vector", lambda e, it=it, bk=bk: e.tensor_copy(f_out[it][:, :], bk[:, 0:W]))
                    step("vector", lambda e, it=it: e.tensor_tensor(f_cur["q"][:, :], f_cur["q"][:, :], f_out[it][:, :],
                                                                   ALU.add))
                    yield
                dsum, dlim, dflag, nflag = (flag[:, i:i + 1] for i in range(4))
                step("vector", lambda e: e.tensor_tensor(f_sq[:, 0:W], f_out[1][:, :], f_out[0][:, :], ALU.subtract))
                step("vector", lambda e: e.tensor_reduce(diff_cols[:, :], f_sq[:, 0:W], AX_X, ALU.add,
                                                         apply_absolute_value=True))
                bk = flip()
                step("tensor", lambda e, bk=bk: e.matmul(bk[:, 0:1], ones, diff_cols[:, :], start=True, stop=True))
                step("vector", lambda e, bk=bk: e.tensor_scalar(dsum, bk[:, 0:1], 1.0 / (N * D), None, ALU.mult))
                step("vector", lambda e: e.scalar_tensor_tensor(dlim, dsum, col("fac"), col("thr"), ALU.mult, ALU.add))
                step("vector", lambda e: e.tensor_tensor(dflag, dsum, dlim, ALU.is_lt))
                step("vector", lambda e: e.tensor_scalar(nflag, dflag, -1.0, 1.0, ALU.mult, ALU.add))
                step("vector", lambda e: e.tensor_scalar(f_o[:, :], f_out[1][:, :], dflag, None, ALU.mult))
                step("vector", lambda e: e.scalar_tensor_tensor(f_o[:, :], f_out[2][:, :], nflag, f_o[:, :],
                                                                ALU.mult, ALU.add))
                yield
                bk = flip()
                for b in range(B):
                    for h in range(HALVES):
                        at = slice((h * B + b) * TA, (h * B + b + 1) * TA)
                        m = Q.op("tensor", lambda e, b=b, h=h, at=at, bk=bk: e.matmul(
                            bk[0:TA, b * D:(b + 1) * D], f_o[:, at], w_in["o"][:, h, :], start=h == 0, stop=h == 1),
                            [last[0]], mark=h == 1)
                last[0] = m
                step("vector", lambda e, bk=bk: e.tensor_copy(y_first[:, :, :], bk[0:TA, :].rearrange("p (b d) -> p b d", b=B)))
                first_y.append(last[0])
                yield

            xr = [sb(st1, f"xr{i}", [P, TPC, D]) for i in range(3)]
            x1t = [sb(st1, f"x1t{i}", [P, TPC, D]) for i in range(2)]
            hno = [sb(st1, f"hno{i}", [P, TPC, D]) for i in range(2)]
            hT = [sb(st1, f"hT{i}", [P, HALVES, CH]) for i in range(2)]
            stt = [sb(st1, f"st1_{i}", [P, TPC, 9]) for i in range(4)]
            sp = [[sb(st1, f"sp{i}{n}", [P, CH], BF16) for n in ("hi", "mid", "lo")] + [sb(st1, f"sp{i}rem", [P, CH])]
                  for i in range(2)]
            ld, x1m, hm, htm, mm_h, st_x1 = {}, {}, {}, {}, {}, {}
            spn, sp_free = [0], [[], []]

            def mid_load(i):
                c = ORDER[i]
                ld[i] = Q.dma("mid_in", xr[i % 3][:, :, :], a["x"][c * CH:(c + 1) * CH, :].rearrange("(j p) d -> p j d", p=P),
                              [x1m.get(i - 3)])

            def mid_a(i):
                c, r = ORDER[i], i % 2
                x = xr[i % 3]
                m = Q.op("gpsimd", lambda e: e.tensor_tensor(x[:, :, :], x[:, :, :], bo4[:, :, :], ALU.add), [ld[i], m_w])
                if c % CPB == 0:
                    b = c // CPB
                    m = Q.op("vector", lambda e: e.tensor_tensor(x[0:TA, 0, :], x[0:TA, 0, :], y_first[:, b, :], ALU.add),
                             [m, first_y[0]])
                x1m[i] = yield from norm4(stt[r], x, x1t[r], [m], [st_x1.get(i - 2), hm.get(i - 2)])
                st_x1[i] = Q.dma("x1_out", x1_d[c * CH:(c + 1) * CH, :].rearrange("(j p) d -> p j d", p=P),
                                 x1t[r][:, :, :], [x1m[i]])
                yield
                hm[i] = yield from norm4(stt[2 + r], x1t[r], hno[r], [x1m[i]], [htm.get(i - 2)])

            def mid_b(i):
                c, r = ORDER[i], i % 2
                b, cc = c // CPB, c % CPB
                at = slice(cc * CH, (cc + 1) * CH)
                htm[i] = transpose4(hno[r], [hT[r][:, h, :] for h in range(HALVES)], 0,
                                    [col("g1_0"), col("g1_1")], [col("c1_0"), col("c1_1")], [hm[i]], [mm_h.get(i - 2)])
                yield
                for kind, o0 in (("q", 0), ("k", D)):
                    for o in range(HALVES):
                        k = spn[0] % 2
                        bk = 2 + k
                        spn[0] += 1
                        for h in range(HALVES):
                            m = Q.op("tensor", lambda e, h=h, o=o, o0=o0, bk=bk: e.matmul(
                                banks[bk][:, :], wqkv[:, h, o0 + o * P:o0 + (o + 1) * P], hT[r][:, h, :],
                                start=h == 0, stop=h == 1), [htm[i], m_w, bank_free[bk]], mark=h == 1)
                        sc = SM if kind == "q" else 1.0
                        hi, mid, lo, rem = sp[k]
                        g = b * HALVES + o
                        m1 = Q.op("scalar", lambda e, hi=hi, bk=bk, sc=sc: e.activation(
                            hi[:, :], banks[bk][:, :], ACT.Identity, scale=sc), [m] + sp_free[k])
                        m2 = Q.op("vector", lambda e, hi=hi, rem=rem, bk=bk, sc=sc: e.scalar_tensor_tensor(
                            rem[:, :], banks[bk][:, :], sc, hi[:, :], ALU.mult, ALU.subtract), [m1])
                        bank_free[bk] = m2
                        m3 = Q.op("vector", lambda e, mid=mid, rem=rem: e.tensor_copy(mid[:, :], rem[:, :]),
                                  [m2] + sp_free[k])
                        m4 = Q.op("vector", lambda e, mid=mid, rem=rem, lo=lo: e.tensor_tensor(
                            lo[:, :], rem[:, :], mid[:, :], ALU.subtract), [m3])
                        sp_free[k] = [Q.dma("parts_out", parts[g][kind][n, :, at], t[:, :], [mm])
                                      for n, (t, mm) in enumerate(((hi, m1), (mid, m3), (lo, m4)))]
                        parts_stored.setdefault(g, []).extend(sp_free[k])
                        yield
                for j in range(TPC):
                    bk = 4 + j // 2
                    for h in range(HALVES):
                        m = Q.op("tensor", lambda e, j=j, h=h, bk=bk: e.matmul(
                            banks[bk][:, (j % 2) * D:(j % 2 + 1) * D], hT[r][:, h, j * P:(j + 1) * P],
                            wqkv[:, h, 2 * D:3 * D], start=h == 0, stop=h == 1), [htm[i], bank_free[bk]], mark=h == 1)
                    if j % 2 == 0:
                        continue
                    for jj in (j - 1, j):
                        for o in range(HALVES):
                            bank_free[bk] = Q.op("scalar", lambda e, j=jj, o=o, bk=bk, kt=cc * TPC + jj: e.activation(
                                v_tok[:, b * HALVES + o, kt, :, 0:HD],
                                banks[bk][:, (j % 2) * D + o * P:(j % 2) * D + (o + 1) * P].rearrange(
                                    "p (h d) -> p h d", h=HG), ACT.Identity), [m, m_ones_v])
                            v_ready[b * HALVES + o] = bank_free[bk]
                    yield
                mm_h[i] = m

            chain = first_attention()
            for i in range(3):
                mid_load(i)
            for _ in mid_a(0):
                pass
            for i in range(NC):
                if i + 1 < NC and ORDER[i + 1] % CPB == 0:
                    for _ in chain:
                        pass
                for _ in in_turn(mid_b(i), *([mid_a(i + 1)] if i + 1 < NC else [])):
                    next(chain, None)
                if i + 3 < NC:
                    mid_load(i + 3)
            mid_end = [(s, s.n) for s in Q.done.values()] + [x for f in sp_free for x in f] + [st_x1[NC - 1], st_x1[NC - 2]]

        def attention(bufs, heads, fillers, on_assembled, start):
            LEAD = 4
            AHEAD = KT + LEAD
            S_BANKS, T_BANKS, PV, MISC = ((0, 1), (2, 3)), (4, 5), 6, 7
            n_heads = len(heads)
            reduced = [None, None]
            s_at, t_at = [0], [0]
            t_marks = [None, None]
            stack_mark, nmax_mark, s_last, t_last = {}, {}, {}, {}
            pv_mark, exp_mark = {}, {}
            max_marks = {}
            oev_dma = {}

            def load_stack(n):
                inst, hh = heads[n]
                sl = n % 3
                sig = bufs["stack_sig"][sl]
                waits = [t_last.get(n - 3), s_last.get(n - 3)] + list(parts_stored[inst])
                for j in range(6):
                    rows = slice(hh * HD, (hh + 1) * HD)
                    dst = slice(j * HD, (j + 1) * HD)
                    Q.dma_on(sig, bufs["qst"][sl][dst, :], parts[inst]["q"][Q_PARTS[j], rows, :], waits)
                    stack_mark[n] = Q.dma_on(sig, bufs["kst"][sl][dst, :], parts[inst]["k"][K_PARTS[j], rows, :], waits)

            def scores(n, qt):
                sl, tiles = n % 3, qt + 1
                first = tiles if tiles * P <= 2 * CH else (tiles + 1) // 2
                mx = bufs["mx"][n % 2]
                for half in range(2):
                    w, start_key = (first * P, 0) if half == 0 else ((tiles - first) * P, first * P)
                    if w == 0:
                        continue
                    buf = s_at[0] % 2
                    s_at[0] += 1
                    m = None
                    for i in range((w + CH - 1) // CH):
                        k0 = start_key + i * CH
                        kw = min(CH, start_key + w - k0)
                        bk = S_BANKS[buf][i]
                        diag = k0 <= qt * P < k0 + kw
                        last = i == (w + CH - 1) // CH - 1
                        m = Q.op("tensor", lambda e, bk=bk, k0=k0, kw=kw, diag=diag: e.matmul(
                            banks[bk][:, 0:kw], bufs["qst"][sl][0:STACK, qt * P:(qt + 1) * P],
                            bufs["kst"][sl][0:STACK, k0:k0 + kw], start=True, stop=not diag),
                            [reduced[buf], stack_mark[n]] + start, mark=last and not diag)
                        if diag:
                            off = qt * P - k0
                            m = Q.op("tensor", lambda e, bk=bk, off=off: e.matmul(
                                banks[bk][:, off:off + P], ident_bf[:, :], mask_s_bf[:, :], start=False, stop=True),
                                [m_c], mark=last)
                    s_last[n] = m
                    src = (bufs["s_wide"][buf][:, 0:w])
                    reduced[buf] = Q.op("vector", lambda e, src=src, qt=qt, half=half: e.tensor_reduce(
                        mx[:, qt, half:half + 1], src, AX_X, ALU.max), [m, max_marks.get(n - 2), bufs["ones_mark"]])

            def combine_max(n):
                mx, mf = bufs["mx"][n % 2], bufs["mf"]
                max_marks[n] = Q.op("vector", lambda e: e.tensor_reduce(mf[:, :], mx[:, :, :], AX_X, ALU.max),
                                    [reduced[0], reduced[1], bank_free[MISC]])

            def turn_max(n):
                mf, nm, rem, mp = bufs["mf"], bufs["nm"], bufs["nm_rem"], bufs["nm_parts"][n % 2]
                m = Q.op("tensor", lambda e: e.transpose(banks[MISC][0:KT, 0:P], mf[:, :], ident),
                         [max_marks[n], bank_free[MISC]])
                v0 = Q.op("scalar", lambda e: e.activation(nm[:, :], banks[MISC][0:KT, 0:P], ACT.Identity, scale=-1.0),
                          [m, bufs.get("nm_free")])
                bank_free[MISC] = v0
                v1 = Q.op("gpsimd", lambda e: e.tensor_copy(mp[:, 0, :], nm[:, :]), [v0, nmax_mark.get(n - 2)])
                v2 = Q.op("gpsimd", lambda e: e.tensor_tensor(rem[:, :], nm[:, :], mp[:, 0, :], ALU.subtract), [v1])
                v3 = Q.op("gpsimd", lambda e: e.tensor_copy(mp[:, 1, :], rem[:, :]), [v2])
                v4 = Q.op("gpsimd", lambda e: e.tensor_tensor(mp[:, 2, :], rem[:, :], mp[:, 1, :], ALU.subtract), [v3])
                bufs["nm_free"] = v4
                sl = n % 3
                for i in range(3):
                    nmax_mark[n] = Q.dma_on(bufs["nmax_sig"][sl], bufs["qst"][sl][STACK + i:STACK + i + 1, :].rearrange(
                        "p (q t) -> p q t", q=KT), mp[:, i, :], [v4, t_last.get(n - 3)])

            def chunks(kt):
                c0 = kt * P // CH
                return [(c, kt * P - c0 * CH if c == c0 else 0) for c in range(c0, CPB)]

            def scores_t(t, c, off):
                n, kt = t // KT, t % KT
                sl, r = n % 3, t_at[0] % 2
                bk = T_BANKS[r]
                t_at[0] += 1
                diag = kt * P // CH == c
                m = Q.op("tensor", lambda e: e.matmul(
                    banks[bk][:, off:CH], bufs["kst"][sl][0:ROWS, kt * P:(kt + 1) * P],
                    bufs["qst"][sl][0:ROWS, c * CH + off:(c + 1) * CH], start=True, stop=not diag),
                    [t_marks[r], nmax_mark[n], bufs["ones_mark"]], mark=not diag)
                if diag:
                    m = Q.op("tensor", lambda e: e.matmul(banks[bk][:, off:off + P], ident_bf[:, :], mask_t_bf[:, :],
                                                         start=False, stop=True), [m_c])
                t_last[n] = m
                t_marks[r] = Q.op("scalar", lambda e: e.activation(
                    bufs["p"][t % 3][:, c * CH + off:(c + 1) * CH], banks[bk][:, off:CH], ACT.Exp),
                    [m, pv_mark.get(t - 3)])
                exp_mark[t] = t_marks[r]

            def values(t):
                n, kt = t // KT, t % KT
                g, hh = heads[n]
                for r in range(CPB):
                    m0 = max(0, -((r - kt) // CPB))
                    if m0 >= KT // CPB:
                        continue
                    mov = bufs["p"][t % 3][:, :].rearrange("p (m r i) -> p r m i", r=CPB, i=P)[:, r, m0:, :]
                    m = Q.op("tensor", lambda e, r=r, m0=m0, mov=mov: e.matmul(
                        banks[PV][r * VW:(r + 1) * VW, m0 * P:CH], v_tok[:, g, kt, hh, :], mov,
                        start=kt == 0, stop=kt == KT - CPB + r),
                        [exp_mark[t], v_ready[g], bank_free[PV] if kt == 0 else None], mark=r == CPB - 1)
                pv_mark[t] = m

            def evacuate(n):
                inst, hh = heads[n]
                o = bufs["oev"][n % 2]
                bank_free[PV] = Q.op("scalar", lambda e: e.activation(o[:, :], banks[PV][:, :], ACT.Identity),
                                     [pv_mark[n * KT + KT - 1]] + list(oev_dma.get(n - 2, ())))
                marks = []
                rows = slice(hh * HD, (hh + 1) * HD)
                for r in range(CPB):
                    for buf, r0 in (("num", r * VW), ("den", r * VW + HD)):
                        dst = bufs[buf][inst % 2][rows, :].rearrange("p (m r i) -> p r m i", r=CPB, i=P)[:, r, :, :]
                        marks.append(Q.dma("assemble", dst, o[r0:r0 + HD, :].rearrange("p (m i) -> p m i", i=P),
                                           [bank_free[PV]] + list(asm_free.get(inst - 2, ())), depth=12))
                oev_dma[n] = marks
                on_assembled.setdefault(inst, []).extend(marks)

            last_t = n_heads * KT
            for t in range(-2 * KT, last_t + 1):
                if t % KT == 0 and 0 <= t // KT + 2 < n_heads:
                    load_stack(t // KT + 2)
                s = t + AHEAD
                todo = chunks(t % KT) if 0 <= t < last_t else []
                for c, off in todo[:2]:
                    scores_t(t, c, off)
                s_ok = 0 <= s < n_heads * KT
                if s_ok:
                    scores(s // KT, t % KT)
                for c, off in todo[2:]:
                    scores_t(t, c, off)
                if 0 <= t - 1 < last_t:
                    values(t - 1)
                    if (t - 1) % KT == KT - 1:
                        evacuate((t - 1) // KT)
                if s_ok and s % KT == KT - 1:
                    combine_max(s // KT)
                if 0 <= s - 1 < n_heads * KT and (s - 1) % KT == KT - 1:
                    turn_max((s - 1) // KT)
                for f in fillers.get(t, ()):
                    f()
            for extra in sorted(k for k in fillers if k > last_t):
                for f in fillers[extra]:
                    f()

        Q.phase("attn")
        w3_in = Signal(sem("w3_in"))
        Q.dma_on(w3_in, wo2[:, :, :], a["w_o"].rearrange("(h p) o -> p h o", p=P))
        Q.dma_on(w3_in, wg[:, :, :], a["w_gate"].rearrange("(h p) o -> p h o", p=P))
        Q.dma_on(w3_in, rc[:, :], a["routes"])
        Q.dma_on(w3_in, b2_sb[:, :, :], a["b2"])
        m_w3 = Q.dma_on(w3_in, b1_sb[:, :, :], a["b1"].rearrange("p (e f) -> p e f", e=E_))
        att = ExitStack()
        bufs = {
            "stack_sig": [Signal(sem(f"stack_in{i}")) for i in range(3)],
            "nmax_sig": [Signal(sem(f"nmax_in{i}")) for i in range(3)],
            "num": num, "den": den,
            "s_wide": [psum[:, 2 * i * CH:2 * (i + 1) * CH] for i in range(2)],
        }
        for name, shape, dt, cnt in (("qst", [P, T], BF16, 3), ("kst", [P, T], BF16, 3), ("p", [P, T], F32, 3),
                                     ("oev", [P, CH], F32, 2),
                                     ("mx", [P, KT, 2], F32, 2), ("nm_parts", [KT, 3, P], BF16, 2)):
            bufs[name] = [sb(att, f"{name}{i}", shape, dt) for i in range(cnt)]
        for name, shape in (("mf", [P, KT]), ("nm", [KT, P]), ("nm_rem", [KT, P])):
            bufs[name] = sb(att, name, shape)
        for sl in range(3):
            Q.op("vector", lambda e, sl=sl: e.memset(bufs["kst"][sl][STACK:ROWS, :], 1.0), mid_end)
        for i in range(2):
            m_o = Q.op("vector", lambda e, i=i: e.memset(bufs["mx"][i][:, :, :], NEG))
        bufs["ones_mark"] = m_o
        for g in parts_stored:
            parts_stored[g] = parts_stored[g] + mid_end
        assembled, asm_free, o_stored = {}, {}, {}

        def fin_stages(g):
            n_, d_ = num[g % 2], den[g % 2]
            asm_free[g] = []
            stages = []
            for cc in range(CPB):
                at = slice(cc * CH, (cc + 1) * CH)
                for j in range(TPC):
                    def rec(cc=cc, j=j):
                        p = slice(cc * CH + j * P, cc * CH + (j + 1) * P)
                        Q.op("vector", lambda e: e.reciprocal(d_[:, p], d_[:, p]), assembled[g], mark=j == TPC - 1)
                    stages.append(rec)

                def mul(cc=cc, at=at):
                    m = Q.op("gpsimd", lambda e: e.tensor_tensor(n_[:, at], n_[:, at], d_[:, at], ALU.mult),
                             [(Q.done["vector"], Q.done["vector"].n)])
                    o_stored[g, cc] = Q.dma("o_out", o_ffn[g, :, at], n_[:, at], [m])
                    asm_free[g].append(o_stored[g, cc])
                stages.append(mul)
            return stages

        fillers = {}
        for g in range(NG - 1):
            for i, f in enumerate(fin_stages(g)):
                fillers.setdefault(HG * KT * (g + 1) + 2 + i, []).append(f)
        attention(bufs, [(g, hh) for g in range(NG) for hh in range(HG)], fillers, assembled, mid_end)
        last_fin = iter(fin_stages(NG - 1))
        att2_end = [(s, s.n) for s in Q.done.values()] + [x for v in asm_free.values() for x in v]
        att.close()

        Q.phase("gate")
        v_stack.close()
        xn_d = dram("xn_d", [N, D])
        y_d = dram("y_d", [2 * N + P, D])
        acc = sb(ctx, "acc", [P, NC, TPC, D])
        gate_w = sb(ctx, "gate_w", [P, NT, 2])
        from_u = sb(ctx, "from_u", [P, E_ * NT], U32)
        to_u = sb(ctx, "to_u", [P, E_ * NT], U32)
        counts_i = sb(ctx, "counts_i", [P, E_], I32)
        w1s = [sb(ctx, f"w1s{i}", [P, HALVES, F_]) for i in range(2)]
        w2s = [sb(ctx, f"w2s{i}", [P, FT, D]) for i in range(2)]
        w_sig = [Signal(sem(f"expert_in{i}")) for i in range(2)]
        settled = {e: Signal(sem(f"settled_{e}")) for e in ("tensor", "vector", "gpsimd")}
        w_mark = {}

        def load_expert(e_, waits):
            i = e_ % 2
            Q.dma_on(w_sig[i], w1s[i][:, :, :], a["w1"][e_].rearrange("(h p) f -> p h f", p=P), waits)
            w_mark[e_] = Q.dma_on(w_sig[i], w2s[i][:, :, :], a["w2"][e_].rearrange("(f p) d -> p f d", p=P), waits)

        with ExitStack() as st3:
            before = rc[:, 0:P]
            iota = rc[:, P:P + E_ * NT]
            row1 = rc[:, P + E_ * NT:P + (E_ + 2) * NT]
            slot0 = rc[:, P + (E_ + 2) * NT:P + (E_ + 2) * NT + E_]
            rank8 = rc[:, P + (E_ + 2) * NT + E_:P + (E_ + 2) * NT + 2 * E_]
            spare1 = rc[:, P + (E_ + 2) * NT + 2 * E_:]
            oin = [[sb(st3, f"of{r}{h}", [P, CH]) for h in range(HALVES)] for r in range(3)]
            x1r = [sb(st3, f"x1r{i}", [P, TPC, D]) for i in range(3)]
            res = [sb(st3, f"res{i}", [P, TPC, D]) for i in range(2)]
            xno = [sb(st3, f"xno{i}", [P, TPC, D]) for i in range(2)]
            xfT = [sb(st3, f"xfT{i}", [P, HALVES, CH]) for i in range(2)]
            stg = [sb(st3, f"stg{i}", [P, TPC, 9]) for i in range(2)]
            ld, xn_m, tr_m, mm_o, acc_m, st_xn, lg_ev, mm_lg = {}, {}, {}, {}, {}, {}, {}, {}

            def g_load(c):
                b, cc, r = c // CPB, c % CPB, c % 3
                at = slice(cc * CH, (cc + 1) * CH)
                ms = [Q.dma("mid_in", oin[r][h][:, :], o_ffn[b * HALVES + h, :, at],
                            [mm_o.get(c - 3), o_stored[b * HALVES + h, cc]] + att2_end) for h in range(HALVES)]
                ms.append(Q.dma("mid_in", x1r[r][:, :, :], x1_d[c * CH:(c + 1) * CH, :].rearrange("(j p) d -> p j d", p=P),
                                [acc_m.get(c - 3)] + att2_end))
                ld[c] = ms

            def g_a(c):
                r = c % 2
                for j in range(TPC):
                    bk = j // 2
                    for h in range(HALVES):
                        m = Q.op("tensor", lambda e, j=j, h=h, bk=bk: e.matmul(
                            banks[bk][:, (j % 2) * D:(j % 2 + 1) * D], oin[c % 3][h][:, j * P:(j + 1) * P], wo2[:, h, :],
                            start=h == 0, stop=h == 1), ld[c] + [m_w3, bank_free[bk]], mark=h == 1)
                    if j % 2 == 1:
                        m1 = Q.op("vector", lambda e, bk=bk, j=j: e.tensor_tensor(
                            res[r][:, j - 1:j + 1, :], banks[bk][:, :].rearrange("p (j d) -> p j d", j=2),
                            x1r[c % 3][:, j - 1:j + 1, :], ALU.add), [m, xn_m.get(c - 2), acc_m.get(c - 2)] + ld[c])
                        bank_free[bk] = m1
                mm_o[c] = m
                yield
                acc_m[c] = Q.op("gpsimd", lambda e: e.tensor_tensor(acc[:, c, :, :], res[r][:, :, :], x1r[c % 3][:, :, :],
                                                                   ALU.add), [m1])
                xn_m[c] = yield from norm4(stg[r], res[r], xno[r], [m1], [tr_m.get(c - 2), st_xn.get(c - 2)])
                st_xn[c] = Q.dma("x1_out", xn_d[c * CH:(c + 1) * CH, :].rearrange("(j p) d -> p j d", p=P),
                                 xno[r][:, :, :], [xn_m[c]])

            B_LG, B_TABLE, B_RANK = 4, 5, 6
            lg = sb(st3, "lg", [P, NT, E_])

            def g_b(c):
                r = c % 2
                tr_m[c] = transpose4(xno[r], [xfT[r][:, h, :] for h in range(HALVES)], 2,
                                     [col("g2_0"), col("g2_1")], [col("c2_0"), col("c2_1")], [xn_m[c]], [mm_lg.get(c - 2)])
                yield
                for j in range(TPC):
                    for h in range(HALVES):
                        m = Q.op("tensor", lambda e, j=j, h=h: e.matmul(
                            banks[B_LG][:, j * E_:(j + 1) * E_], xfT[r][:, h, j * P:(j + 1) * P], wg[:, h, :],
                            start=h == 0, stop=h == 1), [tr_m[c], bank_free[B_LG]], mark=h == 1)
                mm_lg[c] = m
                yield
                bank_free[B_LG] = lg_ev[c] = Q.op("vector", lambda e: e.tensor_copy(
                    lg[:, c * TPC:(c + 1) * TPC, :], banks[B_LG][:, 0:TPC * E_].rearrange("p (t e) -> p t e", e=E_)), [m])

            RC = 2
            RT = RC * TPC
            one = sb(st3, "g_one", [P, RT])
            t1, hot1, hot2, sel, pos, tot_a, tot_b = (
                sb(st3, f"g_{n}", [P, RT, E_]) for n in ("t1", "hot1", "hot2", "sel", "pos", "tot_a", "tot_b"))
            base = sb(st3, "g_base", [P, E_])
            slot_f = sb(st3, "g_slot_f", [P, RT, 2])
            slot_i, lo_i, hi_i = (sb(st3, f"g_{n}", [P, RT, 2], I32) for n in ("slot_i", "lo_i", "hi_i"))
            lo_f, hi_f = (sb(st3, f"g_{n}", [P, RT, 2]) for n in ("lo_f", "hi_f"))
            RING = 4
            at_lo = [sb(st3, f"at_lo{i}", [P, P]) for i in range(RING)]
            at_hi = [sb(st3, f"at_hi{i}", [P, E_ * NT]) for i in range(RING)]
            put = {}

            def bc(x):
                return x.unsqueeze(2).to_broadcast([P, RT, E_])

            def dve(f, waits=()):
                return Q.op("vector", f, [(Q.done["vector"], Q.done["vector"].n)] + list(waits))

            def pick(src, w, hot):
                dve(lambda e: e.tensor_reduce(w, src, AX_X, ALU.max))
                dve(lambda e: e.tensor_tensor(hot[:, :, :], src, bc(w), ALU.is_equal))
                dve(lambda e: e.tensor_tensor(hot[:, :, :], hot[:, :, :], rank_rt, ALU.mult))
                dve(lambda e: e.tensor_reduce(one[:, :], hot[:, :, :], AX_X, ALU.max))
                dve(lambda e: e.tensor_tensor(hot[:, :, :], rank_rt, bc(one[:, :]), ALU.is_equal))

            rank_rt = rank8.unsqueeze(1).to_broadcast([P, RT, E_])

            def g_route(b):
                tiles = slice(b * RT, (b + 1) * RT)
                g = lg[:, tiles, :]
                if b == 0:
                    dve(lambda e: e.tensor_copy(base[:, :], slot0), [m_w3])
                dve(lambda e: e.tensor_reduce(one[:, :], g, AX_X, ALU.max), [lg_ev[(b + 1) * RC - 1]])
                m = dve(lambda e: e.tensor_tensor(g, g, bc(one[:, :]), ALU.subtract))
                m = Q.op("scalar", lambda e: e.activation(g, g, ACT.Exp), [m])
                yield
                dve(lambda e: e.tensor_reduce(one[:, :], g, AX_X, ALU.add), [m])
                dve(lambda e: e.reciprocal(one[:, :], one[:, :]))
                dve(lambda e: e.tensor_tensor(g, g, bc(one[:, :]), ALU.mult))
                w1_, w2_ = gate_w[:, tiles, 0], gate_w[:, tiles, 1]
                pick(g, w1_, hot1)
                dve(lambda e: e.scalar_tensor_tensor(t1[:, :, :], hot1[:, :, :], -2.0, g, ALU.mult, ALU.add))
                pick(t1[:, :, :], w2_, hot2)
                m_sel = dve(lambda e: e.tensor_tensor(sel[:, :, :], hot1[:, :, :], hot2[:, :, :], ALU.add))
                s2 = sel[:, :, :].rearrange("p t e -> p (t e)")
                w = RT * E_
                Q.op("tensor", lambda e: e.matmul(banks[B_RANK][:, 0:w], before, s2, start=True, stop=True),
                     [m_sel, bank_free[B_RANK]], mark=False)
                m_pre = Q.op("tensor", lambda e: e.matmul(banks[B_RANK][:, w:2 * w], ones, s2, start=True, stop=True))
                dve(lambda e: e.tensor_tensor(one[:, :], w1_, w2_, ALU.add))
                dve(lambda e: e.reciprocal(one[:, :], one[:, :]))
                dve(lambda e: e.tensor_tensor(w1_, w1_, one[:, :], ALU.mult))
                dve(lambda e: e.tensor_tensor(w2_, w2_, one[:, :], ALU.mult))
                yield
                tot3 = banks[B_RANK][:, w:2 * w].rearrange("p (t e) -> p t e", e=E_)
                dve(lambda e: e.tensor_copy(tot_a[:, :, :], tot3), [m_pre])
                cur, nxt, step = tot_a, tot_b, 1
                while step < RT:
                    dve(lambda e, x=cur, y=nxt, s=step: e.tensor_copy(y[:, 0:s, :], x[:, 0:s, :]))
                    dve(lambda e, x=cur, y=nxt, s=step: e.tensor_tensor(y[:, s:, :], x[:, s:, :], x[:, 0:RT - s, :], ALU.add))
                    cur, nxt, step = nxt, cur, 2 * step
                base3 = base[:, :].unsqueeze(1).to_broadcast([P, RT, E_])
                rank3 = banks[B_RANK][:, 0:w].rearrange("p (t e) -> p t e", e=E_)
                dve(lambda e: e.tensor_tensor(pos[:, :, :], rank3, base3, ALU.add))
                bank_free[B_RANK] = dve(lambda e: e.tensor_tensor(pos[:, 1:, :], pos[:, 1:, :], cur[:, 0:RT - 1, :], ALU.add))
                dve(lambda e: e.tensor_tensor(base[:, :], base[:, :], cur[:, RT - 1, :], ALU.add))
                for k, hot in ((0, hot1), (1, hot2)):
                    dve(lambda e, hot=hot: e.tensor_tensor(t1[:, :, :], hot[:, :, :], pos[:, :, :], ALU.mult))
                    dve(lambda e, k=k: e.tensor_reduce(slot_f[:, :, k], t1[:, :, :], AX_X, ALU.add))
                dve(lambda e: e.tensor_copy(slot_i[:, :, :], slot_f[:, :, :]))
                dve(lambda e: e.tensor_scalar(lo_i[:, :, :], slot_i[:, :, :], P - 1, None, ALU.bitwise_and))
                dve(lambda e: e.tensor_scalar(hi_i[:, :, :], slot_i[:, :, :], 7, None, ALU.logical_shift_right))
                dve(lambda e: e.tensor_copy(lo_f[:, :, :], lo_i[:, :, :]), [put.get(2 * b * RT - 1)])
                m_lh = dve(lambda e: e.tensor_copy(hi_f[:, :, :], hi_i[:, :, :]))
                yield
                for j in range(RT):
                    for k in range(2):
                        n = (b * RT + j) * 2 + k
                        r = n % RING
                        m0 = Q.op("gpsimd", lambda e, j=j, k=k, r=r: e.tensor_scalar(
                            at_lo[r][:, :], iota[:, 0:P], lo_f[:, j, k:k + 1], None, ALU.is_equal),
                            [m_lh, put.get(n - RING)])
                        m = Q.op("vector", lambda e, j=j, k=k, r=r, n=n: e.tensor_scalar(
                            at_hi[r][:, :], iota, hi_f[:, j, k:k + 1], row1[:, n:n + 1], ALU.is_equal, ALU.mult),
                            [m_lh, put.get(n - RING)])
                        put[n] = Q.op("tensor", lambda e, n=n, r=r: e.matmul(
                            banks[B_TABLE][:, 0:E_ * NT], at_lo[r][:, :], at_hi[r][:, :], start=n == 0,
                            stop=n == 2 * NT - 1), [m0, m, bank_free[B_TABLE] if n == 0 else None])
                    if j % TPC == TPC - 1:
                        yield

            for c in range(3):
                g_load(c)
            load_expert(0, att2_end)
            load_expert(1, att2_end)
            for _ in g_a(0):
                pass
            routing = iter(())
            for c in range(NC):
                works = [g_b(c)] + ([g_a(c + 1)] if c + 1 < NC else [])
                for _ in in_turn(*works, routing):
                    for _ in range(2):
                        for f in (next(last_fin, None),):
                            if f is not None:
                                f()
                if c == 0:
                    for f in last_fin:
                        f()
                if c + 3 < NC:
                    g_load(c + 3)
                routing = g_route(c // RC) if c % RC == RC - 1 else iter(())
            for _ in routing:
                pass
            table, empty, to_f = at_hi[:3]
            bank_free[B_TABLE] = dve(lambda e: e.tensor_copy(table[:, :], banks[B_TABLE][:, 0:E_ * NT]), [put[2 * NT - 1]])
            dve(lambda e: e.tensor_scalar(empty[:, :], table[:, :], 0.0, None, ALU.is_equal))
            dve(lambda e: e.scalar_tensor_tensor(to_f[:, :], empty[:, :], spare1, table[:, :], ALU.mult, ALU.add))
            dve(lambda e: e.tensor_scalar(to_u[:, :], to_f[:, :], -1.0, None, ALU.add))
            dve(lambda e: e.tensor_tensor(table[:, :], table[:, :], empty[:, :], ALU.add))
            dve(lambda e: e.tensor_scalar(from_u[:, :], table[:, :], -1.0, None, ALU.add))
            dve(lambda e: e.tensor_scalar(from_u[:, :], from_u[:, :], 1, None, ALU.logical_shift_right))
            m_counts = dve(lambda e: e.tensor_tensor(counts_i[:, :], base[:, :], slot0, ALU.subtract))
            gate_end = [(s, s.n) for s in Q.done.values()] + [st_xn[NC - 1], st_xn[NC - 2]] + list(st_xn.values())

        T_BANK, H_BANKS, Y_BANKS = 0, (1, 2, 3, 4), (5, 6)
        xg = [[sb(ctx, f"xg{i}{k}", [P, BT, D]) for k in range(2)] for i in range(2)]
        xgT = sb(ctx, "xgT", [P, HALVES, BLK])
        he = sb(ctx, "he", [P, FT, BLK])
        yb = [[sb(ctx, f"yb{i}{k}", [P, BT, D]) for k in range(2)] for i in range(2)]
        for e in Q.ENGINES:
            Q.q[e].append((Q._waits(e, gate_end), lambda g: None, None, 0))
            for e_ in range(E_):
                Q.q[e].append(("count", e_))

        rows, turned, got = {}, {}, {}

        def fetch(e_, j):
            pe_before = (settled["tensor"], e_ - 1) if e_ >= 2 else None
            for t in range(BT):
                colm = e_ * NT + j * BT + t
                rows[e_, j] = Q.gather(got[e_][j % 2], xg[e_ % 2][j % 2][:, t, :], xn_d, from_u[:, colm:colm + 1],
                                       [turned.get((e_, j - 2)), pe_before])

        def fetch_first(e_):
            got[e_] = [Signal(sem(f"rows{e_}_{k}")) for k in range(2)]
            for j in range(2):
                with Q.more_than(e_, j * BLK):
                    fetch(e_, j)

        def expert(e_):
            par = e_ % 2
            Q.phase(f"expert{e_}", ("tensor", "vector", "scalar"))
            turn_sig = Signal(sem(f"turned{e_}"))
            out_sig = Signal(sem(f"y_out{e_}"))
            y_before = (settled["vector"], e_) if e_ >= 1 else None
            out_before = (settled["gpsimd"], e_) if e_ >= 1 else None
            xT_m, he_m, y_ev, stored = {}, {}, {}, {}

            def turn(j):
                for h in range(HALVES):
                    for t in range(BT):
                        m = Q.op("tensor", lambda e, h=h, t=t: e.transpose(
                            banks[T_BANK][:, (h * BT + t) * P:(h * BT + t + 1) * P], xg[par][j % 2][:, t, h * P:(h + 1) * P],
                            ident), [rows[e_, j], xT_m.get(j - 1)], mark=h == 1 and t == BT - 1, signal=turn_sig)
                turned[e_, j] = m
                for h in range(HALVES):
                    xT_m[j] = Q.op("scalar", lambda e, h=h: e.activation(
                        xgT[:, h, :], banks[T_BANK][:, h * BLK:(h + 1) * BLK], ACT.Identity, scale=col(f"g2_{h}"),
                        bias=col(f"c2_{h}")), [m])

            def hidden(j):
                for pair in range(FT // 2):
                    bk = H_BANKS[pair]
                    for f in (2 * pair, 2 * pair + 1):
                        at = slice((f % 2) * BLK, (f % 2 + 1) * BLK)
                        for h in range(HALVES):
                            m = Q.op("tensor", lambda e, f=f, h=h, bk=bk, at=at: e.matmul(
                                banks[bk][:, at], w1s[par][:, h, f * P:(f + 1) * P], xgT[:, h, :],
                                start=h == 0, stop=h == 1), [xT_m[j], w_mark[e_]], mark=h == 1 and f % 2 == 1)
                    for f in (2 * pair, 2 * pair + 1):
                        at = slice((f % 2) * BLK, (f % 2 + 1) * BLK)
                        he_m[j, f] = Q.op("scalar", lambda e, f=f, bk=bk, at=at: e.activation(
                            he[:, f, :], banks[bk][:, at], ACT.Gelu_apprx_tanh, bias=b1_sb[:, e_, f:f + 1]), [m])

            def down(j):
                for t in range(BT):
                    bk = Y_BANKS[t]
                    for f in range(FT):
                        m = Q.op("tensor", lambda e, f=f, t=t, bk=bk: e.matmul(
                            banks[bk][:, 0:D], he[:, f, t * P:(t + 1) * P], w2s[par][:, f, :],
                            start=f == 0, stop=f == FT - 1), [he_m[j, f], y_ev.get((j - 1, t)), y_before],
                            mark=f == FT - 1)
                    y_ev[j, t] = Q.op("vector", lambda e, t=t, bk=bk: e.tensor_tensor(
                        yb[par][j % 2][:, t, :], banks[bk][:, 0:D], b2_sb[:, e_, :], ALU.add), [m, stored.get(j - 2, out_before)])
                for t in range(BT):
                    colm = e_ * NT + j * BT + t
                    stored[j] = Q.scatter(out_sig, y_d, to_u[:, colm:colm + 1], yb[par][j % 2][:, t, :],
                                          [y_ev[j, t], (out_sig, out_sig.n), out_before])

            def block(j):
                hidden(j)
                more = j + 1 < N // BLK
                if j + 2 < N // BLK:
                    with Q.more_than(e_, (j + 2) * BLK):
                        fetch(e_, j + 2)
                if more:
                    with Q.more_than(e_, (j + 1) * BLK):
                        turn(j + 1)
                down(j)
                last_store = stored[j]
                if more:
                    with Q.more_than(e_, (j + 1) * BLK):
                        block(j + 1)
                Q.wait("gpsimd", last_store)

            if e_ + 1 < E_:
                fetch_first(e_ + 1)
            with Q.more_than(e_, 0):
                turn(0)
                block(0)
            for eng, signal in settled.items():
                Q.settle(eng, signal)
            if e_ + 2 < E_:
                load_expert(e_ + 2, [(settled["tensor"], e_ + 1), w_mark[e_]])

        fetch_first(0)
        for e_ in range(E_):
            expert(e_)

        Q.phase("final", ("vector", "scalar", "gpsimd"))
        Q.op("scalar", lambda e: nc.scalar.preload_act_table_set("natural_log_exp_and_others"), mark=False)
        yg = [sb(ctx, f"yg{i}", [P, TPC, 2, D]) for i in range(2)]
        fst = [sb(ctx, f"fst{i}", [P, TPC, 9]) for i in range(2)]
        fin = [sb(ctx, f"fin{i}", [P, TPC, D]) for i in range(2)]
        used, fin_st, yg_m = {}, {}, {}

        def load_rows(c):
            yg_m[c] = Q.dma("mid_in", yg[c % 2][:, :, :, :], y_d[2 * c * CH:2 * (c + 1) * CH, :].rearrange(
                "(j p k) d -> p j k d", p=P, k=2), [used.get(c - 2), (settled["gpsimd"], E_)])

        load_rows(0)
        load_rows(1)

        def final(c):
            for j in range(TPC):
                for k in range(2):
                    m = Q.op("vector", lambda e, c=c, j=j, k=k: e.scalar_tensor_tensor(
                        acc[:, c, j, :], yg[c % 2][:, j, k, :], gate_w[:, c * TPC + j, k:k + 1], acc[:, c, j, :],
                        ALU.mult, ALU.add), [yg_m[c], m if k else None])
            used[c] = m
            if c + 2 < NC:
                load_rows(c + 2)
            r = c % 2
            m = yield from norm4(fst[r], acc[:, c, :, :], fin[r], [used[c]], [fin_st.get(c - 2)], "gpsimd")
            fin_st[c] = Q.dma("x1_out", out[c * CH:(c + 1) * CH, :].rearrange("(j p) d -> p j d", p=P),
                              fin[r][:, :, :], m)
        for c in range(0, NC, 2):
            for _ in in_turn(final(c), final(c + 1)):
                pass
        all_dma = [s for sigs, _ in Q.rings.values() for s in sigs if s.n]
        final_waits = [(s.sem, s.n) for s in all_dma]

        block = ctx.enter_context(nc.Block())

        @block.sync
        def _(eng):
            Q.play("sync", eng, counts_i)
            for s, v in final_waits:
                eng.wait_ge(s, v)

        @block.tensor
        def _(eng):
            Q.play("tensor", eng, counts_i)

        @block.vector
        def _(eng):
            Q.play("vector", eng, counts_i)

        @block.scalar
        def _(eng):
            Q.play("scalar", eng, counts_i)

        @block.gpsimd
        def _(eng):
            Q.play("gpsimd", eng, counts_i)


def shape_constants():
    p = np.arange(P)
    same = (p[:, None] // HD == p[None, :] // HD).astype(np.float32)
    eye = np.eye(P, dtype=np.float32)
    later = np.float32(NEG)
    mask_s = np.where(p[None, :] > p[:, None], later, np.float32(0))
    consts = np.concatenate([eye, same / HD, eye - same / HD, mask_s, mask_s.T, np.ones((P, P), np.float32), same], 1)
    nt = N // P
    row1 = 1 + 2 * (p[:, None, None] + P * np.arange(nt)[None, :, None]) + np.arange(2)[None, None, :]
    rows = [np.broadcast_to(r, (P, len(r))) for r in (np.arange(E_ * nt), np.arange(E_) * N, np.arange(E_, 0, -1))]
    routes = np.concatenate([p[:, None] < p[None, :], rows[0], row1.reshape(P, 2 * nt), rows[1], rows[2],
                             1 + 2 * N + p[:, None]], 1)
    return np.ascontiguousarray(consts.astype(np.float32)), np.ascontiguousarray(routes.astype(np.float32))


def kernel(**inputs):
    import concourse.bacc as _bacc
    from concourse.bass_utils import run_bass_kernel_spmd as _run

    A = {k[len("L0_attn_"):]: np.asarray(v) for k, v in inputs.items() if k.startswith("L0_attn_")}
    G = {k[len("L0_ffn_"):]: np.asarray(v) for k, v in inputs.items() if k.startswith("L0_ffn_")}

    def halves(v):
        return [v[i * P:(i + 1) * P] for i in range(HALVES)]

    def per_head(v):
        return np.tile(v, HG)

    def everywhere(v):
        return np.broadcast_to(v, (P,))

    cols = np.stack(halves(A["bq"]) + halves(A["bv"]) + halves(A["lna_w"]) + halves(G["ln1_g"]) + halves(G["ln1_b"])
                    + halves(G["ln2_g"]) + halves(G["ln2_b"])
                    + [per_head(A["lnc_w"]), per_head(A["lnd_w"]), per_head(A["blq"]), per_head(A["blk"]), per_head(A["blv"]),
                       everywhere(A["temp"]), everywhere(A["threshold"]), everywhere(A["factor"])], axis=1)
    consts, routes = shape_constants()
    arrays = {
        "x": A["x"].reshape(N, D), "consts": consts, "routes": routes, "cols": cols,
        "WqT": A["Wq"].T, "WkT": A["Wk"].T, "WvT": A["Wv"].T, "WoT": A["Wo"].T,
        "WlqT": A["Wlq"].T, "WlkT": A["Wlk"].T, "WlvT": A["Wlv"].T,
        "bo4": np.tile(A["bo"], (P, TPC)),
        "w_qkv": G["w_qkv"], "w_o": G["w_o"], "w_gate": G["w_gate"], "w1": G["w1"], "w2": G["w2"], "b2": np.broadcast_to(G["b2"][None], (P, E_, D)),
        "b1": G["b1"].reshape(E_, FT, P).transpose(2, 0, 1).reshape(P, E_ * FT),
    }
    arrays = {f"in_{k}": np.ascontiguousarray(v) for k, v in arrays.items()}
    nc = _bacc.Bacc("TRN2", target_bir_lowering=False, num_devices=1)
    aps = {k[3:]: nc.dram_tensor(k, v.shape, mybir.dt.from_np(v.dtype), kind="ExternalInput").ap()
           for k, v in arrays.items()}
    res = nc.dram_tensor("out_0", (N, D), F32, kind="ExternalOutput").ap()
    build_program(nc, aps, res)
    r = _run(nc, [arrays], core_ids=[0])
    return r.results[0]["out_0"].reshape(B, T, D)
```
